# Optimizing a Trainium2 kernel written in Bass

```python
import numpy as np
import jax
import jax.numpy as jnp

def _softmax(x, axis=-1):
    return jax.nn.softmax(x, axis=axis)

def _gelu(x):
    return jax.nn.gelu(x, approximate=True)

def _silu(x):
    return jax.nn.silu(x)

def _sigmoid(x):
    return jax.nn.sigmoid(x)

def _layernorm(x, axis=-1, eps=1e-05):
    m = jnp.mean(x, axis=axis, keepdims=True)
    v = jnp.var(x, axis=axis, keepdims=True)
    return (x - m) / jnp.sqrt(v + eps)

def _scatter_add(tgt, idx, src, axis=0):
    return tgt.at[idx].add(src)

def _segment_sum(src, seg, n):
    return jax.ops.segment_sum(src, seg, n)
kernel_name = 'mk_decoder_preln_d1_seqx_r2_e53f35'

def setup_inputs(seed: int=0):
    np.random.seed(seed)
    _w = jnp.asarray

    def _rec_inputs():
        import jax
        import jax.numpy as jnp
        _rk = jax.random.key(seed)
        x = -0.000125 + 0.9999 * jax.random.normal(jax.random.fold_in(_rk, 1), (16, 224, 512), jnp.float32)
        _lenS = 224 - jax.random.randint(jax.random.fold_in(_rk, 7), (16,), 0, max(1, 224 // 4) + 1, jnp.int32)
        _lenS2 = 750 - jax.random.randint(jax.random.fold_in(_rk, 8), (16,), 0, max(1, 750 // 4) + 1, jnp.int32)
        _ctx_1024P = jax.random.normal(jax.random.fold_in(_rk, 11), (16, 16, 512), jnp.float32)
        _ctx_1024c = jax.random.dirichlet(jax.random.fold_in(_rk, 511), 0.3 * jnp.ones((16,), jnp.float32), (16, 750))
        _ctx_1024t = jnp.einsum('bsk,bkd->bsd', _ctx_1024c, _ctx_1024P)
        _ctx_1024t = _ctx_1024t * jax.lax.rsqrt(jnp.mean(jnp.square(_ctx_1024t)) + 1e-12) * 0.953939
        ctx_1024 = -0.000514642 + 1.00011 * (_ctx_1024t + 0.3 * jax.random.normal(jax.random.fold_in(_rk, 611), (16, 750, 512), jnp.float32))
        _validS = jnp.arange(224)[None, :] < _lenS[:, None]
        _validS2 = jnp.arange(750)[None, :] < _lenS2[:, None]
        _causal = jnp.tril(jnp.ones((224, 224), dtype=bool))
        mask_BxS2_bf1 = jnp.ones((16, 750), dtype=bool)
        return (x, ctx_1024, mask_BxS2_bf1)
    x, ctx_1024, mask_BxS2_bf1 = _rec_inputs()

    def _L0_attn_setup():
        import jax, jax.numpy as jnp
        import numpy as np
        N_FILTERS = 512
        N_HEADS = 16
        key = jax.random.key(seed)
        k1, k2, k3 = jax.random.split(key, 3)
        x = jax.random.normal(k1, (8, 512, N_FILTERS), dtype=jnp.float32)
        w_qkv = jax.random.normal(k2, (N_FILTERS, N_FILTERS * 3), dtype=jnp.float32) * (0.02 / N_FILTERS) ** 0.5
        w_out = jax.random.normal(k3, (N_FILTERS, N_FILTERS), dtype=jnp.float32) * (0.02 / N_FILTERS) ** 0.5
        return {'x': x, 'w_qkv': w_qkv, 'w_out': w_out}
    _L0_attn_all = _L0_attn_setup()
    _L0_attn_in = {k: v for k, v in _L0_attn_all.items() if k in ('w_qkv', 'w_out')}
    del _L0_attn_all

    def _L0_xattn_setup():
        import jax, jax.numpy as jnp
        import numpy as np
        EPS = 1e-06
        NUM_HEADS = 16
        DIM_HEADS = 64

        def _ln(x, scale, bias):
            mu = jnp.mean(x, axis=-1, keepdims=True)
            var = jnp.mean(jnp.square(x - mu), axis=-1, keepdims=True)
            return (x - mu) * jax.lax.rsqrt(var + EPS) * scale + bias
        key = jax.random.key(seed)
        ks = jax.random.split(key, 8)
        b, n, m, dim, ctx_dim = (8, 2048, 128, 512, 512)
        inner = NUM_HEADS * DIM_HEADS
        x = jax.random.normal(ks[0], (b, n, dim), dtype=jnp.float32)
        context = jax.random.normal(ks[1], (b, m, ctx_dim), dtype=jnp.float32)
        mask = jnp.ones((b, m), dtype=bool)
        Wq = jax.random.normal(ks[2], (dim, inner), dtype=jnp.float32) / np.sqrt(dim)
        Wkv = jax.random.normal(ks[3], (ctx_dim, 2 * inner), dtype=jnp.float32) / np.sqrt(ctx_dim)
        null_kv = jax.random.normal(ks[4], (2, DIM_HEADS), dtype=jnp.float32)
        Wo = jax.random.normal(ks[5], (inner, dim), dtype=jnp.float32) / np.sqrt(inner)
        return {'x': x, 'context': context, 'mask': mask, 'ln1_s': jnp.ones((dim,), jnp.float32), 'ln1_b': jnp.zeros((dim,), jnp.float32), 'lnc_s': jnp.ones((ctx_dim,), jnp.float32), 'lnc_b': jnp.zeros((ctx_dim,), jnp.float32), 'Wq': Wq, 'Wkv': Wkv, 'null_kv': null_kv, 'Wo': Wo, 'lno_s': jnp.ones((dim,), jnp.float32), 'lno_b': jnp.zeros((dim,), jnp.float32)}
    _L0_xattn_all = _L0_xattn_setup()
    _L0_xattn_in = {k: v for k, v in _L0_xattn_all.items() if k in ('ln1_s', 'ln1_b', 'lnc_s', 'lnc_b', 'Wq', 'Wkv', 'null_kv', 'Wo', 'lno_s', 'lno_b')}
    del _L0_xattn_all

    def _L0_ffn_setup():
        import jax, jax.numpy as jnp
        import numpy as np
        key = jax.random.key(seed)
        ks = jax.random.split(key, 5)
        B, S, D_in, D_out, E, R = (4, 512, 512, 512, 8, 16)
        x = jax.random.normal(ks[0], (B, S, D_in), dtype=jnp.float32)
        weight = jax.random.normal(ks[1], (D_out, D_in), dtype=jnp.float32) / np.sqrt(D_in)
        gate_w = jax.random.normal(ks[2], (E, D_in), dtype=jnp.float32) / np.sqrt(D_in)
        lora_U = jax.random.normal(ks[3], (E, R, D_in), dtype=jnp.float32) / np.sqrt(D_in)
        lora_V = jax.random.normal(ks[4], (E, D_out, R), dtype=jnp.float32) / np.sqrt(R)
        return {'x': x, 'weight': weight, 'gate_w': gate_w, 'lora_U': lora_U, 'lora_V': lora_V}
    _L0_ffn_all = _L0_ffn_setup()
    _L0_ffn_in = {k: v for k, v in _L0_ffn_all.items() if k in ('weight', 'gate_w', 'lora_U', 'lora_V')}
    del _L0_ffn_all
    return {'x': x, 'ctx_1024': ctx_1024, 'mask_BxS2_bf1': mask_BxS2_bf1, 'L0_attn_w_qkv': _L0_attn_in['w_qkv'], 'L0_attn_w_out': _L0_attn_in['w_out'], 'L0_xattn_ln1_s': _L0_xattn_in['ln1_s'], 'L0_xattn_ln1_b': _L0_xattn_in['ln1_b'], 'L0_xattn_lnc_s': _L0_xattn_in['lnc_s'], 'L0_xattn_lnc_b': _L0_xattn_in['lnc_b'], 'L0_xattn_Wq': _L0_xattn_in['Wq'], 'L0_xattn_Wkv': _L0_xattn_in['Wkv'], 'L0_xattn_null_kv': _L0_xattn_in['null_kv'], 'L0_xattn_Wo': _L0_xattn_in['Wo'], 'L0_xattn_lno_s': _L0_xattn_in['lno_s'], 'L0_xattn_lno_b': _L0_xattn_in['lno_b'], 'L0_ffn_weight': _L0_ffn_in['weight'], 'L0_ffn_gate_w': _L0_ffn_in['gate_w'], 'L0_ffn_lora_U': _L0_ffn_in['lora_U'], 'L0_ffn_lora_V': _L0_ffn_in['lora_V']}

def reference(x, ctx_1024, mask_BxS2_bf1, L0_attn_w_qkv, L0_attn_w_out, L0_xattn_ln1_s, L0_xattn_ln1_b, L0_xattn_lnc_s, L0_xattn_lnc_b, L0_xattn_Wq, L0_xattn_Wkv, L0_xattn_null_kv, L0_xattn_Wo, L0_xattn_lno_s, L0_xattn_lno_b, L0_ffn_weight, L0_ffn_gate_w, L0_ffn_lora_U, L0_ffn_lora_V):
    import jax
    import jax.numpy as jnp

    def _L0_attn_ref(x, w_qkv, w_out):
        import jax, jax.numpy as jnp
        import numpy as np
        N_FILTERS = 512
        N_HEADS = 16
        b, n, c = x.shape
        h = N_HEADS
        d = c // h
        qkv = jnp.einsum('bnc,ce->bne', x, w_qkv)
        q, k, v = jnp.split(qkv, 3, axis=-1)
        to_heads = lambda t: t.reshape(b, n, h, d).transpose(0, 2, 1, 3)
        q, k, v = (to_heads(q), to_heads(k), to_heads(v))
        scale = jnp.sqrt(jnp.asarray(c, jnp.float32))
        attn = jnp.einsum('bhnd,bhmd->bhnm', q, k) / scale
        attn = jax.nn.softmax(attn, axis=-1)
        out = jnp.einsum('bhnm,bhmd->bhnd', attn, v)
        out = out.transpose(0, 2, 1, 3).reshape(b, n, c)
        return jnp.einsum('bnc,co->bno', out, w_out)

    def _L0_xattn_ref(x, context, mask, ln1_s, ln1_b, lnc_s, lnc_b, Wq, Wkv, null_kv, Wo, lno_s, lno_b):
        import jax, jax.numpy as jnp
        import numpy as np
        EPS = 1e-06
        NUM_HEADS = 16
        DIM_HEADS = 64

        def _ln(x, scale, bias):
            mu = jnp.mean(x, axis=-1, keepdims=True)
            var = jnp.mean(jnp.square(x - mu), axis=-1, keepdims=True)
            return (x - mu) * jax.lax.rsqrt(var + EPS) * scale + bias
        b, n, _ = x.shape
        h, d = (NUM_HEADS, DIM_HEADS)
        scale = h ** (-0.5)
        xn = _ln(x, ln1_s, ln1_b)
        cn = _ln(context, lnc_s, lnc_b)
        q = xn @ Wq
        kv = cn @ Wkv
        k, v = jnp.split(kv, 2, axis=-1)

        def to_heads(t):
            return t.reshape(t.shape[0], t.shape[1], h, d).transpose(0, 2, 1, 3)
        q, k, v = (to_heads(q), to_heads(k), to_heads(v))
        nk = jnp.broadcast_to(null_kv[0], (b, h, 1, d))
        nv = jnp.broadcast_to(null_kv[1], (b, h, 1, d))
        k = jnp.concatenate((nk, k), axis=2)
        v = jnp.concatenate((nv, v), axis=2)
        sim = jnp.einsum('bhid,bhjd->bhij', q * scale, k)
        mfull = jnp.pad(mask, ((0, 0), (1, 0)), constant_values=True)[:, None, None, :]
        max_neg = -jnp.finfo(sim.dtype).max
        sim = jnp.where(mfull, sim, max_neg)
        attn = jax.nn.softmax(sim, axis=-1)
        out = jnp.einsum('bhij,bhjd->bhid', attn, v)
        out = out.transpose(0, 2, 1, 3).reshape(b, n, h * d)
        out = out @ Wo
        return _ln(out, lno_s, lno_b)

    def _L0_ffn_ref(x, weight, gate_w, lora_U, lora_V):
        import jax, jax.numpy as jnp
        import numpy as np
        scaling = 1.0 / lora_U.shape[1]
        B, S, D_in = x.shape
        xt = x.reshape(-1, D_in)
        gate = jax.nn.softmax(xt @ gate_w.T, axis=-1)
        base = xt @ weight.T
        t = jnp.einsum('nh,erh->ner', xt, lora_U)
        lora = jnp.einsum('ne,eor,ner->no', gate, lora_V, t)
        out = base + scaling * lora
        return out.reshape(B, S, -1)
    x = x + _L0_attn_ref(_layernorm(x, axis=-1), L0_attn_w_qkv, L0_attn_w_out)
    x = x + _L0_xattn_ref(_layernorm(x, axis=-1), ctx_1024, mask_BxS2_bf1, L0_xattn_ln1_s, L0_xattn_ln1_b, L0_xattn_lnc_s, L0_xattn_lnc_b, L0_xattn_Wq, L0_xattn_Wkv, L0_xattn_null_kv, L0_xattn_Wo, L0_xattn_lno_s, L0_xattn_lno_b)
    x = x + _L0_ffn_ref(_layernorm(x, axis=-1), L0_ffn_weight, L0_ffn_gate_w, L0_ffn_lora_U, L0_ffn_lora_V)
    return x

_drawn_inputs = setup_inputs


def setup_inputs(seed=0):
    import zlib

    import numpy as np

    out = dict(_drawn_inputs(seed))
    spreads = {'L0_xattn_ln1_s': (1.0, 0.2),
     'L0_xattn_ln1_b': (0.0, 0.1),
     'L0_xattn_lnc_s': (1.0, 0.2),
     'L0_xattn_lnc_b': (0.0, 0.1),
     'L0_xattn_lno_s': (1.0, 0.2),
     'L0_xattn_lno_b': (0.0, 0.1)}
    factors = {'L0_attn_w_qkv': 8.0,
     'L0_attn_w_out': 8.0,
     'L0_ffn_gate_w': 5.091,
     'L0_ffn_lora_U': 3.303,
     'L0_ffn_lora_V': 3.32}
    for name, (base, spread) in spreads.items():
        noise = np.random.default_rng([zlib.crc32(name.encode()), seed]).standard_normal(out[name].shape)
        drawn = base * np.exp(spread * noise) if base else spread * noise
        out[name] = jnp.asarray(drawn.astype(out[name].dtype))
    for name, factor in factors.items():
        out[name] = (out[name] * factor).astype(out[name].dtype)
    return out
```

```python
from contextlib import ExitStack

import concourse.bass as bass
from concourse import mybir

F32 = mybir.dt.float32
F32R = mybir.dt.float32r
U8 = mybir.dt.uint8
ACT = mybir.ActivationFunctionType
ALU = mybir.AluOpType
AX = mybir.AxisListType

P = 128
DMA = 16
BIG = 3.0e38
LN_EPS, XLN_EPS = 1e-5, 1e-6


class Ring:

    def __init__(self, full, done, first, turn, turns, last=()):
        self.full, self.done = full, done
        self.lists = {"first": list(first), "turn": list(turn), "last": list(last)}
        self.turns = turns
        assert len(self.lists["first"]) % 2 == 0 and len(self.lists["turn"]) % 2 == 0

    def _at(self, use, when):
        kind, t = when
        i = self.lists[kind].index(use)
        f, n = len(self.lists["first"]), len(self.lists["turn"])
        return {"first": 0, "turn": f + t * n, "last": f + self.turns * n}[kind], i, t

    def slot(self, use, when):
        return self.lists[when[0]].index(use) % 2

    def _half(self, when):
        kind, t = when
        f, n = len(self.lists["first"]) // 2, len(self.lists["turn"]) // 2
        return {"first": 0, "turn": f + t * n, "last": f + self.turns * n}[kind]

    def free(self, use, when):
        i = self.lists[when[0]].index(use)
        return self.done[i % 2], self._half(when) + i // 2 + 1

    def filled(self, use, when):
        base, i, _ = self._at(use, when)
        return self.full, base + i + 1

    def emptied(self, use, when):
        i = self.lists[when[0]].index(use)
        return self.done[i % 2], self._half(when) + i // 2 + 2

    def emptied_before(self, use, when):
        kind, t = when
        n = self.lists["turn"]
        back = len(n) - n.index(use)
        assert len(self.lists["first"]) - self.lists["first"].index(use) == back
        i = n.index(use)
        t = self.turns if kind == "last" else t
        return self.done[i % 2], (len(self.lists["first"]) - len(n)) // 2 + t * (len(n) // 2) + i // 2 + 2


def make_constants(nc, pool, ident, minus_half, ready):
    nc.gpsimd.memset(minus_half[:, :], -0.5).then_inc(ready, 1)
    nc.gpsimd.memset(ident[:, :], 1.0).then_inc(ready, 1)
    pool.wait_ge(ready, 2)
    nc.gpsimd.affine_select(out=ident[:, :], in_=ident[:, :], compare_op=ALU.is_equal, fill=0.0, base=0,
                            pattern=[[-1, P]], channel_multiplier=1).then_inc(ready, 1)




class Place:

    def __init__(self, nc, ctx, stage):
        self.nc, self.ctx, self.stage = nc, ctx, stage

    def sb(self, name, shape, dt=F32):
        return self.ctx.enter_context(self.nc.sbuf_tensor(f"{self.stage}_{name}", shape, dt))

    def psum(self, name, shape):
        return self.ctx.enter_context(self.nc.psum_tensor(f"{self.stage}_{name}", shape, F32))

    def sem(self, name):
        return self.ctx.enter_context(self.nc.semaphore(f"{self.stage}_{name}"))


def moments_of(nc, dve, x, stats, moments, eps, step, before, var_ready, passed):
    nc.vector.bn_stats(stats, x).then_inc(step, 1)
    dve.wait_ge(step, before + 1)
    dve.sem_inc(passed, 1)
    nc.vector.bn_aggr(moments, stats).then_inc(step, 1)
    dve.wait_ge(step, before + 2)
    nc.vector.tensor_scalar(moments[:, 1:2], moments[:, 1:2], eps, None, ALU.add).then_inc(var_ready, 1)


def inverse_root(nc, pool, rstd, var, minus_half, var_ready, before, rstd_ready):
    pool.wait_ge(var_ready, before + 1)
    nc.gpsimd.tensor_tensor(rstd, var, minus_half, ALU.pow).then_inc(rstd_ready, 1)


def self_attention(nc, x, w_qkv, w_out, x1):
    B, T, D = x.shape
    HEADS, DH = 16, 32
    QT = T // 2
    KD = D // P
    GROUP = P // DH
    GROUPS = HEADS // GROUP
    SCALE = float(D) ** -0.5

    project = [("st", 0), ("st", 1), ("ln", 0), ("ln", 1), ("xt", 0), ("xt", 1), ("q", 0), ("q", 1), ("k", 0), ("k", 1),
               ("v", 0), ("v", 1)]
    after_head = {1: [("st", 0), ("st", 1)], 3: [("ln", 0), ("ln", 1)], 5: [("xt", 0)], 6: [("xt", 1)], 7: [("q", 0)], 8: [("q", 1)],
                  10: [("k", 0)], 11: [("k", 1)]}

    def attend(project_next):
        order = [("S", 0), ("S", 1)]
        for h in range(HEADS):
            order.append(("T", h))
            if h + 2 < HEADS:
                order.append(("S", h + 2))
            if h % GROUP == 0 and h:
                order += [("PV", h // GROUP - 1), ("R", h // GROUP - 1)]
            if project_next:
                order += after_head.get(h, [])
        order.append(("PV", GROUPS - 1))
        if project_next:
            order += [("v", 0), ("v", 1)]
        order += [("R", GROUPS - 1), ("out", 0), ("out", 1)]
        return order

    turn, last = attend(True), attend(False)
    TURNS = B - 1

    def only(order, *kinds):
        return [u for u in order if u[0] in kinds]

    with ExitStack() as ctx:
        at = Place(nc, ctx, "sa")
        wqkv_raw = at.sb("wqkv_raw", [P, KD, 3 * D])
        wout_raw = at.sb("wout_raw", [P, KD, D])
        wqkv = [at.sb(f"wqkv_{n}", [P, KD, 3 * D], F32R) for n in ("hi", "lo")]
        wout = [at.sb(f"wout_{n}", [P, KD, D], F32R) for n in ("hi", "lo")]
        ident, minus_half = at.sb("ident", [P, P]), at.sb("minus_half", [P, 1])
        xn = at.sb("xn", [QT, 2, D])
        xres = at.sb("xres", [QT, 2, D])
        stats = at.sb("stats", [QT, 2, 6])
        moments = at.sb("moments", [QT, 2, 2])
        rstd = at.sb("rstd", [QT, 2])
        xnT = [at.sb(f"xnT_{n}", [P, KD, T], F32R) for n in ("hi", "lo")]
        qk = [at.sb(f"qk_{n}", [P, 2, GROUPS, T], F32R) for n in ("hi", "lo")]
        stack = [at.sb(f"{n}_stack", [P, GROUP, GROUPS, T], F32R) for n in ("q", "k")]
        v_sb = at.sb("v", [QT, 2, D])
        negmax = at.sb("negmax", [QT, 4, 2])
        prob = at.sb("prob", [QT, 2, 2, T])
        sums = at.sb("sums", [QT, 2, 2, GROUP])
        rsum = at.sb("rsum", [QT, 2, 2, P])
        probT = at.sb("probT", [QT, 2 * GROUP, 2, T])
        spread = at.sb("spread", [P, 2, T])
        o_sb = at.sb("o", [P, T])
        oT = [at.sb(f"oT_{n}", [P, GROUPS, T], F32R) for n in ("hi", "lo")]

        ps_s = [at.psum(f"ps_s{i}", [P, 512]) for i in range(2)]
        ps_t = [at.psum(f"ps_t{i}", [P, 512]) for i in range(2)]
        ps_f = [at.psum(f"ps_f{i}", [P, 512]) for i in range(2)]
        ps_o = [at.psum(f"ps_o{i}", [P, 512]) for i in range(2)]

        def ring(name, *kinds):
            return Ring(at.sem(f"{name}_full"), [at.sem(f"{name}_done{i}") for i in range(2)],
                        only(project, *kinds), only(turn, *kinds), TURNS, only(last, *kinds))

        S = ring("scores", "S", "out")
        TR = ring("transposed", "T", "xt")
        F = ring("projected", "q", "k", "v")
        O = ring("heads", "PV")
        rings = [S, TR, F, O]

        w_in, w_hi, w_lo = at.sem("w_in"), at.sem("w_hi"), at.sem("w_lo")
        ident_ready = at.sem("ident_ready")
        dve_passed, sp_passed = at.sem("dve_passed"), at.sem("sp_passed")
        x_in, xres_in, x1_stored = at.sem("x_in"), at.sem("xres_in"), at.sem("x1_stored")
        ln_step, var_ready, rstd_ready, xn_ready = at.sem("ln_step"), at.sem("var_ready"), at.sem("rstd_ready"), at.sem("xn_ready")
        xt_hi, qk_hi = at.sem("xt_hi"), at.sem("qk_hi")
        stacked = [at.sem(f"stacked{c}") for c in range(GROUP)]
        STACKED = 2 * GROUP * DMA
        negmax_ready = at.sem("negmax_ready")
        rsum_ready, spread_ready, o_step = at.sem("rsum_ready"), at.sem("spread_ready"), at.sem("o_step")

        x_v = x.rearrange("b (q p) d -> b p q d", p=QT)
        x1_v = x1.rearrange("b (q p) d -> b p q d", p=QT)

        def batches(b):
            return bass.ds(b, 1)

        def dram(v, b):
            return v[batches(b)].rearrange("o p q d -> (o p) q d")

        with nc.Block() as block:

            @block.gpsimd
            def _(pool):
                make_constants(nc, pool, ident, minus_half, ident_ready)
                with pool.Fori(0, B) as b:
                    for i in range(2):
                        inverse_root(nc, pool, rstd[:, i:i + 1], moments[:, i, 1:2], minus_half[0:QT, :], var_ready, 2 * b + i, rstd_ready)

            @block.sync
            def _(sp):
                sp.dma_start(xn[:, :, :], dram(x_v, 0)).then_inc(x_in, DMA)
                sp.dma_start(wqkv_raw[:, :, :], w_qkv.rearrange("(k p) n -> p k n", p=P)).then_inc(w_in, DMA)
                sp.dma_start(wout_raw[:, :, :], w_out.rearrange("(k p) n -> p k n", p=P)).then_inc(w_in, DMA)
                sp.dma_start(xres[:, :, :], dram(x_v, 0)).then_inc(xres_in, DMA)

                def stack_heads(when):
                    for use in only(project, "q", "k"):
                        sp.wait_ge(*F.emptied(use, when))
                        sp.sem_inc(sp_passed, 1)
                    for c in range(GROUP):
                        for i, parts in enumerate(((0, 1, 0, 1), (0, 0, 1, 1))):
                            for g, part in enumerate(parts):
                                sp.dma_start(stack[i][g * DH:(g + 1) * DH, c, :, :].bitcast(F32),
                                             qk[part][c * DH:(c + 1) * DH, i, :, :].bitcast(F32)).then_inc(stacked[c], DMA)

                stack_heads(("first", 0))

                def store(b, when):
                    sp.wait_ge(*S.emptied(("out", 0), when))
                    sp.sem_inc(sp_passed, 1)
                    sp.wait_ge(*S.emptied(("out", 1), when))
                    sp.sem_inc(sp_passed, 1)
                    sp.dma_start(dram(x1_v, b), xres[:, :, :]).then_inc(x1_stored, DMA)
                    sp.wait_ge(x1_stored, DMA * b + DMA)
                    sp.sem_inc(sp_passed, 1)

                with sp.Fori(0, TURNS) as b:
                    when = ("turn", b)
                    sp.wait_ge(xt_hi, 2 * b + 2)
                    sp.sem_inc(sp_passed, 1)
                    sp.dma_start(xn[:, :, :], dram(x_v, b + 1)).then_inc(x_in, DMA)
                    sp.wait_ge(*S.filled(("S", HEADS - 1), when))
                    sp.sem_inc(sp_passed, 1)
                    stack_heads(when)
                    store(b, when)
                    sp.dma_start(xres[:, :, :], dram(x_v, b + 1)).then_inc(xres_in, DMA)
                store(TURNS, ("last", TURNS))

            @block.tensor
            def _(pe):
                def split_products(out, lhs, rhs, first, last_):
                    for n, (i, j) in enumerate(((0, 0), (0, 1), (1, 0))):
                        ins = nc.tensor.matmul(out, lhs[i], rhs[j], start=first and n == 0, stop=last_ and n == 2)
                    return ins

                def run(order, b, when, ahead):
                    for use in order:
                        kind, i = use
                        if kind == "S":
                            c, a = i % GROUP, i // GROUP
                            pe.wait_ge(stacked[c], STACKED * b + STACKED)
                            pe.wait_ge(*S.free(use, when))
                            out = ps_s[S.slot(use, when)]
                            for q in range(2):
                                ins = nc.tensor.matmul(out[0:QT, q * T:(q + 1) * T],
                                                       stack[0][:, c, a, q * QT:(q + 1) * QT],
                                                       stack[1][:, c, a, :], start=True, stop=True)
                            ins.then_inc(S.full, 1)
                        elif kind == "T":
                            pe.wait_ge(*S.emptied(("S", i), when))
                            pe.wait_ge(*TR.free(use, when))
                            out = ps_t[TR.slot(use, when)]
                            for k in range(2):
                                for q in range(2):
                                    ins = nc.tensor.transpose(out[0:QT, k * T + q * QT:k * T + (q + 1) * QT],
                                                              prob[:, i % 2, q, k * QT:(k + 1) * QT],
                                                              ident[0:QT, 0:QT])
                            ins.then_inc(TR.full, 1)
                        elif kind == "PV":
                            for h in (GROUP * i + 2, GROUP * i + 3):
                                pe.wait_ge(*TR.emptied(("T", h), when))
                            if i == 0:
                                pe.wait_ge(*F.emptied_before(("v", 0), when))
                                pe.wait_ge(*F.emptied_before(("v", 1), when))
                            pe.wait_ge(*O.free(use, when))
                            out = ps_o[O.slot(use, when)]
                            for k in range(2):
                                for c in range(GROUP):
                                    h = GROUP * i + c
                                    nc.tensor.matmul(out[c * DH:(c + 1) * DH, 0:T],
                                                     v_sb[:, k, h * DH:(h + 1) * DH],
                                                     probT[:, h % (2 * GROUP), k, :], start=k == 0, stop=k == 1)
                        elif kind == "R":
                            pe.wait_ge(rsum_ready, GROUPS * b + i + 1)
                            out = ps_o[O.slot(("PV", i), when)]
                            for q in range(2):
                                ins = nc.tensor.transpose(out[:, 256 + q * QT:256 + (q + 1) * QT], rsum[:, i % 2, q, :],
                                                          ident[0:QT, 0:QT])
                            ins.then_inc(O.full, 1)
                        elif kind == "out":
                            pe.wait_ge(*O.emptied(("PV", GROUPS - 2), when))
                            pe.wait_ge(*O.emptied(("PV", GROUPS - 1), when))
                            pe.wait_ge(*S.free(use, when))
                            out = ps_s[S.slot(use, when)]
                            for a in range(GROUPS):
                                ins = split_products(out[0:QT, :], [p[:, a, i * QT:(i + 1) * QT] for p in oT],
                                                     [w[:, a, :] for w in wout], a == 0, a == GROUPS - 1)
                            ins.then_inc(S.full, 1)
                        elif kind == "xt":
                            pe.wait_ge(xn_ready, 2 * ahead + i + 1)
                            pe.wait_ge(*TR.free(use, when))
                            out = ps_t[TR.slot(use, when)]
                            for k in range(KD):
                                ins = nc.tensor.transpose(out[:, k * QT:(k + 1) * QT], xn[:, i, k * P:(k + 1) * P],
                                                          ident[0:QT, 0:QT])
                            ins.then_inc(TR.full, 1)
                        elif kind in ("q", "k"):
                            if use == ("q", 0):
                                pe.wait_ge(*TR.emptied(("xt", 0), when))
                                pe.wait_ge(*TR.emptied(("xt", 1), when))
                            pe.wait_ge(*F.free(use, when))
                            out = ps_f[F.slot(use, when)]
                            for m in range(2):
                                col = (D if kind == "k" else 0) + (2 * i + m) * P
                                for k in range(KD):
                                    ins = split_products(out[:, m * T:(m + 1) * T],
                                                         [w[:, k, col:col + P] for w in wqkv],
                                                         [t[:, k, :] for t in xnT], k == 0, k == KD - 1)
                            ins.then_inc(F.full, 1)
                        elif kind == "v":
                            pe.wait_ge(*F.free(use, when))
                            out = ps_f[F.slot(use, when)]
                            for k in range(KD):
                                ins = split_products(out[0:QT, :], [t[:, k, i * QT:(i + 1) * QT] for t in xnT],
                                                     [w[:, k, 2 * D:3 * D] for w in wqkv], k == 0, k == KD - 1)
                            ins.then_inc(F.full, 1)

                pe.wait_ge(ident_ready, 3)
                pe.wait_ge(w_lo, 2)
                run(project, 0, ("first", 0), 0)
                with pe.Fori(0, TURNS) as b:
                    run(turn, b, ("turn", b), b + 1)
                run(last, TURNS, ("last", TURNS), B)

            @block.scalar
            def _(act):
                def run(order, b, when, ahead):
                    for use in order:
                        kind, i = use
                        if kind == "S":
                            act.wait_ge(negmax_ready, HEADS * b + i + 1)
                            src = ps_s[S.slot(use, when)]
                            for q in range(2):
                                ins = nc.scalar.activation(prob[:, i % 2, q, :], src[0:QT, q * T:(q + 1) * T], ACT.Exp,
                                                           bias=negmax[:, i % 4, q:q + 1], scale=1.0,
                                                           accum_out=sums[:, (i // GROUP) % 2, q, i % GROUP:i % GROUP + 1])
                            ins.then_inc(S.done[S.slot(use, when)], 1)
                        elif kind == "T" and i % 2 == 1:
                            act.wait_ge(*TR.filled(use, when))
                            src = ps_t[TR.slot(use, when)]
                            nc.scalar.activation(probT[:, i % (2 * GROUP), :, :],
                                                 src[0:QT, 0:2 * T].rearrange("p (k t) -> p k t", k=2),
                                                 ACT.Copy).then_inc(TR.done[TR.slot(use, when)], 1)
                        elif kind == "R":
                            act.wait_ge(*O.filled(("PV", i), when))
                            src = ps_o[O.slot(("PV", i), when)]
                            nc.scalar.activation(spread[:, i % 2, :], src[:, 256:256 + T], ACT.Copy).then_inc(spread_ready, 1)
                        elif kind == "xt":
                            act.wait_ge(*TR.filled(use, when))
                            src = ps_t[TR.slot(use, when)]
                            nc.scalar.activation(xnT[0][:, :, i * QT:(i + 1) * QT],
                                                 src[:, 0:KD * QT].rearrange("p (k t) -> p k t", k=KD),
                                                 ACT.Copy).then_inc(xt_hi, 1)
                        elif kind in ("q", "k"):
                            act.wait_ge(*F.filled(use, when))
                            if use == ("q", 0) and when[0] != "first":
                                for c in range(GROUP):
                                    act.wait_ge(stacked[c], STACKED * ahead)
                            src = ps_f[F.slot(use, when)]
                            nc.scalar.activation(qk[0][:, int(kind == "k"), 2 * i:2 * i + 2, :],
                                                 src[:, 0:2 * T].rearrange("p (m t) -> p m t", m=2), ACT.Copy,
                                                 scale=SCALE if kind == "q" else 1.0).then_inc(qk_hi, 1)
                        elif kind == "v":
                            act.wait_ge(*F.filled(use, when))
                            src = ps_f[F.slot(use, when)]
                            nc.scalar.activation(v_sb[:, i, :], src[0:QT, :], ACT.Copy).then_inc(F.done[F.slot(use, when)], 1)

                act.wait_ge(w_in, 2 * DMA)
                nc.scalar.activation(wqkv[0][:, :, :], wqkv_raw[:, :, :], ACT.Copy).then_inc(w_hi, 1)
                nc.scalar.activation(wout[0][:, :, :], wout_raw[:, :, :], ACT.Copy).then_inc(w_hi, 1)
                run(project, 0, ("first", 0), 0)
                with act.Fori(0, TURNS) as b:
                    run(turn, b, ("turn", b), b + 1)
                run(last, TURNS, ("last", TURNS), B)

            @block.vector
            def _(dve):
                def run(order, b, when, ahead):
                    for use in order:
                        kind, i = use
                        if kind == "S":
                            dve.wait_ge(*S.filled(use, when))
                            src = ps_s[S.slot(use, when)]
                            nc.vector.tensor_reduce(negmax[:, i % 4, :],
                                                    src[0:QT, 0:2 * T].rearrange("p (q t) -> p q t", q=2),
                                                    AX.X, ALU.max, negate=True).then_inc(negmax_ready, 1)
                        elif kind == "T":
                            if i % 2 == 0:
                                dve.wait_ge(*TR.filled(use, when))
                                src = ps_t[TR.slot(use, when)]
                                nc.vector.tensor_copy(probT[:, i % (2 * GROUP), :, :],
                                                      src[0:QT, 0:2 * T].rearrange("p (k t) -> p k t", k=2)
                                                      ).then_inc(TR.done[TR.slot(use, when)], 1)
                            if i % GROUP == GROUP - 1:
                                a = i // GROUP
                                dve.wait_ge(*S.emptied(("S", i), when))
                                nc.vector.reciprocal(rsum[:, a % 2, :, :].rearrange("p q (c d) -> p (q c) d", d=DH),
                                                     sums[:, a % 2, :, :].rearrange("p q c -> p (q c)").unsqueeze(2)
                                                     .to_broadcast([QT, 2 * GROUP, DH])).then_inc(rsum_ready, 1)
                        elif kind == "R":
                            src = ps_o[O.slot(("PV", i), when)]
                            steps = 2 * (GROUPS * b + i)
                            dve.wait_ge(spread_ready, GROUPS * b + i + 1)
                            nc.vector.tensor_tensor(o_sb[:, :], src[:, 0:T], spread[:, i % 2, :], ALU.mult).then_inc(o_step, 1)
                            dve.wait_ge(o_step, steps + 1)
                            nc.vector.tensor_copy(oT[0][:, i, :], o_sb[:, :]).then_inc(o_step, 1)
                            dve.wait_ge(o_step, steps + 2)
                            nc.vector.tensor_tensor(oT[1][:, i, :], o_sb[:, :], oT[0][:, i, :].bitcast(F32),
                                                    ALU.subtract).then_inc(O.done[O.slot(("PV", i), when)], 1)
                        elif kind == "out":
                            if i == 0:
                                dve.wait_ge(xres_in, DMA * b + DMA)
                            dve.wait_ge(*S.filled(use, when))
                            src = ps_s[S.slot(use, when)]
                            nc.vector.tensor_tensor(xres[:, i, :], src[0:QT, :], xres[:, i, :],
                                                    ALU.add).then_inc(S.done[S.slot(use, when)], 1)
                        elif kind == "st":
                            if i == 0:
                                dve.wait_ge(x_in, DMA * ahead + DMA)
                            moments_of(nc, dve, xn[:, i, :], stats[:, i, :], moments[:, i, :], LN_EPS, ln_step,
                                       4 * ahead + 2 * i, var_ready, dve_passed)
                        elif kind == "ln":
                            dve.wait_ge(rstd_ready, 2 * ahead + i + 1)
                            nc.vector.tensor_scalar(xn[:, i, :], xn[:, i, :], moments[:, i, 0:1], rstd[:, i:i + 1],
                                                    ALU.subtract, ALU.mult).then_inc(xn_ready, 1)
                        elif kind == "xt":
                            dve.wait_ge(xt_hi, 2 * ahead + i + 1)
                            src = ps_t[TR.slot(use, when)]
                            part = (slice(None), slice(None), slice(i * QT, (i + 1) * QT))
                            nc.vector.tensor_tensor(xnT[1][part], src[:, 0:KD * QT].rearrange("p (k t) -> p k t", k=KD),
                                                    xnT[0][part].bitcast(F32),
                                                    ALU.subtract).then_inc(TR.done[TR.slot(use, when)], 1)
                        elif kind in ("q", "k"):
                            dve.wait_ge(qk_hi, 4 * ahead + 2 * int(kind == "k") + i + 1)
                            src = ps_f[F.slot(use, when)]
                            part = (slice(None), int(kind == "k"), slice(2 * i, 2 * i + 2), slice(None))
                            nc.vector.scalar_tensor_tensor(
                                qk[1][part], src[:, 0:2 * T].rearrange("p (m t) -> p m t", m=2),
                                SCALE if kind == "q" else 1.0, qk[0][part].bitcast(F32), ALU.mult,
                                ALU.subtract).then_inc(F.done[F.slot(use, when)], 1)

                for r in rings:
                    for d in r.done:
                        dve.sem_inc(d, 1)
                run(project[0:4], 0, ("first", 0), 0)
                dve.wait_ge(w_hi, 1)
                nc.vector.tensor_tensor(wqkv[1][:, :, :], wqkv_raw[:, :, :], wqkv[0][:, :, :].bitcast(F32),
                                        ALU.subtract).then_inc(w_lo, 1)
                dve.wait_ge(w_hi, 2)
                nc.vector.tensor_tensor(wout[1][:, :, :], wout_raw[:, :, :], wout[0][:, :, :].bitcast(F32),
                                        ALU.subtract).then_inc(w_lo, 1)
                run(project[4:], 0, ("first", 0), 0)
                with dve.Fori(0, TURNS) as b:
                    run(turn, b, ("turn", b), b + 1)
                run(last, TURNS, ("last", TURNS), B)


def cross_queries(nc, x1, ln1_s, ln1_b, w_q, q_T):
    B, T, D = x1.shape
    E = w_q.shape[1]
    KD, MD = D // P, E // P
    NB = 2
    N = NB * T
    RT = T // 2
    TILES = N // RT
    TURNS = B // NB
    QSCALE = -0.25

    turn = [("xt", t) for t in range(TILES)] + [("q", m) for m in range(MD)]

    with ExitStack() as ctx:
        at = Place(nc, ctx, "cq")
        wq_raw = at.sb("wq_raw", [P, KD, E])
        wq = [at.sb(f"wq_{n}", [P, KD, E], F32R) for n in ("hi", "lo")]
        s_col, b_col = at.sb("s_col", [P, KD]), at.sb("b_col", [P, KD])
        qbias = at.sb("qbias", [P, MD])
        ident, minus_half = at.sb("ident", [P, P]), at.sb("minus_half", [P, 1])
        xn = at.sb("xn", [RT, TILES, D])
        stats, moments = at.sb("stats", [RT, TILES, 6]), at.sb("moments", [RT, TILES, 2])
        rstd = at.sb("rstd", [RT, TILES])
        xnT = [at.sb(f"xnT_{n}", [P, KD, N], F32R) for n in ("hi", "lo")]
        q_sb = at.sb("q", [P, MD, N])
        ps_t = [at.psum(f"ps_t{i}", [P, 512]) for i in range(2)]
        ps_q = [at.psum(f"ps_q{i}", [P, 512]) for i in range(2)]
        ps_bias = at.psum("ps_bias", [P, 512])

        def ring(name, kind):
            return Ring(at.sem(f"{name}_full"), [at.sem(f"{name}_done{i}") for i in range(2)], [],
                        [u for u in turn if u[0] == kind], TURNS)

        TR, Q = ring("transposed", "xt"), ring("queries", "q")
        w_in, ln_in, w_hi, w_lo = at.sem("w_in"), at.sem("ln_in"), at.sem("w_hi"), at.sem("w_lo")
        bias_full, bias_ready = at.sem("bias_full"), at.sem("bias_ready")
        ident_ready = at.sem("ident_ready")
        dve_passed, sp_passed = at.sem("dve_passed"), at.sem("sp_passed")
        x_in, ln_step, xn_ready, xt_hi = at.sem("x_in"), at.sem("ln_step"), at.sem("xn_ready"), at.sem("xt_hi")
        var_ready, rstd_ready, first_ready = at.sem("var_ready"), at.sem("rstd_ready"), at.sem("first_ready")
        HALF = MD // 2
        q_stored = [at.sem(f"q_stored{i}") for i in range(2)]
        STORED = NB * DMA

        x_v = x1.rearrange("(i n) (t p) d -> i p n t d", n=NB, p=RT)
        q_v = q_T.rearrange("b (m p) t -> b p m t", p=P)

        with nc.Block() as block:

            @block.gpsimd
            def _(pool):
                make_constants(nc, pool, ident, minus_half, ident_ready)
                with pool.Fori(0, TURNS) as i:
                    for norm in range(2):
                        for t in range(TILES):
                            inverse_root(nc, pool, rstd[:, t:t + 1], moments[:, t, 1:2], minus_half[0:RT, :], var_ready,
                                         2 * TILES * i + norm * TILES + t, rstd_ready)

            @block.sync
            def _(sp):
                def load(i):
                    for n in range(NB):
                        sp.dma_start(xn[:, n * (TILES // NB):(n + 1) * (TILES // NB), :],
                                     x_v[bass.ds(i, 1), :, n].rearrange("o p t d -> (o p) t d")).then_inc(x_in, DMA)

                def store(i):
                    for half in range(2):
                        for m in range(half * HALF, (half + 1) * HALF)[-2:]:
                            sp.wait_ge(*Q.emptied(("q", m), ("turn", i)))
                            sp.sem_inc(sp_passed, 1)
                        for n in range(NB):
                            sp.dma_start(q_v[bass.ds(NB * i + n, 1), :, half * HALF:(half + 1) * HALF]
                                         .rearrange("o p m t -> (o p) m t"),
                                         q_sb[:, half * HALF:(half + 1) * HALF, n * T:(n + 1) * T]
                                         ).then_inc(q_stored[half], DMA)

                load(0)
                sp.dma_start(wq_raw[:, :, :], w_q.rearrange("(k p) n -> p k n", p=P)).then_inc(w_in, DMA)
                with nc.allow_non_contiguous_dma(reason="two vectors, once"):
                    sp.dma_start(s_col[:, :], ln1_s.rearrange("(k p) -> p k", p=P)).then_inc(ln_in, DMA)
                    sp.dma_start(b_col[:, :], ln1_b.rearrange("(k p) -> p k", p=P)).then_inc(ln_in, DMA)
                with sp.Fori(0, TURNS - 1) as i:
                    sp.wait_ge(xt_hi, TILES * i + TILES)
                    sp.sem_inc(sp_passed, 1)
                    load(i + 1)
                    store(i)
                store(TURNS - 1)
                for s in q_stored:
                    sp.wait_ge(s, STORED * TURNS + STORED)

            @block.tensor
            def _(pe):
                pe.wait_ge(ident_ready, 3)
                pe.wait_ge(w_in, DMA)
                pe.wait_ge(ln_in, 2 * DMA)
                for m in range(MD):
                    for k in range(KD):
                        ins = nc.tensor.matmul(ps_bias[:, m:m + 1], wq_raw[:, k, m * P:(m + 1) * P], b_col[:, k:k + 1],
                                               start=k == 0, stop=k == KD - 1)
                ins.then_inc(bias_full, 1)
                pe.wait_ge(w_lo, 1)
                with pe.Fori(0, TURNS) as i:
                    when = ("turn", i)
                    for t in range(TILES):
                        use = ("xt", t)
                        pe.wait_ge(xn_ready, TILES * i + t + 1)
                        pe.wait_ge(*TR.free(use, when))
                        for k in range(KD):
                            ins = nc.tensor.transpose(ps_t[t % 2][:, k * RT:(k + 1) * RT], xn[:, t, k * P:(k + 1) * P],
                                                      ident[0:RT, 0:RT])
                        ins.then_inc(TR.full, 1)
                    for t in (TILES - 2, TILES - 1):
                        pe.wait_ge(*TR.emptied(("xt", t), when))
                    for m in range(MD):
                        pe.wait_ge(*Q.free(("q", m), when))
                        for k in range(KD):
                            for n, (w, t) in enumerate(((0, 0), (0, 1), (1, 0))):
                                ins = nc.tensor.matmul(ps_q[m % 2][:, 0:N], wq[w][:, k, m * P:(m + 1) * P], xnT[t][:, k, :],
                                                       start=k == 0 and n == 0, stop=k == KD - 1 and n == 2)
                        ins.then_inc(Q.full, 1)

            @block.scalar
            def _(act):
                act.wait_ge(w_in, DMA)
                act.wait_ge(ln_in, 2 * DMA)
                for k in range(KD):
                    nc.scalar.activation(wq[0][:, k, :], wq_raw[:, k, :], ACT.Copy, scale=s_col[:, k:k + 1]).then_inc(w_hi, 1)
                act.wait_ge(bias_ready, 1)
                for s in q_stored:
                    act.sem_inc(s, STORED)
                with act.Fori(0, TURNS) as i:
                    when = ("turn", i)
                    for t in range(TILES):
                        act.wait_ge(*TR.filled(("xt", t), when))
                        nc.scalar.activation(xnT[0][:, :, t * RT:(t + 1) * RT],
                                             ps_t[t % 2][:, 0:KD * RT].rearrange("p (k t) -> p k t", k=KD),
                                             ACT.Copy).then_inc(xt_hi, 1)
                    for m in range(MD):
                        if m % HALF == 0:
                            act.wait_ge(q_stored[m // HALF], STORED * i + STORED)
                        act.wait_ge(*Q.filled(("q", m), when))
                        nc.scalar.activation(q_sb[:, m, :], ps_q[m % 2][:, 0:N], ACT.Identity, bias=qbias[:, m:m + 1],
                                             scale=QSCALE).then_inc(Q.done[m % 2], 1)

            @block.vector
            def _(dve):
                for r in (TR, Q):
                    for d in r.done:
                        dve.sem_inc(d, 1)
                for k in range(KD):
                    dve.wait_ge(w_hi, k + 1)
                    ins = nc.vector.scalar_tensor_tensor(wq[1][:, k, :], wq_raw[:, k, :], s_col[:, k:k + 1],
                                                         wq[0][:, k, :].bitcast(F32), ALU.mult, ALU.subtract)
                ins.then_inc(w_lo, 1)
                dve.wait_ge(bias_full, 1)
                nc.vector.tensor_scalar(qbias[:, :], ps_bias[:, 0:MD], QSCALE, None, ALU.mult).then_inc(bias_ready, 1)
                with dve.Fori(0, TURNS) as i:
                    dve.wait_ge(x_in, NB * DMA * i + NB * DMA)
                    for norm, eps in ((0, LN_EPS), (1, XLN_EPS)):
                        before = 2 * TILES * i + norm * TILES
                        for t in range(TILES):
                            if norm:
                                dve.wait_ge(first_ready, TILES * i + t + 1)
                            moments_of(nc, dve, xn[:, t, :], stats[:, t, :], moments[:, t, :], eps, ln_step,
                                       4 * TILES * i + 2 * (norm * TILES + t), var_ready, dve_passed)
                        for t in range(TILES):
                            dve.wait_ge(rstd_ready, before + t + 1)
                            nc.vector.tensor_scalar(xn[:, t, :], xn[:, t, :], moments[:, t, 0:1], rstd[:, t:t + 1],
                                                    ALU.subtract, ALU.mult).then_inc(xn_ready if norm else first_ready, 1)
                    for t in range(TILES):
                        dve.wait_ge(xt_hi, TILES * i + t + 1)
                        part = (slice(None), slice(None), slice(t * RT, (t + 1) * RT))
                        nc.vector.tensor_tensor(xnT[1][part], ps_t[t % 2][:, 0:KD * RT].rearrange("p (k t) -> p k t", k=KD),
                                                xnT[0][part].bitcast(F32), ALU.subtract).then_inc(TR.done[t % 2], 1)


def cross_attention(nc, context, mask, lnc_s, lnc_b, w_kv, null_kv, w_o, q_T, y):
    B, KEYS, D = context.shape
    T = q_T.shape[2]
    E = w_o.shape[0]
    DH = null_kv.shape[1]
    HEADS = E // DH
    QT = T // 2
    KD = D // P
    ED = E // P
    STEPS, GH = 4, HEADS // 4
    GE = GH * DH
    KT = -(-(KEYS + 1) // P)
    KP = KT * P
    HALF = KP // 2
    FULL_T, TAIL = KEYS // P, KEYS % P
    KCHUNK = KEYS // 2
    TURNS = B - 1

    def following(g):
        n = (g + 1) % STEPS
        return ([("K", n, 0), ("K", n, 1)], [("V", n, 0)], [("Q", n, 0), ("S", n, 0), ("S", n, 1)], [("V", n, 1)])

    def step(g, ahead):
        heads = [("T", g, 0), ("S", g, 2), ("T", g, 1), ("S", g, 3), ("PV", g, 0), ("R", g, 0)]
        if not ahead:
            return heads + [("T", g, 2), ("T", g, 3), ("PV", g, 1), ("R", g, 1)]
        k, v0, s, v1 = following(g)
        end = v0 + [("PV", g, 1), ("R", g, 1)] + s + v1
        if g < STEPS - 1:
            tiles = range(3 * (g - 1), 3 * g) if g else ()
            st, ln = [("st", 0, t) for t in tiles], [("ln", 0, t) for t in tiles]
            return (heads[0:2] + st[0:1] + heads[2:] + ln[0:1] + k[0:1] + st[1:2] + [("T", g, 2)] + ln[1:2] + k[1:2] + st[2:3]
                    + [("T", g, 3)] + ln[2:3] + end)
        xt = [("xt", 0, t) for t in range(KT)]
        mixed = []
        for t, u in enumerate(heads):
            mixed += [u, xt[t]]
        return mixed + k[0:1] + [("T", g, 2)] + k[1:2] + [("T", g, 3), ("mask", 0, 0)] + end

    def batch(ahead):
        order = []
        for g in range(STEPS):
            order += step(g, ahead or g < STEPS - 1)
        order += [("Wo", 0, 0), ("Wo", 0, 1)]
        return order if ahead else [u for u in order if u[0] not in ("st", "ln")]

    k0, v0, s0, v1 = following(STEPS - 1)
    first = [("st", 0, t) for t in range(KT)] + [("ln", 0, t) for t in range(KT)] + [("xt", 0, t) for t in range(KT)] + k0 + [("mask", 0, 0)] + v0 + s0 + v1
    turn, last = batch(True), batch(False)

    def uses(order, **count):
        out = []
        for u in order:
            if u[0] in count:
                out += [u + (i,) for i in range(count[u[0]])]
        return out

    with ExitStack() as ctx:
        at = Place(nc, ctx, "ca")
        wkv = [at.sb(f"wkv_{n}", [P, KD, 2 * E], F32R) for n in ("hi", "lo")]
        wo = [at.sb(f"wo_{n}", [P, ED, D], F32R) for n in ("hi", "lo")]
        kbias = at.sb("kbias", [P, ED])
        vbias = at.sb("vbias", [P, E])

        with ExitStack() as setup_ctx:
            su = Place(nc, setup_ctx, "cw")
            kv_raw, o_raw = su.sb("kv_raw", [P, KD, 2 * E]), su.sb("o_raw", [P, ED, D])
            s_col, b_col = su.sb("s_col", [P, KD]), su.sb("b_col", [P, KD])
            b_rows = su.sb("b_rows", [P, KD, P])
            ps_k = su.psum("ps_k", [P, 512])
            ps_v = su.psum("ps_v", [P, 2, 512])
            kv_in, o_in, ln_in = [su.sem(f"kv_in{k}") for k in range(KD)], su.sem("o_in"), su.sem("ln_in")
            hi_step, lo_step, rows_ready, bias_full = su.sem("hi_step"), su.sem("lo_step"), su.sem("rows_ready"), su.sem("bias_full")

            with nc.Block() as block:

                @block.sync
                def _(sp):
                    with nc.allow_non_contiguous_dma(reason="two vectors, once"):
                        sp.dma_start(s_col[:, :], lnc_s.rearrange("(k p) -> p k", p=P)).then_inc(ln_in, DMA)
                        sp.dma_start(b_col[:, :], lnc_b.rearrange("(k p) -> p k", p=P)).then_inc(ln_in, DMA)
                    for k in range(KD):
                        sp.dma_start(kv_raw[:, k, :], w_kv[k * P:(k + 1) * P, :]).then_inc(kv_in[k], DMA)
                    sp.dma_start(o_raw[:, :, :], w_o.rearrange("(k p) n -> p k n", p=P)).then_inc(o_in, DMA)

                @block.scalar
                def _(act):
                    act.wait_ge(ln_in, 2 * DMA)
                    for k in range(KD):
                        act.wait_ge(kv_in[k], DMA)
                        nc.scalar.activation(wkv[0][:, k, :], kv_raw[:, k, :], ACT.Copy, scale=s_col[:, k:k + 1]).then_inc(hi_step, 1)
                    act.wait_ge(o_in, DMA)
                    nc.scalar.activation(wo[0][:, :, :], o_raw[:, :, :], ACT.Copy).then_inc(hi_step, 1)

                @block.vector
                def _(dve):
                    dve.wait_ge(ln_in, 2 * DMA)
                    nc.vector.tensor_copy(b_rows[:, :, :], b_col[:, :].unsqueeze(2).to_broadcast([P, KD, P])).then_inc(rows_ready, 1)
                    for k in range(KD):
                        dve.wait_ge(hi_step, k + 1)
                        nc.vector.scalar_tensor_tensor(wkv[1][:, k, :], kv_raw[:, k, :], s_col[:, k:k + 1],
                                                       wkv[0][:, k, :].bitcast(F32), ALU.mult, ALU.subtract)
                    dve.wait_ge(hi_step, KD + 1)
                    nc.vector.tensor_tensor(wo[1][:, :, :], o_raw[:, :, :], wo[0][:, :, :].bitcast(F32), ALU.subtract)
                    dve.wait_ge(bias_full, 1)
                    nc.vector.tensor_copy(kbias[:, :], ps_k[:, 0:ED])
                    nc.vector.tensor_copy(vbias[:, :].rearrange("p (a n) -> p a n", a=2), ps_v[:, :, :]).then_inc(lo_step, 1)
                    dve.wait_ge(lo_step, 1)

                @block.tensor
                def _(pe):
                    pe.wait_ge(rows_ready, 1)
                    for k in range(KD):
                        pe.wait_ge(kv_in[k], DMA)
                    for m in range(ED):
                        for k in range(KD):
                            nc.tensor.matmul(ps_k[:, m:m + 1], kv_raw[:, k, m * P:(m + 1) * P], b_col[:, k:k + 1],
                                             start=k == 0, stop=k == KD - 1)
                    for a in range(2):
                        for k in range(KD):
                            ins = nc.tensor.matmul(ps_v[:, a, :], b_rows[:, k, :], kv_raw[:, k, E + a * 512:E + (a + 1) * 512],
                                                   start=k == 0, stop=k == KD - 1)
                    ins.then_inc(bias_full, 1)

        ident, minus_half = at.sb("ident", [P, P]), at.sb("minus_half", [P, 1])
        cn = at.sb("cn", [P, KT, D])
        stats, moments = at.sb("stats", [P, KT, 6]), at.sb("moments", [P, KT, 2])
        rstd = at.sb("rstd", [P, KT])
        cnT = [at.sb(f"cnT_{n}", [P, KD, KEYS + 2], F32R) for n in ("hi", "lo")]
        kstack = at.sb("kstack", [P, GH, KP], F32R)
        null_k = at.sb("null_k", [P, 1])
        null_part = [at.sb(f"null_{n}", [P, 1], F32R) for n in ("hi", "lo")]
        v_sb = at.sb("v", [P, 2, KT, GE])
        q_raw = at.sb("q_raw", [P, GH, T])
        q_part = [at.sb(f"q_{n}", [P, GH, T], F32R) for n in ("hi", "lo")]
        mask_u8 = at.sb("mask_u8", [QT, KEYS], U8)
        penalty = at.sb("penalty", [QT, KP])
        prob = at.sb("prob", [QT, 2, 2, KP])
        low = at.sb("low", [QT, 2, 2])
        sums, rsum = at.sb("sums", [QT, 2, 2, 2]), at.sb("rsum", [QT, 2, 2, P])
        probT = at.sb("probT", [P, 2, KT, T])
        spread = at.sb("spread", [P, 2, T])
        o_sb = at.sb("o", [P, T])
        oT = [at.sb(f"oT_{n}", [P, ED, T], F32R) for n in ("hi", "lo")]
        y_sb = at.sb("y", [QT, 2, D])

        ps_w = [at.psum(f"ps_w{i}", [P, 2, 512]) for i in range(2)]
        ps_t = [at.psum(f"ps_t{i}", [P, 512]) for i in range(2)]
        ps_o = [at.psum(f"ps_o{i}", [P, 512]) for i in range(2)]

        def ring(name, **count):
            return Ring(at.sem(f"{name}_full"), [at.sem(f"{name}_done{i}") for i in range(2)],
                        uses(first, **count), uses(turn, **count), TURNS, uses(last, **count))

        W = ring("wide", S=2, K=1, V=1)
        TR = ring("transposed", T=3, xt=1)
        O = ring("heads", PV=1, Wo=1)
        rings = [W, TR, O]

        ident_ready = at.sem("ident_ready")
        dve_passed, sp_passed = at.sem("dve_passed"), at.sem("sp_passed")
        ctx_in, mask_in, q_in, y_stored = at.sem("ctx_in"), at.sem("mask_in"), at.sem("q_in"), at.sem("y_stored")
        null_in, null_step, fixed_ready, nullv_in = at.sem("null_in"), at.sem("null_step"), at.sem("fixed_ready"), at.sem("nullv_in")
        var_ready, rstd_ready = at.sem("var_ready"), at.sem("rstd_ready")
        ln_step, cn_ready, xt_hi, k_hi = at.sem("ln_step"), at.sem("cn_ready"), at.sem("xt_hi"), at.sem("k_hi")
        q_hi, q_lo, mask_ready = at.sem("q_hi"), at.sem("q_lo"), at.sem("mask_ready")
        exp_done, rsum_ready, spread_ready, o_step = at.sem("exp_done"), at.sem("rsum_ready"), at.sem("spread_ready"), at.sem("o_step")

        ctx_full = context[:, 0:FULL_T * P, :].rearrange("b (t p) d -> b p t d", p=P)
        q_v = q_T.rearrange("b (h d) t -> b d h t", d=DH)
        y_v = y.rearrange("b (q p) d -> b p q d", p=QT)
        ROWS = [P] * FULL_T + [TAIL]

        def owner(use, b):
            return b + 1 if use[0] in ("st", "ln", "xt", "mask") or (use[1] == 0 and (use[0] in ("K", "V", "Q") or (use[0] == "S" and use[2] < 2))) else b

        with nc.Block() as block:

            @block.gpsimd
            def _(pool):
                make_constants(nc, pool, ident, minus_half, ident_ready)
                nc.gpsimd.memset(kstack[:, :, KEYS + 1:KP].bitcast(F32), 0.0).then_inc(fixed_ready, 1)
                for c in cnT:
                    nc.gpsimd.memset(c[:, :, KEYS:KEYS + 2].bitcast(F32), 0.0).then_inc(fixed_ready, 1)
                nc.gpsimd.memset(penalty[:, KEYS:KEYS + 1], 0.0).then_inc(fixed_ready, 1)
                nc.gpsimd.memset(penalty[:, KEYS + 1:KP], BIG).then_inc(fixed_ready, 1)
                pool.wait_ge(fixed_ready, 5)
                nc.gpsimd.memset(v_sb[96:P, :, KT - 1, :], 0.0).then_inc(fixed_ready, 1)
                with pool.Fori(0, B) as b:
                    for t, n in enumerate(ROWS):
                        inverse_root(nc, pool, rstd[0:n, t:t + 1], moments[0:n, t, 1:2], minus_half[0:n, :], var_ready, KT * b + t, rstd_ready)

            @block.sync
            def _(sp):
                def load_context(b):
                    sp.dma_start(cn[:, 0:FULL_T, :], ctx_full[bass.ds(b, 1)].rearrange("o p t d -> (o p) t d")).then_inc(ctx_in, DMA)
                    sp.dma_start(cn[0:TAIL, FULL_T, :], context[bass.ds(b, 1), FULL_T * P:KEYS, :]
                                 .rearrange("o p d -> (o p) d")).then_inc(ctx_in, DMA)

                def load_mask(b):
                    sp.dma_start(mask_u8[:, :], mask[bass.ds(b, 1), :].rearrange("o s -> (o s)").partition_broadcast(QT)).then_inc(mask_in, DMA)

                def load_queries(b, g):
                    for half in range(2):
                        sp.dma_start(q_raw[half * DH:(half + 1) * DH, :, :],
                                     q_v[bass.ds(b, 1), :, g * GH:(g + 1) * GH].rearrange("o d h t -> (o d) h t")).then_inc(q_in, DMA)

                def store(b, when):
                    sp.wait_ge(*O.emptied(("Wo", 0, 0, 0), when))
                    sp.sem_inc(sp_passed, 1)
                    sp.wait_ge(*O.emptied(("Wo", 0, 1, 0), when))
                    sp.sem_inc(sp_passed, 1)
                    sp.dma_start(y_v[bass.ds(b, 1)].rearrange("o p q d -> (o p) q d"), y_sb[:, :, :]).then_inc(y_stored, DMA)

                load_context(0)
                load_mask(0)
                load_queries(0, 0)
                for half in range(2):
                    sp.dma_start(null_k[half * DH:(half + 1) * DH, :], null_kv[0:1, :].rearrange("o (d x) -> (o d) x", x=1)).then_inc(null_in, DMA)
                sp.wait_ge(fixed_ready, 6)
                for n in range(2):
                    for h in range(GH):
                        sp.dma_start(v_sb[TAIL:TAIL + 1, n, KT - 1, h * DH:(h + 1) * DH], null_kv[1:2, :]).then_inc(nullv_in, DMA)
                sp.wait_ge(q_lo, 1)
                load_queries(0, 1)
                with sp.Fori(0, TURNS) as b:
                    when = ("turn", b)
                    sp.wait_ge(xt_hi, KT * b + KT)
                    sp.sem_inc(sp_passed, 1)
                    load_context(b + 1)
                    sp.wait_ge(mask_ready, b + 1)
                    sp.sem_inc(sp_passed, 1)
                    load_mask(b + 1)
                    for g in range(STEPS):
                        sp.wait_ge(q_lo, STEPS * b + g + 2)
                        sp.sem_inc(sp_passed, 1)
                        if g + 2 < STEPS:
                            load_queries(b, g + 2)
                        else:
                            load_queries(b + 1, g + 2 - STEPS)
                    store(b, when)
                for g in range(STEPS - 2):
                    sp.wait_ge(q_lo, STEPS * TURNS + g + 2)
                    sp.sem_inc(sp_passed, 1)
                    load_queries(TURNS, g + 2)
                store(TURNS, ("last", TURNS))
                sp.wait_ge(y_stored, DMA * B + DMA)

            @block.tensor
            def _(pe):
                def split_products(out, lhs, rhs, first_, last_):
                    for n, (i, j) in enumerate(((0, 0), (0, 1), (1, 0))):
                        ins = nc.tensor.matmul(out, lhs[i], rhs[j], start=first_ and n == 0, stop=last_ and n == 2)
                    return ins

                def run(order, turn_b, when):
                    for task in order:
                        kind, g, i = task
                        b = owner(task, turn_b)
                        if kind == "S":
                            if i == 0:
                                pe.wait_ge(q_lo, STEPS * b + g + 1)
                                for j in range(2):
                                    pe.wait_ge(*W.emptied(("K", g, j, 0), when))
                            for q in range(2):
                                use = task + (q,)
                                pe.wait_ge(*W.free(use, when))
                                out = ps_w[W.slot(use, when)]
                                for n in range(2):
                                    for c in range(2):
                                        ins = nc.tensor.matmul(out[0:QT, c, 0:HALF], q_part[n][:, i, q * QT:(q + 1) * QT],
                                                               kstack[:, i, c * HALF:(c + 1) * HALF], start=n == 0, stop=n == 1)
                                ins.then_inc(W.full, 1)
                        elif kind == "T":
                            pe.wait_ge(exp_done, 2 * (HEADS * b + GH * g + i) + 2)
                            for u in range(KT // 2):
                                use = task + (u,)
                                pe.wait_ge(*TR.free(use, when))
                                out = ps_t[TR.slot(use, when)]
                                for k in range(2):
                                    for q in range(2):
                                        ins = nc.tensor.transpose(out[:, k * T + q * QT:k * T + (q + 1) * QT],
                                                                  prob[:, i % 2, q, (2 * u + k) * P:(2 * u + k + 1) * P],
                                                                  ident[0:QT, 0:QT])
                                ins.then_inc(TR.full, 1)
                        elif kind == "PV":
                            for u in (1, 2):
                                pe.wait_ge(*TR.emptied(("T", g, 2 * i + 1, u), when))
                            if i == 0:
                                for j in range(2):
                                    pe.wait_ge(*(W.emptied_before if g == 0 else W.emptied)(("V", g, j, 0), when))
                            use = task + (0,)
                            pe.wait_ge(*O.free(use, when))
                            out = ps_o[O.slot(use, when)]
                            for k in range(KT):
                                for j in range(2):
                                    col = (2 * i + j) * DH
                                    nc.tensor.matmul(out[j * DH:(j + 1) * DH, 0:T], v_sb[:, g % 2, k, col:col + DH],
                                                     probT[:, j, k, :], start=k == 0, stop=k == KT - 1)
                        elif kind == "R":
                            pe.wait_ge(rsum_ready, ED * b + 2 * g + i + 1)
                            out = ps_o[O.slot(("PV", g, i, 0), when)]
                            for q in range(2):
                                ins = nc.tensor.transpose(out[:, 256 + q * QT:256 + (q + 1) * QT], rsum[:, i, q, :], ident[0:QT, 0:QT])
                            ins.then_inc(O.full, 1)
                        elif kind == "xt":
                            use = task + (0,)
                            pe.wait_ge(cn_ready, KT * b + i + 1)
                            pe.wait_ge(*TR.free(use, when))
                            out = ps_t[TR.slot(use, when)]
                            n = ROWS[i]
                            for k in range(KD):
                                ins = nc.tensor.transpose(out[:, k * P:k * P + n], cn[0:n, i, k * P:(k + 1) * P], ident[0:n, 0:n])
                            ins.then_inc(TR.full, 1)
                        elif kind == "K":
                            if g == 0 and i == 0:
                                for t in (KT - 2, KT - 1):
                                    pe.wait_ge(*TR.emptied(("xt", 0, t, 0), when))
                            use = task + (0,)
                            pe.wait_ge(*W.free(use, when))
                            out = ps_w[W.slot(use, when)]
                            col = (2 * g + i) * P
                            for c in range(2):
                                for k in range(KD):
                                    ins = split_products(out[:, c, 0:KCHUNK + 1], [w[:, k, col:col + P] for w in wkv],
                                                         [t[:, k, c * KCHUNK:(c + 1) * KCHUNK + 1] for t in cnT], k == 0, k == KD - 1)
                            ins.then_inc(W.full, 1)
                        elif kind == "V":
                            use = task + (0,)
                            pe.wait_ge(*W.free(use, when))
                            out = ps_w[W.slot(use, when)]
                            col = E + g * GE
                            for t in (range(4) if i == 0 else range(4, KT)):
                                n = ROWS[t]
                                for k in range(KD):
                                    ins = split_products(out[0:n, (t % 4) // 2, (t % 2) * GE:(t % 2 + 1) * GE],
                                                         [c[:, k, t * P:t * P + n] for c in cnT],
                                                         [w[:, k, col:col + GE] for w in wkv], k == 0, k == KD - 1)
                            ins.then_inc(W.full, 1)
                        elif kind == "Wo":
                            use = task + (0,)
                            for p in range(2):
                                pe.wait_ge(*O.emptied(("PV", STEPS - 1, p, 0), when))
                            pe.wait_ge(*O.free(use, when))
                            out = ps_o[O.slot(use, when)]
                            for m in range(ED):
                                ins = split_products(out[0:QT, :], [o[:, m, i * QT:(i + 1) * QT] for o in oT],
                                                     [w[:, m, :] for w in wo], m == 0, m == ED - 1)
                            ins.then_inc(O.full, 1)

                pe.wait_ge(ident_ready, 3)
                pe.wait_ge(fixed_ready, 6)
                pe.wait_ge(null_step, 6)
                pe.wait_ge(nullv_in, 2 * GH * DMA)
                run(first, -1, ("first", 0))
                with pe.Fori(0, TURNS) as b:
                    run(turn, b, ("turn", b))
                run(last, TURNS, ("last", TURNS))

            @block.scalar
            def _(act):
                def run(order, turn_b, when):
                    for task in order:
                        kind, g, i = task
                        b = owner(task, turn_b)
                        if kind == "S":
                            for q in range(2):
                                act.wait_ge(*W.emptied(task + (q,), when))
                                nc.scalar.activation(prob[:, i % 2, q, :], prob[:, i % 2, q, :], ACT.Exp,
                                                     bias=low[:, i % 2, q:q + 1], scale=-1.0,
                                                     accum_out=sums[:, i // 2, q, i % 2:i % 2 + 1]).then_inc(exp_done, 1)
                        elif kind == "T":
                            for u in (0, 2):
                                use = task + (u,)
                                act.wait_ge(*TR.filled(use, when))
                                src = ps_t[TR.slot(use, when)]
                                nc.scalar.activation(probT[:, i % 2, 2 * u:2 * u + 2, :],
                                                     src[:, 0:2 * T].rearrange("p (k t) -> p k t", k=2),
                                                     ACT.Copy).then_inc(TR.done[TR.slot(use, when)], 1)
                        elif kind == "R":
                            use = ("PV", g, i, 0)
                            act.wait_ge(*O.filled(use, when))
                            nc.scalar.activation(spread[:, i, :], ps_o[O.slot(use, when)][:, 256:256 + T], ACT.Copy).then_inc(spread_ready, 1)
                        elif kind == "xt":
                            use = task + (0,)
                            act.wait_ge(*TR.filled(use, when))
                            n = ROWS[i]
                            nc.scalar.activation(cnT[0][:, :, i * P:i * P + n],
                                                 ps_t[TR.slot(use, when)][:, :].rearrange("p (k t) -> p k t", k=KD)[:, :, 0:n],
                                                 ACT.Copy).then_inc(xt_hi, 1)
                        elif kind == "K":
                            use = task + (0,)
                            act.wait_ge(*W.filled(use, when))
                            src = ps_w[W.slot(use, when)]
                            for j in range(2):
                                rows = slice(j * DH, (j + 1) * DH)
                                ins = nc.scalar.activation(kstack[rows, 2 * i + j, 0:KEYS].rearrange("p (c s) -> p c s", c=2),
                                                           src[rows, :, 0:KCHUNK], ACT.Identity,
                                                           bias=kbias[rows, 2 * g + i:2 * g + i + 1], scale=1.0)
                            ins.then_inc(k_hi, 1)
                        elif kind == "Q":
                            act.wait_ge(q_in, 2 * DMA * (STEPS * b + g) + 2 * DMA)
                            if when[0] != "first":
                                act.wait_ge(*W.filled(("S", (g - 1) % STEPS, GH - 1, 1), when))
                            nc.scalar.activation(q_part[0][:, :, :], q_raw[:, :, :], ACT.Copy).then_inc(q_hi, 1)
                        elif kind == "Wo":
                            use = task + (0,)
                            if i == 0:
                                act.wait_ge(y_stored, DMA * b + DMA)
                            act.wait_ge(*O.filled(use, when))
                            nc.scalar.activation(y_sb[:, i, :], ps_o[O.slot(use, when)][0:QT, :], ACT.Copy).then_inc(O.done[O.slot(use, when)], 1)

                act.sem_inc(y_stored, DMA)
                act.wait_ge(fixed_ready, 6)
                run(first, -1, ("first", 0))
                with act.Fori(0, TURNS) as b:
                    run(turn, b, ("turn", b))
                run(last, TURNS, ("last", TURNS))

            @block.vector
            def _(dve):
                def run(order, turn_b, when):
                    for task in order:
                        kind, g, i = task
                        b = owner(task, turn_b)
                        if kind == "S":
                            for q in range(2):
                                use = task + (q,)
                                dve.wait_ge(*W.filled(use, when))
                                if i == 0 and g == 0 and q == 0:
                                    dve.wait_ge(mask_ready, b + 1)
                                dve.sem_inc(dve_passed, 1)
                                dst = prob[:, i % 2, q, :].rearrange("p (c s) -> p c s", c=2)
                                nc.vector.tensor_tensor_reduce(out=dst, in0=ps_w[W.slot(use, when)][0:QT, :, 0:HALF],
                                                               in1=penalty[:, :].rearrange("p (c s) -> p c s", c=2),
                                                               scale=1.0, scalar=BIG, op0=ALU.add, op1=ALU.min,
                                                               accum_out=low[:, i % 2, q:q + 1]).then_inc(W.done[W.slot(use, when)], 1)
                        elif kind == "T":
                            use = task + (1,)
                            dve.wait_ge(*TR.filled(use, when))
                            nc.vector.tensor_copy(probT[:, i % 2, 2:4, :],
                                                  ps_t[TR.slot(use, when)][:, 0:2 * T].rearrange("p (k t) -> p k t", k=2)
                                                  ).then_inc(TR.done[TR.slot(use, when)], 1)
                            if i % 2 == 1:
                                dve.wait_ge(exp_done, 2 * (HEADS * b + GH * g + i) + 2)
                                nc.vector.reciprocal(rsum[:, i // 2, :, :].rearrange("p q (j d) -> p (q j) d", d=DH),
                                                     sums[:, i // 2, :, :].rearrange("p q j -> p (q j)").unsqueeze(2)
                                                     .to_broadcast([QT, 4, DH])).then_inc(rsum_ready, 1)
                        elif kind == "R":
                            use = ("PV", g, i, 0)
                            m = 2 * g + i
                            steps = 2 * (ED * b + m)
                            dve.wait_ge(spread_ready, ED * b + m + 1)
                            nc.vector.tensor_tensor(o_sb[:, :], ps_o[O.slot(use, when)][:, 0:T], spread[:, i, :], ALU.mult).then_inc(o_step, 1)
                            dve.wait_ge(o_step, steps + 1)
                            nc.vector.tensor_copy(oT[0][:, m, :], o_sb[:, :]).then_inc(o_step, 1)
                            dve.wait_ge(o_step, steps + 2)
                            nc.vector.tensor_tensor(oT[1][:, m, :], o_sb[:, :], oT[0][:, m, :].bitcast(F32),
                                                    ALU.subtract).then_inc(O.done[O.slot(use, when)], 1)
                        elif kind == "st":
                            if i == 0:
                                dve.wait_ge(ctx_in, 2 * DMA * b + 2 * DMA)
                            n = ROWS[i]
                            moments_of(nc, dve, cn[0:n, i, :], stats[0:n, i, :], moments[0:n, i, :], XLN_EPS, ln_step,
                                       2 * (KT * b + i), var_ready, dve_passed)
                        elif kind == "ln":
                            n = ROWS[i]
                            dve.wait_ge(rstd_ready, KT * b + i + 1)
                            nc.vector.tensor_scalar(cn[0:n, i, :], cn[0:n, i, :], moments[0:n, i, 0:1], rstd[0:n, i:i + 1],
                                                    ALU.subtract, ALU.mult).then_inc(cn_ready, 1)
                        elif kind == "xt":
                            use = task + (0,)
                            dve.wait_ge(xt_hi, KT * b + i + 1)
                            n = ROWS[i]
                            part = (slice(None), slice(None), slice(i * P, i * P + n))
                            nc.vector.tensor_tensor(cnT[1][part], ps_t[TR.slot(use, when)][:, :].rearrange("p (k t) -> p k t", k=KD)[:, :, 0:n],
                                                    cnT[0][part].bitcast(F32), ALU.subtract).then_inc(TR.done[TR.slot(use, when)], 1)
                        elif kind == "K":
                            use = task + (0,)
                            dve.wait_ge(k_hi, 2 * (STEPS * b + g) + i + 1)
                            src = ps_w[W.slot(use, when)]
                            for j in range(2):
                                rows, other = slice(j * DH, (j + 1) * DH), slice((1 - j) * DH, (2 - j) * DH)
                                ins = nc.vector.scalar_tensor_tensor(
                                    kstack[other, 2 * i + j, 0:KEYS].rearrange("p (c s) -> p c s", c=2), src[rows, :, 0:KCHUNK],
                                    kbias[rows, 2 * g + i:2 * g + i + 1],
                                    kstack[rows, 2 * i + j, 0:KEYS].bitcast(F32).rearrange("p (c s) -> p c s", c=2),
                                    ALU.add, ALU.subtract)
                            ins.then_inc(W.done[W.slot(use, when)], 1)
                        elif kind == "V":
                            use = task + (0,)
                            dve.wait_ge(*W.filled(use, when))
                            src = ps_w[W.slot(use, when)][:, :, :].rearrange("p a (t n) -> p (a t) n", t=2)
                            bias = vbias[:, g * GE:(g + 1) * GE]
                            if i == 0:
                                ins = nc.vector.tensor_tensor(v_sb[:, g % 2, 0:4, :], src, bias.unsqueeze(1).to_broadcast([P, 4, GE]), ALU.add)
                            else:
                                for t in range(4, KT):
                                    n = ROWS[t]
                                    ins = nc.vector.tensor_tensor(v_sb[0:n, g % 2, t, :], src[0:n, t % 4, :], bias[0:n, :], ALU.add)
                            ins.then_inc(W.done[W.slot(use, when)], 1)
                        elif kind == "Q":
                            dve.wait_ge(q_hi, STEPS * b + g + 1)
                            nc.vector.tensor_tensor(q_part[1][:, :, :], q_raw[:, :, :], q_part[0][:, :, :].bitcast(F32),
                                                    ALU.subtract).then_inc(q_lo, 1)
                        elif kind == "mask":
                            dve.wait_ge(mask_in, DMA * b + DMA)
                            nc.vector.tensor_scalar(penalty[:, 0:KEYS], mask_u8[:, :], -1.0, -BIG, ALU.add, ALU.mult).then_inc(mask_ready, 1)

                for r in rings:
                    for d in r.done:
                        dve.sem_inc(d, 1)
                dve.wait_ge(null_in, 2 * DMA)
                nc.vector.tensor_copy(null_part[0][:, :], null_k[:, :]).then_inc(null_step, 1)
                dve.wait_ge(null_step, 1)
                nc.vector.tensor_tensor(null_part[1][:, :], null_k[:, :], null_part[0][:, :].bitcast(F32), ALU.subtract).then_inc(null_step, 1)
                dve.wait_ge(null_step, 2)
                dve.wait_ge(fixed_ready, 6)
                for j in range(2):
                    for half in range(2):
                        rows = slice(half * DH, (half + 1) * DH)
                        nc.vector.tensor_copy(kstack[rows, j:GH:2, KEYS:KEYS + 1],
                                              null_part[(half + j) % 2][rows, :].bitcast(F32).unsqueeze(1).to_broadcast([DH, GH // 2, 1])
                                              ).then_inc(null_step, 1)
                run(first, -1, ("first", 0))
                with dve.Fori(0, TURNS) as b:
                    run(turn, b, ("turn", b))
                run(last, TURNS, ("last", TURNS))


def feed_forward(nc, x1, y, lno_s, lno_b, weight, gate_w, lora_U, lora_V, out):
    B, T, D = x1.shape
    NE, RANK, _ = lora_U.shape
    ER = NE * RANK
    KD = D // P
    TILES = B * T // P
    TURNS = TILES - 1
    MIX = ER + NE

    begin = [("yln", 1), ("x2", 1), ("xln", 1), ("xt", 1), ("ug", 1), ("base", 1)]
    both = [("gmax", 0), ("yln", 1), ("x2", 1), ("gate", 0), ("xln", 1), ("xt", 1), ("gT", 0), ("ug", 1), ("lora", 0), ("base", 1), ("fin", 0)]
    finish = [("gmax", 0), ("gate", 0), ("gT", 0), ("lora", 0), ("fin", 0)]

    with ExitStack() as ctx:
        at = Place(nc, ctx, "ff")
        w_raw = at.sb("w_raw", [P, KD, D])
        u_raw, g_raw = at.sb("u_raw", [ER, D]), at.sb("g_raw", [NE, D])
        v_raw = at.sb("v_raw", [P, KD, NE, RANK])
        wT = [at.sb(f"wT_{n}", [P, KD, D], F32R) for n in ("hi", "lo")]
        mixT = [at.sb(f"mixT_{n}", [P, KD, MIX], F32R) for n in ("hi", "lo")]
        vT = [at.sb(f"vT_{n}", [P, D], F32R) for n in ("hi", "lo")]
        s_rows, b_rows = at.sb("s_rows", [P, D]), at.sb("b_rows", [P, D])
        ident, minus_half = at.sb("ident", [P, P]), at.sb("minus_half", [P, 1])
        y_sb, x1_sb = at.sb("y", [P, 2, D]), at.sb("x1", [P, 2, D])
        xb = at.sb("xb", [P, 2, D])
        t_sb = at.sb("t", [P, D])
        x2 = at.sb("x2", [P, 2, D])
        xn = at.sb("xn", [P, D])
        x3 = at.sb("x3", [P, 2, D])
        stats, moments, rstd = at.sb("stats", [P, 2, 6]), at.sb("moments", [P, 2, 2]), at.sb("rstd", [P, 2])
        xnT = [at.sb(f"xnT_{n}", [P, KD, P], F32R) for n in ("hi", "lo")]
        negmax, esum, ersum = at.sb("negmax", [P, 1]), at.sb("esum", [P, 1]), at.sb("ersum", [P, 1])
        egate, gate = at.sb("egate", [P, NE]), at.sb("gate", [P, NE])
        gt = at.sb("gt", [P, NE, RANK])
        gT = [at.sb(f"gT_{n}", [P, P], F32R) for n in ("hi", "lo")]

        ps_t = [at.psum(f"ps_t{i}", [P, 512]) for i in range(2)]
        ps_u = [at.psum(f"ps_u{i}", [P, 512]) for i in range(2)]
        ps_b = [at.psum(f"ps_b{i}", [P, 512]) for i in range(2)]

        w_in = at.sem("w_in")
        dve_passed, sp_passed = at.sem("dve_passed"), at.sem("sp_passed")
        ident_ready, setup_full, setup_hi, setup_lo = at.sem("ident_ready"), at.sem("setup_full"), at.sem("setup_hi"), at.sem("setup_lo")
        y_in = [at.sem(f"y_in{i}") for i in range(2)]
        xb_ready, ln_step, xn_ready = at.sem("xb_ready"), at.sem("ln_step"), at.sem("xn_ready")
        var_ready, rstd_ready, x2_ready = at.sem("var_ready"), at.sem("rstd_ready"), at.sem("x2_ready")
        xt_full, xt_hi, xt_lo = at.sem("xt_full"), at.sem("xt_hi"), at.sem("xt_lo")
        ug_full, base_full, lora_full = at.sem("ug_full"), at.sem("base_full"), at.sem("lora_full")
        negmax_ready, egate_ready, gate_step, gt_ready = at.sem("negmax_ready"), at.sem("egate_ready"), at.sem("gate_step"), at.sem("gt_ready")
        gT_full, gT_hi, gT_lo = at.sem("gT_full"), at.sem("gT_hi"), at.sem("gT_lo")
        x3_ready = at.sem("x3_ready")
        out_stored = [at.sem(f"out_stored{i}") for i in range(2)]

        rows = [v.rearrange("b t d -> (b t) d").rearrange("(n p) d -> n p d", p=P) for v in (y, x1, out)]
        setup = ([("wT", k) for k in range(KD)] + [("mixT", k) for k in range(KD)] + [("vT", 0)])
        banks = ps_t + ps_u + ps_b

        def setup_parts(use):
            kind, k = use
            return {"wT": ([w[:, k, :] for w in wT], D), "mixT": ([w[:, k, :] for w in mixT], MIX),
                    "vT": ([w[:, :] for w in vT], D)}[kind]

        def count_of(t, each, p, half, parity):
            if half is None:
                return each * (t // 2 + 1)
            return each * half + each * (2 if parity == 1 else 1)

        def all_tiles(engine, run):
            run(begin, -1, 1)
            with engine.Fori(0, (TILES - 2) // 2) as j:
                for u in range(2):
                    run(both, 2 * j + u, u, j)
            run(both, TILES - 2, 0)
            run(finish, TILES - 1, 1)

        with nc.Block() as block:

            @block.gpsimd
            def _(pool):
                make_constants(nc, pool, ident, minus_half, ident_ready)
                pool.wait_ge(w_in, 9 * DMA)

                def run(order, n, parity, half=None):
                    for kind, ahead in order:
                        t, p = n + 1, (parity + 1) % 2
                        if kind == "yln":
                            pool.wait_ge(y_in[p], count_of(t, 2 * DMA, p, half, parity))
                            nc.gpsimd.tensor_tensor(xb[:, p, :], x1_sb[:, p, :], b_rows[:, :], ALU.add).then_inc(xb_ready, 1)
                            inverse_root(nc, pool, rstd[:, 0:1], moments[:, 0, 1:2], minus_half[:, :], var_ready, 2 * t, rstd_ready)
                        elif kind == "xln":
                            inverse_root(nc, pool, rstd[:, 1:2], moments[:, 1, 1:2], minus_half[:, :], var_ready, 2 * t + 1, rstd_ready)

                all_tiles(pool, run)

            @block.sync
            def _(sp):
                def load(t, p):
                    for v, buf in zip(rows[0:2], (y_sb, x1_sb)):
                        sp.dma_start(buf[:, p, :], v[bass.ds(t, 1)].rearrange("o p d -> (o p) d")).then_inc(y_in[p], DMA)

                def store(n, p):
                    sp.wait_ge(x3_ready, n + 3)
                    sp.sem_inc(sp_passed, 1)
                    sp.dma_start(rows[2][bass.ds(n, 1)].rearrange("o p d -> (o p) d"), x3[:, p, :]).then_inc(out_stored[p], DMA)

                load(0, 0)
                sp.dma_start(s_rows[:, :], lno_s.partition_broadcast(P)).then_inc(w_in, DMA)
                sp.dma_start(b_rows[:, :], lno_b.partition_broadcast(P)).then_inc(w_in, DMA)
                sp.dma_start(w_raw[:, :, :], weight.rearrange("(k p) n -> p k n", p=P)).then_inc(w_in, DMA)
                sp.dma_start(u_raw[:, :], lora_U.rearrange("e r n -> (e r) n")).then_inc(w_in, DMA)
                sp.dma_start(g_raw[:, :], gate_w).then_inc(w_in, DMA)
                for k in range(KD):
                    sp.dma_start(v_raw[:, k, :, :], lora_V[:, k * P:(k + 1) * P, :].rearrange("e o r -> o e r")).then_inc(w_in, DMA)
                load(1, 1)
                with sp.Fori(0, (TILES - 2) // 2) as j:
                    for u in range(2):
                        sp.wait_ge(xn_ready, 2 * j + u + 1)
                        sp.sem_inc(sp_passed, 1)
                        load(2 * j + u + 2, u)
                        store(2 * j + u, u)
                store(TILES - 2, 0)
                store(TILES - 1, 1)
                for s in out_stored:
                    sp.wait_ge(s, DMA * (TILES // 2) + DMA)

            @block.tensor
            def _(pe):
                def split_products(out, lhs, rhs, first, last):
                    for n, (i, j) in enumerate(((0, 0), (0, 1), (1, 0))):
                        ins = nc.tensor.matmul(out, lhs[i], rhs[j], start=first and n == 0, stop=last and n == 2)
                    return ins

                def run(order, n, parity, half=None):
                    for kind, ahead in order:
                        t, p = n + ahead, (parity + ahead) % 2
                        if kind == "xt":
                            pe.wait_ge(xn_ready, t + 1)
                            if order is both:
                                pe.wait_ge(xt_lo, t)
                            for k in range(KD):
                                ins = nc.tensor.transpose(ps_t[0][:, k * P:(k + 1) * P], xn[:, k * P:(k + 1) * P], ident[:, :])
                            ins.then_inc(xt_full, 1)
                        elif kind == "ug":
                            pe.wait_ge(xt_lo, t + 1)
                            for k in range(KD):
                                ins = split_products(ps_u[p][:, 0:MIX], [x[:, k, :] for x in xnT], [w[:, k, :] for w in mixT],
                                                     k == 0, k == KD - 1)
                            ins.then_inc(ug_full, 1)
                        elif kind == "base":
                            pe.wait_ge(x3_ready, t + 1)
                            for k in range(KD):
                                split_products(ps_b[p][:, :], [x[:, k, :] for x in xnT], [w[:, k, :] for w in wT], k == 0, False)
                        elif kind == "gT":
                            pe.wait_ge(gt_ready, t + 1)
                            nc.tensor.transpose(ps_t[1][:, 0:ER], gt[:, :, :].rearrange("p e r -> p (e r)"), ident[:, :]).then_inc(gT_full, 1)
                        elif kind == "lora":
                            pe.wait_ge(gT_lo, t + 1)
                            split_products(ps_b[p][:, :], [g[:, :] for g in gT], [v[:, :] for v in vT], False, True).then_inc(lora_full, 1)

                pe.wait_ge(ident_ready, 3)
                pe.wait_ge(w_in, 9 * DMA)
                for j, (kind, k) in enumerate(setup):
                    bank = banks[j % len(banks)]
                    if j >= len(banks):
                        pe.wait_ge(setup_lo, j - len(banks) + 1)
                    if kind == "wT":
                        for o in range(KD):
                            ins = nc.tensor.transpose(bank[:, o * P:(o + 1) * P], w_raw[:, o, k * P:(k + 1) * P], ident[:, :])
                    elif kind == "mixT":
                        nc.tensor.transpose(bank[:, 0:ER], u_raw[:, k * P:(k + 1) * P], ident[:, :])
                        ins = nc.tensor.transpose(bank[:, ER:MIX], g_raw[:, k * P:(k + 1) * P], ident[0:NE, 0:NE])
                    else:
                        for o in range(KD):
                            ins = nc.tensor.transpose(bank[:, o * P:(o + 1) * P], v_raw[:, o, :, :].rearrange("p e r -> p (e r)"), ident[:, :])
                    ins.then_inc(setup_full, 1)
                pe.wait_ge(setup_lo, len(setup))
                all_tiles(pe, run)

            @block.scalar
            def _(act):
                for j, use in enumerate(setup):
                    parts, n = setup_parts(use)
                    act.wait_ge(setup_full, j + 1)
                    nc.scalar.activation(parts[0], banks[j % len(banks)][:, 0:n], ACT.Copy).then_inc(setup_hi, 1)

                def run(order, n, parity, half=None):
                    for kind, ahead in order:
                        t, p = n + ahead, (parity + ahead) % 2
                        if kind == "gmax":
                            act.wait_ge(negmax_ready, t + 1)
                            nc.scalar.activation(egate[:, :], ps_u[p][:, ER:MIX], ACT.Exp, bias=negmax[:, :], scale=1.0,
                                                 accum_out=esum[:, :]).then_inc(egate_ready, 1)
                        elif kind == "xt":
                            act.wait_ge(xt_full, t + 1)
                            nc.scalar.activation(xnT[0][:, :, :], ps_t[0][:, :].rearrange("p (k t) -> p k t", k=KD),
                                                 ACT.Copy).then_inc(xt_hi, 1)
                        elif kind == "gT":
                            act.wait_ge(gT_full, t + 1)
                            nc.scalar.activation(gT[0][:, :], ps_t[1][:, 0:ER], ACT.Copy).then_inc(gT_hi, 1)

                all_tiles(act, run)

            @block.vector
            def _(dve):
                dve.sem_inc(x3_ready, 2)
                for s in out_stored:
                    dve.sem_inc(s, DMA)
                for j, use in enumerate(setup):
                    parts, n = setup_parts(use)
                    dve.wait_ge(setup_hi, j + 1)
                    nc.vector.tensor_tensor(parts[1], banks[j % len(banks)][:, 0:n], parts[0].bitcast(F32),
                                            ALU.subtract).then_inc(setup_lo, 1)
                dve.wait_ge(w_in, 9 * DMA)

                def run(order, n, parity, half=None):
                    for kind, ahead in order:
                        t, p = n + ahead, (parity + ahead) % 2
                        if kind == "yln":
                            dve.wait_ge(y_in[p], count_of(t, 2 * DMA, p, half, parity))
                            moments_of(nc, dve, y_sb[:, p, :], stats[:, 0, :], moments[:, 0, :], XLN_EPS, ln_step, 5 * t, var_ready, dve_passed)
                            nc.vector.scalar_tensor_tensor(t_sb[:, :], y_sb[:, p, :], moments[:, 0, 0:1], s_rows[:, :],
                                                           ALU.subtract, ALU.mult).then_inc(ln_step, 1)
                        elif kind == "x2":
                            dve.wait_ge(ln_step, 5 * t + 3)
                            dve.wait_ge(xb_ready, t + 1)
                            dve.wait_ge(rstd_ready, 2 * t + 1)
                            nc.vector.scalar_tensor_tensor(x2[:, p, :], t_sb[:, :], rstd[:, 0:1], xb[:, p, :],
                                                           ALU.mult, ALU.add).then_inc(x2_ready, 1)
                            dve.wait_ge(x2_ready, t + 1)
                            moments_of(nc, dve, x2[:, p, :], stats[:, 1, :], moments[:, 1, :], LN_EPS, ln_step, 5 * t + 3, var_ready, dve_passed)
                        elif kind == "xln":
                            dve.wait_ge(rstd_ready, 2 * t + 2)
                            if order is both:
                                dve.wait_ge(xt_full, t)
                            nc.vector.tensor_scalar(xn[:, :], x2[:, p, :], moments[:, 1, 0:1], rstd[:, 1:2],
                                                    ALU.subtract, ALU.mult).then_inc(xn_ready, 1)
                        elif kind == "gmax":
                            dve.wait_ge(ug_full, t + 1)
                            nc.vector.tensor_reduce(negmax[:, :], ps_u[p][:, ER:MIX], AX.X, ALU.max, negate=True).then_inc(negmax_ready, 1)
                        elif kind == "gate":
                            dve.wait_ge(egate_ready, t + 1)
                            nc.vector.reciprocal(ersum[:, :], esum[:, :]).then_inc(gate_step, 1)
                            dve.wait_ge(gate_step, 2 * t + 1)
                            nc.vector.tensor_scalar(gate[:, :], egate[:, :], ersum[:, :], 1.0 / RANK, ALU.mult, ALU.mult).then_inc(gate_step, 1)
                            dve.wait_ge(gate_step, 2 * t + 2)
                            nc.vector.tensor_tensor(gt[:, :, :], ps_u[p][:, 0:ER].rearrange("p (e r) -> p e r", e=NE),
                                                    gate[:, :].unsqueeze(2).to_broadcast([P, NE, RANK]), ALU.mult).then_inc(gt_ready, 1)
                        elif kind == "xt":
                            dve.wait_ge(xt_hi, t + 1)
                            nc.vector.tensor_tensor(xnT[1][:, :, :], ps_t[0][:, :].rearrange("p (k t) -> p k t", k=KD),
                                                    xnT[0][:, :, :].bitcast(F32), ALU.subtract).then_inc(xt_lo, 1)
                        elif kind == "gT":
                            dve.wait_ge(gT_hi, t + 1)
                            nc.vector.tensor_tensor(gT[1][:, :], ps_t[1][:, 0:ER], gT[0][:, :].bitcast(F32), ALU.subtract).then_inc(gT_lo, 1)
                        elif kind == "fin":
                            dve.wait_ge(lora_full, t + 1)
                            dve.wait_ge(out_stored[p], DMA * (t // 2) + DMA if half is None else DMA * half + DMA)
                            nc.vector.tensor_tensor(x3[:, p, :], ps_b[p][:, :], x2[:, p, :], ALU.add).then_inc(x3_ready, 1)

                all_tiles(dve, run)


_INS = ["x", "ctx_1024", "mask_BxS2_bf1", "L0_attn_w_qkv", "L0_attn_w_out", "L0_xattn_ln1_s", "L0_xattn_ln1_b",
        "L0_xattn_lnc_s", "L0_xattn_lnc_b", "L0_xattn_Wq", "L0_xattn_Wkv", "L0_xattn_null_kv", "L0_xattn_Wo",
        "L0_xattn_lno_s", "L0_xattn_lno_b", "L0_ffn_weight", "L0_ffn_gate_w", "L0_ffn_lora_U", "L0_ffn_lora_V"]


def decoder_layer(nc, x, context, mask, w_qkv, w_out, ln1_s, ln1_b, lnc_s, lnc_b, w_q, w_kv, null_kv, w_o,
                  lno_s, lno_b, weight, gate_w, lora_U, lora_V, out):
    B, T, D = x.shape
    x1 = nc.dram_tensor("x1", [B, T, D], F32, kind="Internal").ap()
    q_T = nc.dram_tensor("q_T", [B, w_q.shape[1], T], F32, kind="Internal").ap()
    y = nc.dram_tensor("y", [B, T, D], F32, kind="Internal").ap()
    self_attention(nc, x, w_qkv, w_out, x1)
    cross_queries(nc, x1, ln1_s, ln1_b, w_q, q_T)
    cross_attention(nc, context, mask, lnc_s, lnc_b, w_kv, null_kv, w_o, q_T, y)
    feed_forward(nc, x1, y, lno_s, lno_b, weight, gate_w, lora_U, lora_V, out)


def kernel(**inputs):
    import numpy as _np
    import concourse.bacc as _bacc
    from concourse import mybir as _mybir
    from concourse.bass_utils import run_bass_kernel_spmd as _run

    nc = _bacc.Bacc("TRN2", target_bir_lowering=False, num_devices=1, dynamic_dma_scratch_size=1024)
    arrays, args = {}, []
    for name in _INS:
        a = _np.ascontiguousarray(inputs[name])
        arrays[f"in_{name}_dram"] = a
        args.append(nc.dram_tensor(f"in_{name}_dram", a.shape, _mybir.dt.from_np(a.dtype), kind="ExternalInput").ap())
    shape = inputs["x"].shape
    args.append(nc.dram_tensor("out_0_dram", shape, F32, kind="ExternalOutput").ap())
    decoder_layer(nc, *args)
    r = _run(nc, [arrays], core_ids=[0])
    return r.results[0]["out_0_dram"]
```

```python
from contextlib import ExitStack

import concourse.bass as bass
from concourse import mybir

F32 = mybir.dt.float32
F32R = mybir.dt.float32r
U8 = mybir.dt.uint8
ACT = mybir.ActivationFunctionType
ALU = mybir.AluOpType
AX = mybir.AxisListType

P = 128
DMA = 16
BIG = 3.0e38
LN_EPS, XLN_EPS = 1e-5, 1e-6


class Ring:

    def __init__(self, full, done, first, turn, turns, last=()):
        self.full, self.done, self.slots, self.turns = full, done, len(done), turns
        self.lists = {"first": list(first), "turn": list(turn), "last": list(last)}
        assert len(self.lists["turn"]) % self.slots == 0

    def place(self, use, when):
        rest = self.lists[when[0]].index(use) + (len(self.lists["first"]) if when[0] != "first" else 0)
        return when[1] * (len(self.lists["turn"]) // self.slots), rest

    def slot(self, use, when):
        return self.place(use, when)[1] % self.slots

    def free(self, use, when):
        turns, rest = self.place(use, when)
        return self.done[rest % self.slots], turns + rest // self.slots + 1

    def filled(self, use, when):
        rest = self.place(use, when)[1]
        return self.full, when[1] * len(self.lists["turn"]) + rest + 1

    def emptied(self, use, when):
        done, count = self.free(use, when)
        return done, count + 1

    def emptied_before(self, use, when):
        first, turn = self.lists["first"], self.lists["turn"]
        assert len(first) - first.index(use) == len(turn) - turn.index(use)
        turns, rest = when[1] * (len(turn) // self.slots), first.index(use)
        return self.done[rest % self.slots], turns + rest // self.slots + 2


def tasks(table):
    found = []
    for word in table.split():
        name = word.rstrip("0123456789.")
        found.append((name,) + tuple(int(n) for n in word[len(name):].split(".") if n))
    return found


def latest(ring, *uses):
    last = {}
    for use, when in uses:
        turns, rest = ring.place(use, when)
        slot = rest % ring.slots
        if slot not in last or rest > last[slot][0]:
            last[slot] = (rest, use)
    return [use for _, use in last.values()]


def make_constants(nc, pool, ident, minus_half, ready):
    nc.gpsimd.memset(minus_half[:, :], -0.5).then_inc(ready, 1)
    nc.gpsimd.memset(ident[:, :], 1.0).then_inc(ready, 1)
    pool.wait_ge(ready, 2)
    nc.gpsimd.affine_select(out=ident[:, :], in_=ident[:, :], compare_op=ALU.is_equal, fill=0.0, base=0,
                            pattern=[[-1, P]], channel_multiplier=1).then_inc(ready, 1)




class Place:

    def __init__(self, nc, ctx, stage):
        self.nc, self.ctx, self.stage = nc, ctx, stage

    def sb(self, name, shape, dt=F32):
        return self.ctx.enter_context(self.nc.sbuf_tensor(f"{self.stage}_{name}", shape, dt))

    def psum(self, name, shape):
        return self.ctx.enter_context(self.nc.psum_tensor(f"{self.stage}_{name}", shape, F32))

    def sem(self, name):
        return self.ctx.enter_context(self.nc.semaphore(f"{self.stage}_{name}"))


def moments_of(nc, dve, x, stats, moments, eps, step, before, var_ready, passed):
    nc.vector.bn_stats(stats, x).then_inc(step, 1)
    dve.wait_ge(step, before + 1)
    dve.sem_inc(passed, 1)
    nc.vector.bn_aggr(moments, stats).then_inc(step, 1)
    dve.wait_ge(step, before + 2)
    nc.vector.tensor_scalar(moments[:, 1:2], moments[:, 1:2], eps, None, ALU.add).then_inc(var_ready, 1)


def inverse_root(nc, pool, rstd, var, minus_half, var_ready, before, rstd_ready):
    pool.wait_ge(var_ready, before + 1)
    nc.gpsimd.tensor_tensor(rstd, var, minus_half, ALU.pow).then_inc(rstd_ready, 1)


def self_attention(nc, x, w_qkv, w_out, x1):
    B, T, D = x.shape
    HEADS, DH = 16, 32
    QT = T // 2
    KD = D // P
    GROUP = P // DH
    GROUPS = HEADS // GROUP
    SCALE = float(D) ** -0.5

    table = {
        "tensor": """
            T2 S4 S5 T3 S6 xt0 xt1 PV0 R0 T4 S7 T5 qk0 S8 T6 qk1 S9 T7 qk2 S10 qk3 T8 S11 qk4 T9 S12 qk5 qk6 T10 S13 qk7 T11
            PV1 S14 R1 T12 S15 T13 v0 T14 T15 PV2 R2 PV3 R3 S0 v1 T0 S1 out0 S2 out1 S3 T1""",
        "scalar": """
            S4 T3 inv0 xt0 xt1 S5 S6 S7 T5 qk0 qk1 S8 T7 R0 qk2 S9 qk3 S10 qk4 S11 qk5 inv1 T9 qk6 S12 qk7 S13 T11 S14 inv2
            T13 R1 S15 T15 inv3 R2 R3 S0 S1 S2 T1 S3 v0 v1""",
        "vector": """
            st0 S4 st1 inv0 ln0 T2 ln1 S5 xt0 xt1 S6 S7 T4 S8 qk0 T6 qk1 S9 S10 inv1 qk2 S11 qk3 qk4 T8 S12 qk5 R0 T10 inv2
            S13 qk6 qk7 S14 T12 S15 R1 T14 inv3 R2 S0 R3 T0 out0 S1 S2 out1 S3""",
    }
    table = {engine: tasks(t) for engine, t in table.items()}

    def ahead(task):
        kind = task[0]
        return kind in ("st", "ln", "xt", "qk", "v") or (kind == "S" and task[1] < 4) or (kind == "T" and task[1] < 2)

    first = {engine: [t for t in order if ahead(t)] for engine, order in table.items()}
    last = {engine: [t for t in order if not ahead(t)] for engine, order in table.items()}
    TURNS = B - 1

    def only(order, *kinds):
        return [u for u in order if u[0] in kinds]

    with ExitStack() as ctx:
        at = Place(nc, ctx, "sa")
        wqkv_raw = at.sb("wqkv_raw", [P, KD, 3 * D])
        wout_raw = at.sb("wout_raw", [P, KD, D])
        wqkv = [at.sb(f"wqkv_{n}", [P, KD, 3 * D], F32R) for n in ("hi", "lo")]
        wout = [at.sb(f"wout_{n}", [P, KD, D], F32R) for n in ("hi", "lo")]
        ident, minus_half = at.sb("ident", [P, P]), at.sb("minus_half", [P, 1])
        xn = at.sb("xn", [QT, 2, D])
        xres = at.sb("xres", [QT, 2, D])
        stats = at.sb("stats", [QT, 2, 6])
        moments = at.sb("moments", [QT, 2, 2])
        rstd = at.sb("rstd", [QT, 2])
        xnT = [at.sb(f"xnT_{n}", [P, KD, T], F32R) for n in ("hi", "lo")]
        qk = [at.sb(f"qk_{n}", [P, 2, GROUPS, T], F32R) for n in ("hi", "lo")]
        stack = at.sb("stack", [P, 2, GROUP, GROUPS, T], F32R)
        v_sb = at.sb("v", [QT, 2, D])
        negmax = at.sb("negmax", [QT, 4, 2])
        prob = at.sb("prob", [QT, 2, 2, T])
        sums, recip = at.sb("sums", [QT, 2, 2, GROUP]), at.sb("recip", [QT, 2, 2, GROUP])
        rsum = at.sb("rsum", [QT, 2, 2, P])
        probT = at.sb("probT", [QT, 2 * GROUP, 2, T])
        spread = at.sb("spread", [P, 2, T])
        o_sb = at.sb("o", [P, 2, T])
        oT = [at.sb(f"oT_{n}", [P, GROUPS, T], F32R) for n in ("hi", "lo")]

        ps_s = [at.psum(f"ps_s{i}", [P, 512]) for i in range(2)]
        ps_t = [at.psum(f"ps_t{i}", [P, 512]) for i in range(2)]
        ps_f = [at.psum(f"ps_f{i}", [P, 512]) for i in range(2)]
        ps_o = [at.psum(f"ps_o{i}", [P, 512]) for i in range(2)]

        def ring(name, *kinds):
            return Ring(at.sem(f"{name}_full"), [at.sem(f"{name}_done{i}") for i in range(2)],
                        only(first["tensor"], *kinds), only(table["tensor"], *kinds), TURNS, only(last["tensor"], *kinds))

        S = ring("scores", "S")
        TR = ring("transposed", "T", "xt")
        F = ring("projected", "qk", "v")
        O = ring("heads", "PV", "out")
        rings = [S, TR, F, O]

        def emptied(ring, use, when, task):
            return ring.emptied_before(use, when) if ahead(use) and not ahead(task) else ring.emptied(use, when)

        w_in, w_hi, w_lo = at.sem("w_in"), at.sem("w_hi"), at.sem("w_lo")
        ident_ready = at.sem("ident_ready")
        dve_passed, sp_passed = at.sem("dve_passed"), at.sem("sp_passed")
        x_in, xres_in, x1_stored = at.sem("x_in"), at.sem("xres_in"), at.sem("x1_stored")
        ln_step, var_ready, rstd_ready, xn_ready = at.sem("ln_step"), at.sem("var_ready"), at.sem("rstd_ready"), at.sem("xn_ready")
        xt_hi, qk_hi = at.sem("xt_hi"), at.sem("qk_hi")
        stacked = [at.sem(f"stacked{c}") for c in range(GROUP)]
        STACKED = 6 * DMA
        negmax_ready = at.sem("negmax_ready")
        recip_ready, rsum_ready, spread_ready, o_step = at.sem("recip_ready"), at.sem("rsum_ready"), at.sem("spread_ready"), at.sem("o_step")

        x_v = x.rearrange("b (q p) d -> b p q d", p=QT)
        x1_v = x1.rearrange("b (q p) d -> b p q d", p=QT)

        def batches(b):
            return bass.ds(b, 1)

        def dram(v, b):
            return v[batches(b)].rearrange("o p q d -> (o p) q d")

        with nc.Block() as block:

            @block.gpsimd
            def _(pool):
                make_constants(nc, pool, ident, minus_half, ident_ready)
                with pool.Fori(0, B) as b:
                    for i in range(2):
                        inverse_root(nc, pool, rstd[:, i:i + 1], moments[:, i, 1:2], minus_half[0:QT, :], var_ready, 2 * b + i, rstd_ready)

            @block.sync
            def _(sp):
                sp.dma_start(xn[:, :, :], dram(x_v, 0)).then_inc(x_in, DMA)
                sp.dma_start(wqkv_raw[:, :, :], w_qkv.rearrange("(k p) n -> p k n", p=P)).then_inc(w_in, DMA)
                sp.dma_start(wout_raw[:, :, :], w_out.rearrange("(k p) n -> p k n", p=P)).then_inc(w_in, DMA)
                sp.dma_start(xres[:, :, :], dram(x_v, 0)).then_inc(xres_in, DMA)

                def load(b):
                    sp.dma_start(xn[:, :, :], dram(x_v, b)).then_inc(x_in, DMA)

                def stack_heads(when):
                    for use in only(table["tensor"], "qk")[-2:]:
                        sp.wait_ge(*F.emptied(use, when))
                        sp.sem_inc(sp_passed, 1)
                    for c in range(GROUP):
                        if when[0] != "first":
                            sp.wait_ge(*S.filled(("S", HEADS - GROUP + c), when))
                            sp.sem_inc(sp_passed, 1)
                        for g, i, part in ((0, slice(0, 2), 0), (3, slice(0, 2), 1), (1, slice(0, 1), 1), (1, slice(1, 2), 0),
                                           (2, slice(0, 1), 0), (2, slice(1, 2), 1)):
                            sp.dma_start(stack[g * DH:(g + 1) * DH, i, c, :, :].bitcast(F32),
                                         qk[part][c * DH:(c + 1) * DH, i, :, :].bitcast(F32)).then_inc(stacked[c], DMA)

                def store(b, when):
                    for i in range(2):
                        sp.wait_ge(*O.emptied(("out", i), when))
                        sp.sem_inc(sp_passed, 1)
                    sp.dma_start(dram(x1_v, b), xres[:, :, :]).then_inc(x1_stored, DMA)
                    sp.wait_ge(x1_stored, DMA * b + DMA)
                    sp.sem_inc(sp_passed, 1)

                def turn(b, when):
                    stack_heads(when)
                    store(b, when)
                    sp.dma_start(xres[:, :, :], dram(x_v, b + 1)).then_inc(xres_in, DMA)

                sp.wait_ge(xt_hi, 2)
                load(1)
                stack_heads(("first", 0))
                with sp.Fori(0, TURNS - 1) as b:
                    sp.wait_ge(xt_hi, 2 * b + 4)
                    sp.sem_inc(sp_passed, 1)
                    load(b + 2)
                    turn(b, ("turn", b))
                turn(TURNS - 1, ("turn", TURNS - 1))
                store(TURNS, ("last", TURNS))

            @block.tensor
            def _(pe):
                def split_products(out, lhs, rhs, first, last_):
                    for n, (i, j) in enumerate(((0, 0), (0, 1), (1, 0))):
                        ins = nc.tensor.matmul(out, lhs[i], rhs[j], start=first and n == 0, stop=last_ and n == 2)
                    return ins

                def run(order, turn, when):
                    for task in order:
                        kind, i = task
                        b = turn + 1 if ahead(task) else turn
                        if kind == "S":
                            c, a = i % GROUP, i // GROUP
                            pe.wait_ge(stacked[c], STACKED * b + STACKED)
                            pe.wait_ge(*S.free(task, when))
                            out = ps_s[S.slot(task, when)]
                            for q in range(2):
                                ins = nc.tensor.matmul(out[0:QT, q * T:(q + 1) * T],
                                                       stack[:, 0, c, a, q * QT:(q + 1) * QT],
                                                       stack[:, 1, c, a, :], start=True, stop=True)
                            ins.then_inc(S.full, 1)
                        elif kind == "T":
                            pe.wait_ge(*emptied(S, ("S", i), when, task))
                            pe.wait_ge(*TR.free(task, when))
                            out = ps_t[TR.slot(task, when)]
                            for k in range(2):
                                for q in range(2):
                                    ins = nc.tensor.transpose(out[0:QT, k * T + q * QT:k * T + (q + 1) * QT],
                                                              prob[:, i % 2, q, k * QT:(k + 1) * QT],
                                                              ident[0:QT, 0:QT])
                            ins.then_inc(TR.full, 1)
                        elif kind == "PV":
                            group = [("T", GROUP * i + c) for c in range(GROUP)]
                            mine = latest(TR, *((t, when) for t in group if not ahead(t)))
                            for use in mine:
                                pe.wait_ge(*TR.emptied(use, when))
                            for use in [t for t in group if ahead(t)]:
                                if TR.slot(use, ("turn", 0)) not in [TR.slot(t, when) for t in mine]:
                                    pe.wait_ge(*TR.emptied_before(use, when))
                            if i == 0:
                                for use in latest(F, *((("v", t), ("turn", 0)) for t in range(2))):
                                    pe.wait_ge(*F.emptied_before(use, when))
                            pe.wait_ge(*O.free(task, when))
                            out = ps_o[O.slot(task, when)]
                            for k in range(2):
                                for c in range(GROUP):
                                    h = GROUP * i + c
                                    nc.tensor.matmul(out[c * DH:(c + 1) * DH, 0:T],
                                                     v_sb[:, k, h * DH:(h + 1) * DH],
                                                     probT[:, h % (2 * GROUP), k, :], start=k == 0, stop=k == 1)
                        elif kind == "R":
                            pe.wait_ge(rsum_ready, GROUPS * b + i + 1)
                            out = ps_o[O.slot(("PV", i), when)]
                            for q in range(2):
                                ins = nc.tensor.transpose(out[:, 256 + q * QT:256 + (q + 1) * QT], rsum[:, i % 2, q, :],
                                                          ident[0:QT, 0:QT])
                            ins.then_inc(O.full, 1)
                        elif kind == "out":
                            for use in latest(O, *((("PV", a), when) for a in range(GROUPS))):
                                pe.wait_ge(*O.emptied(use, when))
                            pe.wait_ge(*O.free(task, when))
                            out = ps_o[O.slot(task, when)]
                            for a in range(GROUPS):
                                ins = split_products(out[0:QT, :], [p[:, a, i * QT:(i + 1) * QT] for p in oT],
                                                     [w[:, a, :] for w in wout], a == 0, a == GROUPS - 1)
                            ins.then_inc(O.full, 1)
                        elif kind == "xt":
                            pe.wait_ge(xn_ready, 2 * b + i + 1)
                            pe.wait_ge(*TR.free(task, when))
                            out = ps_t[TR.slot(task, when)]
                            for k in range(KD):
                                ins = nc.tensor.transpose(out[:, k * QT:(k + 1) * QT], xn[:, i, k * P:(k + 1) * P],
                                                          ident[0:QT, 0:QT])
                            ins.then_inc(TR.full, 1)
                        elif kind == "qk":
                            if i == 0:
                                for use in latest(TR, *((("xt", t), when) for t in range(2))):
                                    pe.wait_ge(*TR.emptied(use, when))
                            pe.wait_ge(*F.free(task, when))
                            out = ps_f[F.slot(task, when)]
                            for k in range(KD):
                                ins = split_products(out[:, 0:T], [w[:, k, i * P:(i + 1) * P] for w in wqkv],
                                                     [t[:, k, :] for t in xnT], k == 0, k == KD - 1)
                            ins.then_inc(F.full, 1)
                        elif kind == "v":
                            pe.wait_ge(*F.free(task, when))
                            out = ps_f[F.slot(task, when)]
                            for k in range(KD):
                                ins = split_products(out[0:QT, :], [t[:, k, i * QT:(i + 1) * QT] for t in xnT],
                                                     [w[:, k, 2 * D:3 * D] for w in wqkv], k == 0, k == KD - 1)
                            ins.then_inc(F.full, 1)

                pe.wait_ge(ident_ready, 3)
                pe.wait_ge(w_lo, 2)
                run(first["tensor"], -1, ("first", 0))
                with pe.Fori(0, TURNS) as b:
                    run(table["tensor"], b, ("turn", b))
                run(last["tensor"], TURNS, ("last", TURNS))

            @block.scalar
            def _(act):
                def run(order, turn, when):
                    for task in order:
                        kind, i = task
                        b = turn + 1 if ahead(task) else turn
                        if kind == "S":
                            if when[0] != "first" or i >= 2:
                                act.wait_ge(*TR.filled(("T", (i - 2) % HEADS), when))
                            act.wait_ge(negmax_ready, HEADS * b + i + 1)
                            src = ps_s[S.slot(task, when)]
                            for q in range(2):
                                ins = nc.scalar.activation(prob[:, i % 2, q, :], src[0:QT, q * T:(q + 1) * T], ACT.Exp,
                                                           bias=negmax[:, i % 4, q:q + 1], scale=1.0,
                                                           accum_out=sums[:, (i // GROUP) % 2, q, i % GROUP:i % GROUP + 1])
                            ins.then_inc(S.done[S.slot(task, when)], 1)
                        elif kind == "T":
                            act.wait_ge(*TR.filled(task, when))
                            src = ps_t[TR.slot(task, when)]
                            nc.scalar.activation(probT[:, i % (2 * GROUP), :, :],
                                                 src[0:QT, 0:2 * T].rearrange("p (k t) -> p k t", k=2),
                                                 ACT.Copy).then_inc(TR.done[TR.slot(task, when)], 1)
                        elif kind == "inv":
                            act.wait_ge(recip_ready, GROUPS * b + i + 1)
                            nc.scalar.activation(rsum[:, i % 2, :, :].rearrange("p q (c d) -> p (q c) d", d=DH),
                                                 recip[:, i % 2, :, :].rearrange("p q c -> p (q c)").unsqueeze(2)
                                                 .to_broadcast([QT, 2 * GROUP, DH]), ACT.Copy).then_inc(rsum_ready, 1)
                        elif kind == "R":
                            act.wait_ge(*O.filled(("PV", i), when))
                            src = ps_o[O.slot(("PV", i), when)]
                            nc.scalar.activation(spread[:, i % 2, :], src[:, 256:256 + T], ACT.Copy).then_inc(spread_ready, 1)
                        elif kind == "xt":
                            act.wait_ge(*TR.filled(task, when))
                            src = ps_t[TR.slot(task, when)]
                            nc.scalar.activation(xnT[0][:, :, i * QT:(i + 1) * QT],
                                                 src[:, 0:KD * QT].rearrange("p (k t) -> p k t", k=KD),
                                                 ACT.Copy).then_inc(xt_hi, 1)
                        elif kind == "qk":
                            act.wait_ge(*F.filled(task, when))
                            if i == 0 and when[0] != "first":
                                for c in range(GROUP):
                                    act.wait_ge(stacked[c], STACKED * b)
                            src = ps_f[F.slot(task, when)]
                            nc.scalar.activation(qk[0][:, i // GROUPS, i % GROUPS, :], src[:, 0:T], ACT.Copy,
                                                 scale=SCALE if i < GROUPS else 1.0).then_inc(qk_hi, 1)
                        elif kind == "v":
                            act.wait_ge(*F.filled(task, when))
                            if i == 0 and when[0] != "first":
                                act.wait_ge(*O.filled(("PV", GROUPS - 1), when))
                            src = ps_f[F.slot(task, when)]
                            nc.scalar.activation(v_sb[:, i, :], src[0:QT, :], ACT.Copy).then_inc(F.done[F.slot(task, when)], 1)

                act.wait_ge(w_in, 2 * DMA)
                nc.scalar.activation(wqkv[0][:, :, :], wqkv_raw[:, :, :], ACT.Copy).then_inc(w_hi, 1)
                nc.scalar.activation(wout[0][:, :, :], wout_raw[:, :, :], ACT.Copy).then_inc(w_hi, 1)
                run(first["scalar"], -1, ("first", 0))
                with act.Fori(0, TURNS) as b:
                    run(table["scalar"], b, ("turn", b))
                run(last["scalar"], TURNS, ("last", TURNS))

            @block.vector
            def _(dve):
                def run(order, turn, when):
                    for task in order:
                        kind, i = task
                        b = turn + 1 if ahead(task) else turn
                        if kind == "S":
                            dve.wait_ge(*S.filled(task, when))
                            src = ps_s[S.slot(task, when)]
                            nc.vector.tensor_reduce(negmax[:, i % 4, :],
                                                    src[0:QT, 0:2 * T].rearrange("p (q t) -> p q t", q=2),
                                                    AX.X, ALU.max, negate=True).then_inc(negmax_ready, 1)
                        elif kind == "T":
                            dve.wait_ge(*TR.filled(task, when))
                            src = ps_t[TR.slot(task, when)]
                            nc.vector.tensor_copy(probT[:, i % (2 * GROUP), :, :],
                                                  src[0:QT, 0:2 * T].rearrange("p (k t) -> p k t", k=2)
                                                  ).then_inc(TR.done[TR.slot(task, when)], 1)
                        elif kind == "inv":
                            use = ("S", GROUP * i + GROUP - 1)
                            dve.wait_ge(*emptied(S, use, when, task))
                            nc.vector.reciprocal(recip[:, i % 2, :, :], sums[:, i % 2, :, :]).then_inc(recip_ready, 1)
                        elif kind == "R":
                            src = ps_o[O.slot(("PV", i), when)]
                            steps = 2 * (GROUPS * b + i)
                            dve.wait_ge(spread_ready, GROUPS * b + i + 1)
                            nc.vector.tensor_tensor(o_sb[:, i % 2, :], src[:, 0:T], spread[:, i % 2, :], ALU.mult).then_inc(o_step, 1)
                            dve.wait_ge(o_step, steps + 1)
                            nc.vector.tensor_copy(oT[0][:, i, :], o_sb[:, i % 2, :]).then_inc(o_step, 1)
                            dve.wait_ge(o_step, steps + 2)
                            nc.vector.tensor_tensor(oT[1][:, i, :], o_sb[:, i % 2, :], oT[0][:, i, :].bitcast(F32),
                                                    ALU.subtract).then_inc(O.done[O.slot(("PV", i), when)], 1)
                        elif kind == "out":
                            if i == 0:
                                dve.wait_ge(xres_in, DMA * b + DMA)
                            dve.wait_ge(*O.filled(task, when))
                            src = ps_o[O.slot(task, when)]
                            nc.vector.tensor_tensor(xres[:, i, :], src[0:QT, :], xres[:, i, :],
                                                    ALU.add).then_inc(O.done[O.slot(task, when)], 1)
                        elif kind == "st":
                            if i == 0:
                                dve.wait_ge(x_in, DMA * b + DMA)
                            moments_of(nc, dve, xn[:, i, :], stats[:, i, :], moments[:, i, :], LN_EPS, ln_step,
                                       4 * b + 2 * i, var_ready, dve_passed)
                        elif kind == "ln":
                            dve.wait_ge(rstd_ready, 2 * b + i + 1)
                            nc.vector.tensor_scalar(xn[:, i, :], xn[:, i, :], moments[:, i, 0:1], rstd[:, i:i + 1],
                                                    ALU.subtract, ALU.mult).then_inc(xn_ready, 1)
                        elif kind == "xt":
                            dve.wait_ge(xt_hi, 2 * b + i + 1)
                            src = ps_t[TR.slot(task, when)]
                            part = (slice(None), slice(None), slice(i * QT, (i + 1) * QT))
                            nc.vector.tensor_tensor(xnT[1][part], src[:, 0:KD * QT].rearrange("p (k t) -> p k t", k=KD),
                                                    xnT[0][part].bitcast(F32),
                                                    ALU.subtract).then_inc(TR.done[TR.slot(task, when)], 1)
                        elif kind == "qk":
                            dve.wait_ge(qk_hi, 2 * GROUPS * b + i + 1)
                            src = ps_f[F.slot(task, when)]
                            part = (slice(None), i // GROUPS, i % GROUPS, slice(None))
                            nc.vector.scalar_tensor_tensor(
                                qk[1][part], src[:, 0:T], SCALE if i < GROUPS else 1.0, qk[0][part].bitcast(F32), ALU.mult,
                                ALU.subtract).then_inc(F.done[F.slot(task, when)], 1)

                for r in rings:
                    for d in r.done:
                        dve.sem_inc(d, 1)
                run(only(first["vector"], "st", "ln"), -1, ("first", 0))
                dve.wait_ge(w_hi, 1)
                nc.vector.tensor_tensor(wqkv[1][:, :, :], wqkv_raw[:, :, :], wqkv[0][:, :, :].bitcast(F32),
                                        ALU.subtract).then_inc(w_lo, 1)
                dve.wait_ge(w_hi, 2)
                nc.vector.tensor_tensor(wout[1][:, :, :], wout_raw[:, :, :], wout[0][:, :, :].bitcast(F32),
                                        ALU.subtract).then_inc(w_lo, 1)
                run([t for t in first["vector"] if t[0] not in ("st", "ln")], -1, ("first", 0))
                with dve.Fori(0, TURNS) as b:
                    run(table["vector"], b, ("turn", b))
                run(last["vector"], TURNS, ("last", TURNS))


def cross_queries(nc, x1, ln1_s, ln1_b, w_q, q_T):
    B, T, D = x1.shape
    E = w_q.shape[1]
    KD, MD = D // P, E // P
    NB = 2
    N = NB * T
    RT = T // 2
    TILES = N // RT
    GROUPS = B // NB
    TURNS = GROUPS // 2 - 1
    HALF = MD // 2
    QSCALE = -0.25

    def project(u, following):
        order = [("q", u, m) for m in range(MD)]
        if following:
            for t in range(TILES):
                order.insert(2 * t + 2, ("xt", u + 1, t))
        return order

    first = [("xt", 0, t) for t in range(TILES)]
    turn = project(0, True) + project(1, True)
    last = project(0, True) + project(1, False)

    with ExitStack() as ctx:
        at = Place(nc, ctx, "cq")
        wq_raw = at.sb("wq_raw", [P, KD, E])
        wq = [at.sb(f"wq_{n}", [P, KD, E], F32R) for n in ("hi", "lo")]
        s_col, b_col = at.sb("s_col", [P, KD]), at.sb("b_col", [P, KD])
        qbias = at.sb("qbias", [P, MD])
        ident, minus_half = at.sb("ident", [P, P]), at.sb("minus_half", [P, 1])
        xn = at.sb("xn", [RT, 2, TILES, D])
        stats, moments = at.sb("stats", [RT, TILES, 6]), at.sb("moments", [RT, TILES, 2])
        rstd = at.sb("rstd", [RT, TILES])
        xnT = [[at.sb(f"xnT{u}_{n}", [P, KD, N], F32R) for n in ("hi", "lo")] for u in range(2)]
        q_sb = at.sb("q", [P, MD, N])
        ps_t = [at.psum(f"ps_t{i}", [P, 512]) for i in range(2)]
        ps_q = [at.psum(f"ps_q{i}", [P, 512]) for i in range(2)]
        ps_bias = at.psum("ps_bias", [P, 512])

        Q = Ring(at.sem("queries_full"), [at.sem(f"queries_done{i}") for i in range(2)], [],
                 [t for t in turn if t[0] == "q"], TURNS, [t for t in last if t[0] == "q"])
        xt_full, xt_done = at.sem("xt_full"), [at.sem(f"xt_done{i}") for i in range(2)]
        w_in, ln_in, w_hi, w_lo = at.sem("w_in"), at.sem("ln_in"), at.sem("w_hi"), at.sem("w_lo")
        bias_full, bias_ready = at.sem("bias_full"), at.sem("bias_ready")
        ident_ready = at.sem("ident_ready")
        dve_passed, sp_passed = at.sem("dve_passed"), at.sem("sp_passed")
        x_in = [at.sem(f"x_in{i}") for i in range(2)]
        ln_step, xn_ready, xt_hi = at.sem("ln_step"), at.sem("xn_ready"), at.sem("xt_hi")
        var_ready, rstd_ready, first_ready = at.sem("var_ready"), at.sem("rstd_ready"), at.sem("first_ready")
        q_stored = [at.sem(f"q_stored{i}") for i in range(2)]
        LOADED, STORED = NB * DMA, NB * DMA

        x_v = x1.rearrange("(i n) (t p) d -> i p n t d", n=NB, p=RT)
        q_v = q_T.rearrange("b (m p) t -> b p m t", p=P)

        with nc.Block() as block:

            @block.gpsimd
            def _(pool):
                make_constants(nc, pool, ident, minus_half, ident_ready)
                with pool.Fori(0, GROUPS) as i:
                    for norm in range(2):
                        for t in range(TILES):
                            inverse_root(nc, pool, rstd[:, t:t + 1], moments[:, t, 1:2], minus_half[0:RT, :], var_ready,
                                         2 * TILES * i + norm * TILES + t, rstd_ready)

            @block.sync
            def _(sp):
                def load(j, u):
                    for n in range(NB):
                        sp.dma_start(xn[:, u % 2, n * (TILES // NB):(n + 1) * (TILES // NB), :],
                                     x_v[bass.ds(2 * j + u, 1), :, n].rearrange("o p t d -> (o p) t d")).then_inc(x_in[u % 2], DMA)

                def store(j, u, when):
                    for half in range(2):
                        for m in range(half * HALF, (half + 1) * HALF)[-2:]:
                            sp.wait_ge(*Q.emptied(("q", u, m), when))
                            sp.sem_inc(sp_passed, 1)
                        for n in range(NB):
                            sp.dma_start(q_v[bass.ds(2 * NB * j + NB * u + n, 1), :, half * HALF:(half + 1) * HALF]
                                         .rearrange("o p m t -> (o p) m t"),
                                         q_sb[:, half * HALF:(half + 1) * HALF, n * T:(n + 1) * T]
                                         ).then_inc(q_stored[half], DMA)

                load(0, 0)
                load(0, 1)
                sp.dma_start(wq_raw[:, :, :], w_q.rearrange("(k p) n -> p k n", p=P)).then_inc(w_in, DMA)
                with nc.allow_non_contiguous_dma(reason="two vectors, once"):
                    sp.dma_start(s_col[:, :], ln1_s.rearrange("(k p) -> p k", p=P)).then_inc(ln_in, DMA)
                    sp.dma_start(b_col[:, :], ln1_b.rearrange("(k p) -> p k", p=P)).then_inc(ln_in, DMA)
                with sp.Fori(0, TURNS) as j:
                    for u in range(2):
                        sp.wait_ge(xt_hi, 2 * TILES * j + TILES * (u + 1))
                        sp.sem_inc(sp_passed, 1)
                        load(j, u + 2)
                        store(j, u, ("turn", j))
                for u in range(2):
                    store(TURNS, u, ("last", TURNS))
                for s in q_stored:
                    sp.wait_ge(s, STORED * GROUPS + STORED)

            @block.tensor
            def _(pe):
                def run(order, j, when):
                    for kind, u, i in order:
                        task = (kind, u, i)
                        if kind == "xt":
                            pe.wait_ge(xn_ready, 2 * TILES * j + TILES * u + i + 1)
                            pe.wait_ge(xt_done[i % 2], TILES * j + (TILES * u + i) // 2 + 1)
                            out = ps_t[i % 2]
                            for k in range(KD):
                                ins = nc.tensor.transpose(out[:, k * RT:(k + 1) * RT], xn[:, u % 2, i, k * P:(k + 1) * P], ident[0:RT, 0:RT])
                            ins.then_inc(xt_full, 1)
                        else:
                            if i == 0:
                                for t in (TILES - 2, TILES - 1):
                                    pe.wait_ge(xt_done[t % 2], TILES * j + (TILES * u + t) // 2 + 2)
                            pe.wait_ge(*Q.free(task, when))
                            out = ps_q[Q.slot(task, when)]
                            for k in range(KD):
                                for n, (w, t) in enumerate(((0, 0), (0, 1), (1, 0))):
                                    ins = nc.tensor.matmul(out[:, 0:N], wq[w][:, k, i * P:(i + 1) * P], xnT[u % 2][t][:, k, :],
                                                           start=k == 0 and n == 0, stop=k == KD - 1 and n == 2)
                            ins.then_inc(Q.full, 1)

                pe.wait_ge(ident_ready, 3)
                run(first, 0, ("first", 0))
                pe.wait_ge(w_in, DMA)
                pe.wait_ge(ln_in, 2 * DMA)
                for m in range(MD):
                    for k in range(KD):
                        ins = nc.tensor.matmul(ps_bias[:, m:m + 1], wq_raw[:, k, m * P:(m + 1) * P], b_col[:, k:k + 1],
                                               start=k == 0, stop=k == KD - 1)
                ins.then_inc(bias_full, 1)
                pe.wait_ge(w_lo, 1)
                with pe.Fori(0, TURNS) as j:
                    run(turn, j, ("turn", j))
                run(last, TURNS, ("last", TURNS))

            @block.scalar
            def _(act):
                def run(order, j, when):
                    for kind, u, i in order:
                        task = (kind, u, i)
                        if kind == "xt":
                            act.wait_ge(xt_full, 2 * TILES * j + TILES * u + i + 1)
                            nc.scalar.activation(xnT[u % 2][0][:, :, i * RT:(i + 1) * RT],
                                                 ps_t[i % 2][:, 0:KD * RT].rearrange("p (k t) -> p k t", k=KD),
                                                 ACT.Copy).then_inc(xt_hi, 1)
                        else:
                            if i % HALF == 0:
                                act.wait_ge(q_stored[i // HALF], 2 * STORED * j + STORED * u + STORED)
                            act.wait_ge(*Q.filled(task, when))
                            nc.scalar.activation(q_sb[:, i, :], ps_q[Q.slot(task, when)][:, 0:N], ACT.Identity,
                                                 bias=qbias[:, i:i + 1], scale=QSCALE).then_inc(Q.done[Q.slot(task, when)], 1)

                act.wait_ge(w_in, DMA)
                act.wait_ge(ln_in, 2 * DMA)
                for k in range(KD):
                    nc.scalar.activation(wq[0][:, k, :], wq_raw[:, k, :], ACT.Copy, scale=s_col[:, k:k + 1]).then_inc(w_hi, 1)
                for s in q_stored:
                    act.sem_inc(s, STORED)
                run(first, 0, ("first", 0))
                act.wait_ge(bias_ready, 1)
                with act.Fori(0, TURNS) as j:
                    run(turn, j, ("turn", j))
                run(last, TURNS, ("last", TURNS))

            @block.vector
            def _(dve):
                def statistics(j, u, norm):
                    before = 2 * TILES * j + TILES * u
                    if norm == 0:
                        dve.wait_ge(x_in[u % 2], LOADED * j + LOADED * (u // 2 + 1))
                    for t in range(TILES):
                        if norm:
                            dve.wait_ge(first_ready, before + t + 1)
                        moments_of(nc, dve, xn[:, u % 2, t, :], stats[:, t, :], moments[:, t, :], (LN_EPS, XLN_EPS)[norm], ln_step,
                                   4 * before + 2 * (norm * TILES + t), var_ready, dve_passed)

                def normalise(j, u, norm):
                    before = 2 * TILES * j + TILES * u
                    for t in range(TILES):
                        dve.wait_ge(rstd_ready, 2 * before + norm * TILES + t + 1)
                        nc.vector.tensor_scalar(xn[:, u % 2, t, :], xn[:, u % 2, t, :], moments[:, t, 0:1], rstd[:, t:t + 1],
                                                ALU.subtract, ALU.mult).then_inc(xn_ready if norm else first_ready, 1)

                def low_part(j, u, t):
                    dve.wait_ge(xt_hi, 2 * TILES * j + TILES * u + t + 1)
                    part = (slice(None), slice(None), slice(t * RT, (t + 1) * RT))
                    nc.vector.tensor_tensor(xnT[u % 2][1][part],
                                            ps_t[t % 2][:, 0:KD * RT].rearrange("p (k t) -> p k t", k=KD),
                                            xnT[u % 2][0][part].bitcast(F32), ALU.subtract).then_inc(xt_done[t % 2], 1)

                for s in xt_done + Q.done:
                    dve.sem_inc(s, 1)
                for u in range(2):
                    for norm in range(2):
                        statistics(0, u, norm)
                        normalise(0, u, norm)
                    if u == 0:
                        for k in range(KD):
                            dve.wait_ge(w_hi, k + 1)
                            ins = nc.vector.scalar_tensor_tensor(wq[1][:, k, :], wq_raw[:, k, :], s_col[:, k:k + 1],
                                                                 wq[0][:, k, :].bitcast(F32), ALU.mult, ALU.subtract)
                        ins.then_inc(w_lo, 1)
                        for t in range(TILES):
                            low_part(0, 0, t)
                        dve.wait_ge(bias_full, 1)
                        nc.vector.tensor_scalar(qbias[:, :], ps_bias[:, 0:MD], QSCALE, None, ALU.mult).then_inc(bias_ready, 1)
                with dve.Fori(0, TURNS) as j:
                    for u in range(2):
                        statistics(j, u + 2, 0)
                        for t in (0, 1):
                            low_part(j, u + 1, t)
                        normalise(j, u + 2, 0)
                        for t in (2, 3):
                            low_part(j, u + 1, t)
                        statistics(j, u + 2, 1)
                        normalise(j, u + 2, 1)
                for t in range(TILES):
                    low_part(TURNS, 1, t)


def cross_attention(nc, context, mask, lnc_s, lnc_b, w_kv, null_kv, w_o, q_T, y):
    B, KEYS, D = context.shape
    T = q_T.shape[2]
    E = w_o.shape[0]
    DH = null_kv.shape[1]
    HEADS = E // DH
    QT = T // 2
    KD = D // P
    ED = E // P
    STEPS, GH = 4, HEADS // 4
    GE = GH * DH
    KT = -(-(KEYS + 1) // P)
    KP = KT * P
    HALF = KP // 2
    FULL_T, TAIL = KEYS // P, KEYS % P
    KCHUNK = KEYS // 2
    TURNS = B - 1

    table = {
        "tensor": """
            T0.0.0 T0.0.1 K1.0.0 T0.0.2 S0.2.0 K1.0.1 T0.1.0 T0.1.1 S0.2.1 T0.1.2 V1.0 S0.3.0 PV0.0 S0.3.1 T0.2.0 T0.2.1 V1.1
            S1.0.0 T0.2.2 K1.1.0 T0.3.0 R0.0 S1.0.1 T0.3.1 K1.1.1 S1.1.0 T0.3.2 V1.2 S1.1.1 PV0.1
            T1.0.0 T1.0.1 R0.1 S1.2.0 T1.0.2 K2.0.0 T1.1.0 S1.2.1 K2.0.1 T1.1.1 T1.1.2 S1.3.0 V2.0 S1.3.1 PV1.0 T1.2.0 R1.0
            S2.0.0 T1.2.1 T1.2.2 V2.1 S2.0.1 T1.3.0 K2.1.0 S2.1.0 T1.3.1 K2.1.1 T1.3.2 V2.2 S2.1.1 PV1.1
            T2.0.0 S2.2.0 T2.0.1 R1.1 T2.0.2 K3.0.0 T2.1.0 S2.2.1 K3.0.1 T2.1.1 S2.3.0 T2.1.2 V3.0 PV2.0 T2.2.0 S2.3.1 T2.2.1
            V3.1 T2.2.2 S3.0.0 T2.3.0 R2.0 K3.1.0 S3.0.1 T2.3.1 T2.3.2 K3.1.1 S3.1.0 V3.2 xt0 xt1 S3.1.1 PV2.1
            T3.0.0 T3.0.1 S3.2.0 T3.0.2 xt2 xt3 S3.2.1 T3.1.0 R2.1 T3.1.1 T3.1.2 S3.3.0 xt4 xt5 PV3.0 S3.3.1 K0.0.0 R3.0
            T3.2.0 K0.0.1 T3.2.1 T3.2.2 V0.0 T3.3.0 S0.0.0 K0.1.0 T3.3.1 S0.0.1 K0.1.1 S0.1.0 T3.3.2 V0.1 PV3.1 R3.1 V0.2 out0
            S0.1.1 out1""",
        "scalar": """
            T0.0.0 T0.0.2 K1.0.0 S0.2.0 T0.1.0 T0.1.2 K1.0.1 S0.2.1 Q1.0 S0.3.0 S0.3.1 T0.2.0 Q1.1 inv0.0 inv0.1 T0.2.2 K1.1.0
            T0.3.0 S1.0.0 T0.3.2 R0.0 S1.0.1 K1.1.1
            T1.0.0 S1.1.0 S1.1.1 T1.0.2 Q2.0 K2.0.0 inv1.0 T1.1.0 S1.2.0 T1.1.2 S1.2.1 K2.0.1 T1.2.0 S1.3.0 R0.1 S1.3.1 Q2.1
            S2.0.0 T1.2.2 R1.0 T1.3.0 K2.1.0 inv1.1 T1.3.2 S2.0.1 K2.1.1
            T2.0.0 S2.1.0 S2.1.1 T2.0.2 T2.1.0 K3.0.0 S2.2.0 S2.2.1 Q3.0 T2.1.2 R1.1 K3.0.1 T2.2.0 S2.3.0 S2.3.1 inv2.0 T2.2.2
            Q3.1 T2.3.0 inv2.1 R2.0 K3.1.0 K3.1.1 S3.0.0 T2.3.2 S3.0.1 S3.1.0 xt0 xt1
            T3.0.0 S3.1.1 T3.0.2 xt2 xt3 inv3.0 T3.1.0 T3.1.2 R2.1 xt4 xt5 S3.2.0 S3.2.1 S3.3.0 K0.0.0 T3.2.0 S3.3.1 Q0.0
            K0.0.1 T3.2.2 T3.3.0 K0.1.0 S0.0.0 R3.0 inv3.1 S0.0.1 T3.3.2 K0.1.1 Q0.1 S0.1.0 R3.1 out0 S0.1.1 out1""",
        "vector": """
            T0.0.1 inv0.0 st0 S0.2.0 K1.0.0 T0.1.1 S0.2.1 S0.3.0 K1.0.1 S0.3.1 V1.0 Q1.0 T0.2.1 V1.1 inv0.1 S1.0.0 S1.0.1
            T0.3.1 K1.1.0 Q1.1 S1.1.0 K1.1.1 S1.1.1 R0.0 V1.2
            T1.0.1 ln0 S1.2.0 st1 inv1.0 S1.2.1 Q2.0 K2.0.0 S1.3.0 T1.1.1 S1.3.1 K2.0.1 T1.2.1 S2.0.0 V2.0 st2 Q2.1 S2.0.1
            V2.1 R0.1 K2.1.0 inv1.1 T1.3.1 S2.1.0 st3 S2.1.1 K2.1.1 V2.2 R1.0
            T2.0.1 S2.2.0 S2.2.1 K3.0.0 ln1 T2.1.1 st4 K3.0.1 S2.3.0 inv2.0 V3.0 S2.3.1 R1.1 Q3.0 T2.2.1 ln2 S3.0.0 inv2.1
            V3.1 ln3 S3.0.1 K3.1.0 Q3.1 R2.0 S3.1.0 T2.3.1 ln4 K3.1.1 st5 xt0 S3.1.1 xt1 V3.2
            T3.0.1 ln5 S3.2.0 inv3.0 xt2 xt3 S3.2.1 T3.1.1 S3.3.0 xt4 xt5 S3.3.1 K0.0.0 T3.2.1 Q0.0 K0.0.1 mask V0.0 S0.0.0
            R2.1 T3.3.1 S0.0.1 inv3.1 K0.1.0 R3.0 S0.1.0 V0.1 K0.1.1 R3.1 V0.2 S0.1.1 Q0.1""",
    }
    table = {engine: tasks(t) for engine, t in table.items()}

    def ahead(task):
        kind = task[0]
        return (kind in ("st", "ln", "xt", "mask") or (kind in ("K", "V", "Q") and task[1] == 0)
                or (kind == "S" and task[1] == 0 and task[2] < 2))

    first = {engine: [t for t in order if ahead(t)] for engine, order in table.items()}
    last = {engine: [t for t in order if not ahead(t)] for engine, order in table.items()}

    def only(order, *kinds):
        return [u for u in order if u[0] in kinds]

    with ExitStack() as ctx:
        at = Place(nc, ctx, "ca")
        wkv = [at.sb(f"wkv_{n}", [P, KD, 2 * E], F32R) for n in ("hi", "lo")]
        wo = [at.sb(f"wo_{n}", [P, ED, D], F32R) for n in ("hi", "lo")]
        kbias = at.sb("kbias", [P, ED])
        vbias = at.sb("vbias", [P, E])

        with ExitStack() as setup_ctx:
            su = Place(nc, setup_ctx, "cw")
            kv_raw, o_raw = su.sb("kv_raw", [P, KD, 2 * E]), su.sb("o_raw", [P, ED, D])
            s_col, b_col = su.sb("s_col", [P, KD]), su.sb("b_col", [P, KD])
            b_rows = su.sb("b_rows", [P, KD, P])
            ps_k = su.psum("ps_k", [P, 512])
            ps_v = su.psum("ps_v", [P, 2, 512])
            kv_in, o_in, ln_in = [su.sem(f"kv_in{k}") for k in range(KD)], su.sem("o_in"), su.sem("ln_in")
            hi_step, lo_step, rows_ready, bias_full = su.sem("hi_step"), su.sem("lo_step"), su.sem("rows_ready"), su.sem("bias_full")

            with nc.Block() as block:

                @block.sync
                def _(sp):
                    with nc.allow_non_contiguous_dma(reason="two vectors, once"):
                        sp.dma_start(s_col[:, :], lnc_s.rearrange("(k p) -> p k", p=P)).then_inc(ln_in, DMA)
                        sp.dma_start(b_col[:, :], lnc_b.rearrange("(k p) -> p k", p=P)).then_inc(ln_in, DMA)
                    for k in range(KD):
                        sp.dma_start(kv_raw[:, k, :], w_kv[k * P:(k + 1) * P, :]).then_inc(kv_in[k], DMA)
                    sp.dma_start(o_raw[:, :, :], w_o.rearrange("(k p) n -> p k n", p=P)).then_inc(o_in, DMA)

                @block.scalar
                def _(act):
                    act.wait_ge(ln_in, 2 * DMA)
                    for k in range(KD):
                        act.wait_ge(kv_in[k], DMA)
                        nc.scalar.activation(wkv[0][:, k, :], kv_raw[:, k, :], ACT.Copy, scale=s_col[:, k:k + 1]).then_inc(hi_step, 1)
                    act.wait_ge(o_in, DMA)
                    nc.scalar.activation(wo[0][:, :, :], o_raw[:, :, :], ACT.Copy).then_inc(hi_step, 1)

                @block.vector
                def _(dve):
                    dve.wait_ge(ln_in, 2 * DMA)
                    nc.vector.tensor_copy(b_rows[:, :, :], b_col[:, :].unsqueeze(2).to_broadcast([P, KD, P])).then_inc(rows_ready, 1)
                    for k in range(KD):
                        dve.wait_ge(hi_step, k + 1)
                        nc.vector.scalar_tensor_tensor(wkv[1][:, k, :], kv_raw[:, k, :], s_col[:, k:k + 1],
                                                       wkv[0][:, k, :].bitcast(F32), ALU.mult, ALU.subtract)
                    dve.wait_ge(hi_step, KD + 1)
                    nc.vector.tensor_tensor(wo[1][:, :, :], o_raw[:, :, :], wo[0][:, :, :].bitcast(F32), ALU.subtract)
                    dve.wait_ge(bias_full, 1)
                    nc.vector.tensor_copy(kbias[:, :], ps_k[:, 0:ED])
                    nc.vector.tensor_copy(vbias[:, :].rearrange("p (a n) -> p a n", a=2), ps_v[:, :, :]).then_inc(lo_step, 1)
                    dve.wait_ge(lo_step, 1)

                @block.tensor
                def _(pe):
                    pe.wait_ge(rows_ready, 1)
                    for k in range(KD):
                        pe.wait_ge(kv_in[k], DMA)
                    for m in range(ED):
                        for k in range(KD):
                            nc.tensor.matmul(ps_k[:, m:m + 1], kv_raw[:, k, m * P:(m + 1) * P], b_col[:, k:k + 1],
                                             start=k == 0, stop=k == KD - 1)
                    for a in range(2):
                        for k in range(KD):
                            ins = nc.tensor.matmul(ps_v[:, a, :], b_rows[:, k, :], kv_raw[:, k, E + a * 512:E + (a + 1) * 512],
                                                   start=k == 0, stop=k == KD - 1)
                    ins.then_inc(bias_full, 1)

        ident, minus_half = at.sb("ident", [P, P]), at.sb("minus_half", [P, 1])
        cn = at.sb("cn", [P, KT, D])
        stats, moments = at.sb("stats", [P, KT, 6]), at.sb("moments", [P, KT, 2])
        rstd = at.sb("rstd", [P, KT])
        cnT = [at.sb(f"cnT_{n}", [P, KD, KEYS + 2], F32R) for n in ("hi", "lo")]
        kstack = at.sb("kstack", [P, GH, KP], F32R)
        null_k = at.sb("null_k", [P, 1])
        null_part = [at.sb(f"null_{n}", [P, 1], F32R) for n in ("hi", "lo")]
        v_sb = at.sb("v", [P, 2, KT, GE])
        q_raw = at.sb("q_raw", [P, GH, T])
        q_part = [at.sb(f"q_{n}", [P, GH, T], F32R) for n in ("hi", "lo")]
        mask_u8 = at.sb("mask_u8", [QT, KEYS], U8)
        penalty = at.sb("penalty", [QT, KP])
        prob = at.sb("prob", [QT, 2, 2, KP])
        low = at.sb("low", [QT, 2, 2])
        sums, recip = at.sb("sums", [QT, 2, 2, 2]), at.sb("recip", [QT, 2, 2, 2])
        rsum = at.sb("rsum", [QT, 2, 2, P])
        probT = at.sb("probT", [P, 2, KT, T])
        spread = at.sb("spread", [P, 2, T])
        o_sb = at.sb("o", [P, 2, T])
        oT = [at.sb(f"oT_{n}", [P, ED, T], F32R) for n in ("hi", "lo")]
        y_sb = at.sb("y", [QT, 2, D])

        ps_s = at.psum("ps_s", [P, 2, 512])
        ps_t = [at.psum(f"ps_t{i}", [P, 512]) for i in range(2)]
        ps_f = [at.psum(f"ps_f{i}", [P, 512]) for i in range(2)]
        ps_o = [at.psum(f"ps_o{i}", [P, 512]) for i in range(2)]

        def ring(name, slots, *kinds):
            return Ring(at.sem(f"{name}_full"), [at.sem(f"{name}_done{i}") for i in range(slots)],
                        only(first["tensor"], *kinds), only(table["tensor"], *kinds), TURNS, only(last["tensor"], *kinds))

        S = ring("scores", 1, "S")
        TR = ring("transposed", 2, "T", "xt")
        F = ring("projected", 2, "K", "V")
        O = ring("heads", 2, "PV", "out")
        rings = [S, TR, F, O]

        ident_ready = at.sem("ident_ready")
        dve_passed, sp_passed = at.sem("dve_passed"), at.sem("sp_passed")
        ctx_in, mask_in, q_in, y_stored = at.sem("ctx_in"), at.sem("mask_in"), at.sem("q_in"), at.sem("y_stored")
        null_in, null_step, fixed_ready, nullv_in = at.sem("null_in"), at.sem("null_step"), at.sem("fixed_ready"), at.sem("nullv_in")
        var_ready, rstd_ready = at.sem("var_ready"), at.sem("rstd_ready")
        ln_step, cn_ready, xt_hi, k_hi = at.sem("ln_step"), at.sem("cn_ready"), at.sem("xt_hi"), at.sem("k_hi")
        q_hi, q_lo, mask_ready = at.sem("q_hi"), at.sem("q_lo"), at.sem("mask_ready")
        exp_done, recip_ready, rsum_ready, spread_ready, o_step = at.sem("exp_done"), at.sem("recip_ready"), at.sem("rsum_ready"), at.sem("spread_ready"), at.sem("o_step")

        ctx_full = context[:, 0:FULL_T * P, :].rearrange("b (t p) d -> b p t d", p=P)
        q_v = q_T.rearrange("b (h d) t -> b d h t", d=DH)
        y_v = y.rearrange("b (q p) d -> b p q d", p=QT)
        ROWS = [P] * FULL_T + [TAIL]

        with nc.Block() as block:

            @block.gpsimd
            def _(pool):
                make_constants(nc, pool, ident, minus_half, ident_ready)
                nc.gpsimd.memset(kstack[:, :, KEYS + 1:KP].bitcast(F32), 0.0).then_inc(fixed_ready, 1)
                for c in cnT:
                    nc.gpsimd.memset(c[:, :, KEYS:KEYS + 2].bitcast(F32), 0.0).then_inc(fixed_ready, 1)
                nc.gpsimd.memset(penalty[:, KEYS:KEYS + 1], 0.0).then_inc(fixed_ready, 1)
                nc.gpsimd.memset(penalty[:, KEYS + 1:KP], BIG).then_inc(fixed_ready, 1)
                pool.wait_ge(fixed_ready, 5)
                nc.gpsimd.memset(v_sb[96:P, :, KT - 1, :], 0.0).then_inc(fixed_ready, 1)
                with pool.Fori(0, B) as b:
                    for t, n in enumerate(ROWS):
                        inverse_root(nc, pool, rstd[0:n, t:t + 1], moments[0:n, t, 1:2], minus_half[0:n, :], var_ready, KT * b + t, rstd_ready)

            @block.sync
            def _(sp):
                def load_context(b):
                    sp.dma_start(cn[:, 0:FULL_T, :], ctx_full[bass.ds(b, 1)].rearrange("o p t d -> (o p) t d")).then_inc(ctx_in, DMA)
                    sp.dma_start(cn[0:TAIL, FULL_T, :], context[bass.ds(b, 1), FULL_T * P:KEYS, :]
                                 .rearrange("o p d -> (o p) d")).then_inc(ctx_in, DMA)

                def load_mask(b):
                    sp.dma_start(mask_u8[:, :], mask[bass.ds(b, 1), :].rearrange("o s -> (o s)").partition_broadcast(QT)).then_inc(mask_in, DMA)

                def load_queries(b, g):
                    for half in range(2):
                        sp.dma_start(q_raw[half * DH:(half + 1) * DH, :, :],
                                     q_v[bass.ds(b, 1), :, g * GH:(g + 1) * GH].rearrange("o d h t -> (o d) h t")).then_inc(q_in, DMA)

                def store(b, when):
                    sp.wait_ge(*O.emptied(("out", 0), when))
                    sp.sem_inc(sp_passed, 1)
                    sp.wait_ge(*O.emptied(("out", 1), when))
                    sp.sem_inc(sp_passed, 1)
                    sp.dma_start(y_v[bass.ds(b, 1)].rearrange("o p q d -> (o p) q d"), y_sb[:, :, :]).then_inc(y_stored, DMA)

                load_context(0)
                load_mask(0)
                load_queries(0, 0)
                for half in range(2):
                    sp.dma_start(null_k[half * DH:(half + 1) * DH, :], null_kv[0:1, :].rearrange("o (d x) -> (o d) x", x=1)).then_inc(null_in, DMA)
                sp.wait_ge(fixed_ready, 6)
                for n in range(2):
                    for h in range(GH):
                        sp.dma_start(v_sb[TAIL:TAIL + 1, n, KT - 1, h * DH:(h + 1) * DH], null_kv[1:2, :]).then_inc(nullv_in, DMA)
                sp.wait_ge(q_lo, 2)
                load_queries(0, 1)
                with sp.Fori(0, TURNS) as b:
                    when = ("turn", b)
                    sp.wait_ge(xt_hi, KT * b + KT)
                    sp.sem_inc(sp_passed, 1)
                    load_context(b + 1)
                    sp.wait_ge(mask_ready, b + 1)
                    sp.sem_inc(sp_passed, 1)
                    load_mask(b + 1)
                    for g in range(STEPS):
                        sp.wait_ge(q_lo, 2 * STEPS * b + 2 * g + 4)
                        sp.sem_inc(sp_passed, 1)
                        if g + 2 < STEPS:
                            load_queries(b, g + 2)
                        else:
                            load_queries(b + 1, g + 2 - STEPS)
                    store(b, when)
                for g in range(STEPS - 2):
                    sp.wait_ge(q_lo, 2 * STEPS * TURNS + 2 * g + 4)
                    sp.sem_inc(sp_passed, 1)
                    load_queries(TURNS, g + 2)
                store(TURNS, ("last", TURNS))
                sp.wait_ge(y_stored, DMA * B + DMA)

            @block.tensor
            def _(pe):
                def split_products(out, lhs, rhs, first_, last_):
                    for n, (i, j) in enumerate(((0, 0), (0, 1), (1, 0))):
                        ins = nc.tensor.matmul(out, lhs[i], rhs[j], start=first_ and n == 0, stop=last_ and n == 2)
                    return ins

                def run(order, turn, when):
                    for task in order:
                        kind, b = task[0], turn + 1 if ahead(task) else turn
                        if kind == "S":
                            _, g, h, q = task
                            if h % 2 == 0 and q == 0:
                                pe.wait_ge(q_lo, 2 * STEPS * b + 2 * g + h // 2 + 1)
                                for c in range(2):
                                    pe.wait_ge(*(F.emptied_before if g == 0 and h >= 2 else F.emptied)(("K", g, h // 2, c), when))
                            pe.wait_ge(*S.free(task, when))
                            for n in range(2):
                                for c in range(2):
                                    ins = nc.tensor.matmul(ps_s[0:QT, c, 0:HALF], q_part[n][:, h, q * QT:(q + 1) * QT],
                                                           kstack[:, h, c * HALF:(c + 1) * HALF], start=n == 0, stop=n == 1)
                            ins.then_inc(S.full, 1)
                        elif kind == "T":
                            _, g, h, u = task
                            if u == 0:
                                pe.wait_ge(exp_done, 2 * (HEADS * b + GH * g + h) + 2)
                            pe.wait_ge(*TR.free(task, when))
                            out = ps_t[TR.slot(task, when)]
                            for k in range(2):
                                for q in range(2):
                                    ins = nc.tensor.transpose(out[:, k * T + q * QT:k * T + (q + 1) * QT],
                                                              prob[:, h % 2, q, (2 * u + k) * P:(2 * u + k + 1) * P],
                                                              ident[0:QT, 0:QT])
                            ins.then_inc(TR.full, 1)
                        elif kind == "PV":
                            _, g, i = task
                            for use in latest(TR, *((("T", g, 2 * i + j, u), when) for j in range(2) for u in range(KT // 2))):
                                pe.wait_ge(*TR.emptied(use, when))
                            if i == 0:
                                mine = when if g else ("turn", 0)
                                for use in latest(F, *((("V", g, j), mine) for j in range(KT // 2))):
                                    pe.wait_ge(*(F.emptied if g else F.emptied_before)(use, when))
                            pe.wait_ge(*O.free(task, when))
                            out = ps_o[O.slot(task, when)]
                            for k in range(KT):
                                for j in range(2):
                                    col = (2 * i + j) * DH
                                    nc.tensor.matmul(out[j * DH:(j + 1) * DH, 0:T], v_sb[:, g % 2, k, col:col + DH],
                                                     probT[:, j, k, :], start=k == 0, stop=k == KT - 1)
                        elif kind == "R":
                            _, g, i = task
                            pe.wait_ge(rsum_ready, ED * b + 2 * g + i + 1)
                            out = ps_o[O.slot(("PV", g, i), when)]
                            for q in range(2):
                                ins = nc.tensor.transpose(out[:, 256 + q * QT:256 + (q + 1) * QT], rsum[:, i, q, :], ident[0:QT, 0:QT])
                            ins.then_inc(O.full, 1)
                        elif kind == "xt":
                            _, i = task
                            pe.wait_ge(cn_ready, KT * b + i + 1)
                            pe.wait_ge(*TR.free(task, when))
                            out = ps_t[TR.slot(task, when)]
                            n = ROWS[i]
                            for k in range(KD):
                                ins = nc.tensor.transpose(out[:, k * P:k * P + n], cn[0:n, i, k * P:(k + 1) * P], ident[0:n, 0:n])
                            ins.then_inc(TR.full, 1)
                        elif kind == "K":
                            _, g, i, c = task
                            if g == 0 and i == 0 and c == 0:
                                for use in latest(TR, *((("xt", t), when) for t in range(KT))):
                                    pe.wait_ge(*TR.emptied(use, when))
                            pe.wait_ge(*F.free(task, when))
                            out = ps_f[F.slot(task, when)]
                            col = (2 * g + i) * P
                            for k in range(KD):
                                ins = split_products(out[:, 0:KCHUNK + 1], [w[:, k, col:col + P] for w in wkv],
                                                     [t[:, k, c * KCHUNK:(c + 1) * KCHUNK + 1] for t in cnT], k == 0, k == KD - 1)
                            ins.then_inc(F.full, 1)
                        elif kind == "V":
                            _, g, j = task
                            pe.wait_ge(*F.free(task, when))
                            out = ps_f[F.slot(task, when)]
                            col = E + g * GE
                            for t in (2 * j, 2 * j + 1):
                                n = ROWS[t]
                                for k in range(KD):
                                    ins = split_products(out[0:n, (t % 2) * GE:(t % 2 + 1) * GE],
                                                         [c[:, k, t * P:t * P + n] for c in cnT],
                                                         [w[:, k, col:col + GE] for w in wkv], k == 0, k == KD - 1)
                            ins.then_inc(F.full, 1)
                        elif kind == "out":
                            _, i = task
                            for p in range(2):
                                pe.wait_ge(*O.emptied(("PV", STEPS - 1, p), when))
                            pe.wait_ge(*O.free(task, when))
                            out = ps_o[O.slot(task, when)]
                            for m in range(ED):
                                ins = split_products(out[0:QT, :], [o[:, m, i * QT:(i + 1) * QT] for o in oT],
                                                     [w[:, m, :] for w in wo], m == 0, m == ED - 1)
                            ins.then_inc(O.full, 1)

                pe.wait_ge(ident_ready, 3)
                pe.wait_ge(fixed_ready, 6)
                pe.wait_ge(null_step, 6)
                pe.wait_ge(nullv_in, 2 * GH * DMA)
                run(first["tensor"], -1, ("first", 0))
                with pe.Fori(0, TURNS) as b:
                    run(table["tensor"], b, ("turn", b))
                run(last["tensor"], TURNS, ("last", TURNS))

            @block.scalar
            def _(act):
                def run(order, turn, when):
                    for task in order:
                        kind, b = task[0], turn + 1 if ahead(task) else turn
                        if kind == "S":
                            _, g, h, q = task
                            act.wait_ge(*S.emptied(task, when))
                            nc.scalar.activation(prob[:, h % 2, q, :], prob[:, h % 2, q, :], ACT.Exp,
                                                 bias=low[:, h % 2, q:q + 1], scale=-1.0,
                                                 accum_out=sums[:, h // 2, q, h % 2:h % 2 + 1]).then_inc(exp_done, 1)
                        elif kind == "T":
                            _, g, h, u = task
                            act.wait_ge(*TR.filled(task, when))
                            src = ps_t[TR.slot(task, when)]
                            nc.scalar.activation(probT[:, h % 2, 2 * u:2 * u + 2, :],
                                                 src[:, 0:2 * T].rearrange("p (k t) -> p k t", k=2),
                                                 ACT.Copy).then_inc(TR.done[TR.slot(task, when)], 1)
                        elif kind == "inv":
                            _, g, i = task
                            act.wait_ge(recip_ready, ED * b + 2 * g + i + 1)
                            nc.scalar.activation(rsum[:, i, :, :].rearrange("p q (j d) -> p (q j) d", d=DH),
                                                 recip[:, i, :, :].rearrange("p q j -> p (q j)").unsqueeze(2)
                                                 .to_broadcast([QT, 4, DH]), ACT.Copy).then_inc(rsum_ready, 1)
                        elif kind == "R":
                            _, g, i = task
                            use = ("PV", g, i)
                            act.wait_ge(*O.filled(use, when))
                            nc.scalar.activation(spread[:, i, :], ps_o[O.slot(use, when)][:, 256:256 + T], ACT.Copy).then_inc(spread_ready, 1)
                        elif kind == "xt":
                            _, i = task
                            act.wait_ge(*TR.filled(task, when))
                            n = ROWS[i]
                            nc.scalar.activation(cnT[0][:, :, i * P:i * P + n],
                                                 ps_t[TR.slot(task, when)][:, :].rearrange("p (k t) -> p k t", k=KD)[:, :, 0:n],
                                                 ACT.Copy).then_inc(xt_hi, 1)
                        elif kind == "K":
                            _, g, i, c = task
                            act.wait_ge(*F.filled(task, when))
                            src = ps_f[F.slot(task, when)]
                            for j in range(2):
                                rows = slice(j * DH, (j + 1) * DH)
                                ins = nc.scalar.activation(kstack[rows, 2 * i + j, c * KCHUNK:(c + 1) * KCHUNK], src[rows, 0:KCHUNK],
                                                           ACT.Identity, bias=kbias[rows, 2 * g + i:2 * g + i + 1], scale=1.0)
                            ins.then_inc(k_hi, 1)
                        elif kind == "Q":
                            _, g, i = task
                            if i == 0:
                                act.wait_ge(q_in, 2 * DMA * (STEPS * b + g) + 2 * DMA)
                            nc.scalar.activation(q_part[0][:, 2 * i:2 * i + 2, :], q_raw[:, 2 * i:2 * i + 2, :], ACT.Copy).then_inc(q_hi, 1)
                        elif kind == "out":
                            _, i = task
                            if i == 0:
                                act.wait_ge(y_stored, DMA * b + DMA)
                            act.wait_ge(*O.filled(task, when))
                            nc.scalar.activation(y_sb[:, i, :], ps_o[O.slot(task, when)][0:QT, :], ACT.Copy).then_inc(O.done[O.slot(task, when)], 1)

                act.sem_inc(y_stored, DMA)
                act.wait_ge(fixed_ready, 6)
                run(first["scalar"], -1, ("first", 0))
                with act.Fori(0, TURNS) as b:
                    run(table["scalar"], b, ("turn", b))
                run(last["scalar"], TURNS, ("last", TURNS))

            @block.vector
            def _(dve):
                def run(order, turn, when):
                    for task in order:
                        kind, b = task[0], turn + 1 if ahead(task) else turn
                        if kind == "S":
                            _, g, h, q = task
                            if g == 0 and h == 0 and q == 0:
                                dve.wait_ge(mask_ready, b + 1)
                            if q == 0 and when[0] != "first":
                                dve.wait_ge(*TR.filled(("T", g, h - 2, 2) if h >= 2 else ("T", (g - 1) % STEPS, h + 2, 2), when))
                            dve.wait_ge(*S.filled(task, when))
                            dve.sem_inc(dve_passed, 1)
                            nc.vector.tensor_tensor_reduce(out=prob[:, h % 2, q, :].rearrange("p (c s) -> p c s", c=2),
                                                           in0=ps_s[0:QT, :, 0:HALF],
                                                           in1=penalty[:, :].rearrange("p (c s) -> p c s", c=2),
                                                           scale=1.0, scalar=BIG, op0=ALU.add, op1=ALU.min,
                                                           accum_out=low[:, h % 2, q:q + 1]).then_inc(S.done[0], 1)
                        elif kind == "T":
                            _, g, h, u = task
                            dve.wait_ge(*TR.filled(task, when))
                            nc.vector.tensor_copy(probT[:, h % 2, 2 * u:2 * u + 2, :],
                                                  ps_t[TR.slot(task, when)][:, 0:2 * T].rearrange("p (k t) -> p k t", k=2)
                                                  ).then_inc(TR.done[TR.slot(task, when)], 1)
                        elif kind == "inv":
                            _, g, i = task
                            dve.wait_ge(exp_done, 2 * (HEADS * b + GH * g + 2 * i + 1) + 2)
                            nc.vector.reciprocal(recip[:, i, :, :], sums[:, i, :, :]).then_inc(recip_ready, 1)
                        elif kind == "R":
                            _, g, i = task
                            use = ("PV", g, i)
                            m = 2 * g + i
                            steps = 2 * (ED * b + m)
                            dve.wait_ge(spread_ready, ED * b + m + 1)
                            nc.vector.tensor_tensor(o_sb[:, i, :], ps_o[O.slot(use, when)][:, 0:T], spread[:, i, :], ALU.mult).then_inc(o_step, 1)
                            dve.wait_ge(o_step, steps + 1)
                            nc.vector.tensor_copy(oT[0][:, m, :], o_sb[:, i, :]).then_inc(o_step, 1)
                            dve.wait_ge(o_step, steps + 2)
                            nc.vector.tensor_tensor(oT[1][:, m, :], o_sb[:, i, :], oT[0][:, m, :].bitcast(F32),
                                                    ALU.subtract).then_inc(O.done[O.slot(use, when)], 1)
                        elif kind == "st":
                            _, i = task
                            if i == 0:
                                dve.wait_ge(ctx_in, 2 * DMA * b + 2 * DMA)
                            n = ROWS[i]
                            moments_of(nc, dve, cn[0:n, i, :], stats[0:n, i, :], moments[0:n, i, :], XLN_EPS, ln_step,
                                       2 * (KT * b + i), var_ready, dve_passed)
                        elif kind == "ln":
                            _, i = task
                            n = ROWS[i]
                            dve.wait_ge(rstd_ready, KT * b + i + 1)
                            nc.vector.tensor_scalar(cn[0:n, i, :], cn[0:n, i, :], moments[0:n, i, 0:1], rstd[0:n, i:i + 1],
                                                    ALU.subtract, ALU.mult).then_inc(cn_ready, 1)
                        elif kind == "xt":
                            _, i = task
                            dve.wait_ge(xt_hi, KT * b + i + 1)
                            n = ROWS[i]
                            part = (slice(None), slice(None), slice(i * P, i * P + n))
                            nc.vector.tensor_tensor(cnT[1][part], ps_t[TR.slot(task, when)][:, :].rearrange("p (k t) -> p k t", k=KD)[:, :, 0:n],
                                                    cnT[0][part].bitcast(F32), ALU.subtract).then_inc(TR.done[TR.slot(task, when)], 1)
                        elif kind == "K":
                            _, g, i, c = task
                            dve.wait_ge(k_hi, 4 * (STEPS * b + g) + 2 * i + c + 1)
                            src = ps_f[F.slot(task, when)]
                            keys = slice(c * KCHUNK, (c + 1) * KCHUNK)
                            for j in range(2):
                                rows, other = slice(j * DH, (j + 1) * DH), slice((1 - j) * DH, (2 - j) * DH)
                                ins = nc.vector.scalar_tensor_tensor(
                                    kstack[other, 2 * i + j, keys], src[rows, 0:KCHUNK], kbias[rows, 2 * g + i:2 * g + i + 1],
                                    kstack[rows, 2 * i + j, keys].bitcast(F32), ALU.add, ALU.subtract)
                            ins.then_inc(F.done[F.slot(task, when)], 1)
                        elif kind == "V":
                            _, g, j = task
                            dve.wait_ge(*F.filled(task, when))
                            src = ps_f[F.slot(task, when)][:, :].rearrange("p (t n) -> p t n", t=2)
                            bias = vbias[:, g * GE:(g + 1) * GE]
                            if ROWS[2 * j + 1] == P:
                                ins = nc.vector.tensor_tensor(v_sb[:, g % 2, 2 * j:2 * j + 2, :], src,
                                                              bias.unsqueeze(1).to_broadcast([P, 2, GE]), ALU.add)
                            else:
                                for t in (2 * j, 2 * j + 1):
                                    n = ROWS[t]
                                    ins = nc.vector.tensor_tensor(v_sb[0:n, g % 2, t, :], src[0:n, t % 2, :], bias[0:n, :], ALU.add)
                            ins.then_inc(F.done[F.slot(task, when)], 1)
                        elif kind == "Q":
                            _, g, i = task
                            part = (slice(None), slice(2 * i, 2 * i + 2), slice(None))
                            dve.wait_ge(q_hi, 2 * (STEPS * b + g) + i + 1)
                            nc.vector.tensor_tensor(q_part[1][part], q_raw[part], q_part[0][part].bitcast(F32),
                                                    ALU.subtract).then_inc(q_lo, 1)
                        elif kind == "mask":
                            dve.wait_ge(mask_in, DMA * b + DMA)
                            nc.vector.tensor_scalar(penalty[:, 0:KEYS], mask_u8[:, :], -1.0, -BIG, ALU.add, ALU.mult).then_inc(mask_ready, 1)

                for r in rings:
                    for d in r.done:
                        dve.sem_inc(d, 1)
                dve.wait_ge(null_in, 2 * DMA)
                nc.vector.tensor_copy(null_part[0][:, :], null_k[:, :]).then_inc(null_step, 1)
                dve.wait_ge(null_step, 1)
                nc.vector.tensor_tensor(null_part[1][:, :], null_k[:, :], null_part[0][:, :].bitcast(F32), ALU.subtract).then_inc(null_step, 1)
                dve.wait_ge(null_step, 2)
                dve.wait_ge(fixed_ready, 6)
                for j in range(2):
                    for half in range(2):
                        rows = slice(half * DH, (half + 1) * DH)
                        nc.vector.tensor_copy(kstack[rows, j:GH:2, KEYS:KEYS + 1],
                                              null_part[(half + j) % 2][rows, :].bitcast(F32).unsqueeze(1).to_broadcast([DH, GH // 2, 1])
                                              ).then_inc(null_step, 1)
                run(first["vector"], -1, ("first", 0))
                with dve.Fori(0, TURNS) as b:
                    run(table["vector"], b, ("turn", b))
                run(last["vector"], TURNS, ("last", TURNS))


def feed_forward(nc, x1, y, lno_s, lno_b, weight, gate_w, lora_U, lora_V, out):
    B, T, D = x1.shape
    NE, RANK, _ = lora_U.shape
    ER = NE * RANK
    KD = D // P
    TILES = B * T // P
    MIX = ER + NE
    UNROLL, LEAD = 4, 4
    assert TILES % UNROLL == 0 and LEAD == UNROLL

    table = {
        "tensor": [("base", 0), ("gT", 0), ("ug", 1), ("lora", 0), ("xt", 2)],
        "scalar": [("gexp", 0), ("xt", 1), ("xln", 2), ("gT", 0), ("yln", 4)],
        "vector": [("xsh", 2), ("xt", 1), ("gt", 0), ("yst", 4), ("x2", 3), ("gT", 0), ("yag", 4), ("xst", 3), ("yeps", 4),
                   ("xag", 3), ("gmax", 1), ("xeps", 3), ("ysh", 4), ("fin", 0)],
        "gpsimd": [("xb", 4), ("yinv", 4), ("xinv", 3), ("ymul", 4)],
    }

    with ExitStack() as ctx:
        at = Place(nc, ctx, "ff")
        w_raw = at.sb("w_raw", [P, KD, D])
        u_raw, g_raw = at.sb("u_raw", [ER, D]), at.sb("g_raw", [NE, D])
        v_raw = at.sb("v_raw", [P, KD, NE, RANK])
        wT = [at.sb(f"wT_{n}", [P, KD, D], F32R) for n in ("hi", "lo")]
        mixT = [at.sb(f"mixT_{n}", [P, KD, MIX], F32R) for n in ("hi", "lo")]
        vT = [at.sb(f"vT_{n}", [P, D], F32R) for n in ("hi", "lo")]
        s_rows, b_rows = at.sb("s_rows", [P, D]), at.sb("b_rows", [P, D])
        ident, minus_half = at.sb("ident", [P, P]), at.sb("minus_half", [P, 1])
        y_sb, x1_sb = at.sb("y", [P, 2, D]), at.sb("x1", [P, 2, D])
        xb = at.sb("xb", [P, 2, D])
        yn, ys = at.sb("yn", [P, D]), at.sb("ys", [P, D])
        x2 = at.sb("x2", [P, 4, D])
        xn = at.sb("xn", [P, D])
        x3 = at.sb("x3", [P, 2, D])
        stats, moments = at.sb("stats", [P, 2, 6]), at.sb("moments", [P, 2, 2])
        y_rstd, y_shift = at.sb("y_rstd", [P, 1]), at.sb("y_shift", [P, 1])
        x_rstd, x_shift = at.sb("x_rstd", [P, 2]), at.sb("x_shift", [P, 2])
        xnT = [[at.sb(f"xnT{i}_{n}", [P, KD, P], F32R) for n in ("hi", "lo")] for i in range(2)]
        negmax, esum, ersum = at.sb("negmax", [P, 1]), at.sb("esum", [P, 1]), at.sb("ersum", [P, 1])
        egate = at.sb("egate", [P, NE])
        gt = at.sb("gt", [P, NE, RANK])
        gT = [at.sb(f"gT_{n}", [P, P], F32R) for n in ("hi", "lo")]

        ps_t = [at.psum(f"ps_t{i}", [P, 512]) for i in range(2)]
        ps_u = [at.psum(f"ps_u{i}", [P, 512]) for i in range(2)]
        ps_b = [at.psum(f"ps_b{i}", [P, 512]) for i in range(2)]

        w_in, rows_in = at.sem("w_in"), at.sem("rows_in")
        dve_passed, sp_passed = at.sem("dve_passed"), at.sem("sp_passed")
        ident_ready, setup_full, setup_hi, setup_lo = at.sem("ident_ready"), at.sem("setup_full"), at.sem("setup_hi"), at.sem("setup_lo")
        y_in = [at.sem(f"y_in{i}") for i in range(2)]
        y_stats, y_moments, y_var = at.sem("y_stats"), at.sem("y_moments"), at.sem("y_var")
        x_stats, x_moments, x_var = at.sem("x_stats"), at.sem("x_moments"), at.sem("x_var")
        y_rstd_ready, y_shift_ready, yn_ready, ys_ready = at.sem("y_rstd_ready"), at.sem("y_shift_ready"), at.sem("yn_ready"), at.sem("ys_ready")
        x_rstd_ready, x_shift_ready = at.sem("x_rstd_ready"), at.sem("x_shift_ready")
        xb_ready, x2_ready, xn_ready = at.sem("xb_ready"), at.sem("x2_ready"), at.sem("xn_ready")
        xt_full, xt_hi, xt_lo = at.sem("xt_full"), at.sem("xt_hi"), at.sem("xt_lo")
        ug_full, lora_full = at.sem("ug_full"), at.sem("lora_full")
        negmax_ready, egate_ready, ersum_ready, gt_ready = at.sem("negmax_ready"), at.sem("egate_ready"), at.sem("ersum_ready"), at.sem("gt_ready")
        gT_full, gT_hi, gT_lo = at.sem("gT_full"), at.sem("gT_hi"), at.sem("gT_lo")
        x3_ready = at.sem("x3_ready")
        out_stored = [at.sem(f"out_stored{i}") for i in range(2)]
        W_LOADS = 3 + KD

        rows = [v.rearrange("b t d -> (b t) d").rearrange("(i p) d -> i p d", p=P) for v in (y, x1, out)]
        setup = [("wT", k) for k in range(KD)] + [("mixT", k) for k in range(KD)] + [("vT", 0)]
        banks = ps_t + ps_u + ps_b

        def setup_parts(use):
            kind, k = use
            return {"wT": ([w[:, k, :] for w in wT], D, 1.0), "mixT": ([w[:, k, :] for w in mixT], MIX, 1.0),
                    "vT": ([w[:, :] for w in vT], D, 1.0 / RANK)}[kind]

        def all_turns(engine, order, run):
            def turns(j, whole):
                for u in range(UNROLL):
                    for task, lead in order:
                        v = u + lead
                        if whole or 0 <= UNROLL * j + v < TILES:
                            run(task, UNROLL * j + v, UNROLL // 2 * j + v // 2, v)

            LAST = TILES // UNROLL - 1
            turns(-1, False)
            with engine.Fori(0, LAST) as j:
                turns(j, True)
            turns(LAST, False)

        with nc.Block() as block:

            @block.gpsimd
            def _(pool):
                make_constants(nc, pool, ident, minus_half, ident_ready)
                pool.wait_ge(rows_in, 2 * DMA)

                def run(task, t, half, v):
                    p = v % 2
                    if task == "xb":
                        pool.wait_ge(y_in[p], 2 * DMA * half + 2 * DMA)
                        nc.gpsimd.tensor_tensor(xb[:, p, :], x1_sb[:, p, :], b_rows[:, :], ALU.add).then_inc(xb_ready, 1)
                    elif task == "yinv":
                        inverse_root(nc, pool, y_rstd[:, :], moments[:, 0, 1:2], minus_half[:, :], y_var, t, y_rstd_ready)
                    elif task == "ymul":
                        pool.wait_ge(yn_ready, t + 1)
                        nc.gpsimd.tensor_tensor(ys[:, :], yn[:, :], s_rows[:, :], ALU.mult).then_inc(ys_ready, 1)
                    elif task == "xinv":
                        inverse_root(nc, pool, x_rstd[:, p:p + 1], moments[:, 1, 1:2], minus_half[:, :], x_var, t, x_rstd_ready)

                all_turns(pool, table["gpsimd"], run)

            @block.sync
            def _(sp):
                def load(t, p):
                    for v, buf in zip(rows[0:2], (y_sb, x1_sb)):
                        sp.dma_start(buf[:, p, :], v[bass.ds(t, 1)].rearrange("o p d -> (o p) d")).then_inc(y_in[p], DMA)

                def load_next(t, p):
                    sp.wait_ge(ys_ready, t - 1)
                    sp.sem_inc(sp_passed, 1)
                    load(t, p)

                def store(t, p):
                    sp.wait_ge(x3_ready, t + 3)
                    sp.sem_inc(sp_passed, 1)
                    sp.dma_start(rows[2][bass.ds(t, 1)].rearrange("o p d -> (o p) d"), x3[:, p, :]).then_inc(out_stored[p], DMA)

                load(0, 0)
                load(1, 1)
                sp.dma_start(s_rows[:, :], lno_s.partition_broadcast(P)).then_inc(rows_in, DMA)
                sp.dma_start(b_rows[:, :], lno_b.partition_broadcast(P)).then_inc(rows_in, DMA)
                sp.dma_start(w_raw[:, :, :], weight.rearrange("(k p) n -> p k n", p=P)).then_inc(w_in, DMA)
                sp.dma_start(u_raw[:, :], lora_U.rearrange("e r n -> (e r) n")).then_inc(w_in, DMA)
                sp.dma_start(g_raw[:, :], gate_w).then_inc(w_in, DMA)
                for k in range(KD):
                    sp.dma_start(v_raw[:, k, :, :], lora_V[:, k * P:(k + 1) * P, :].rearrange("e o r -> o e r")).then_inc(w_in, DMA)
                AHEAD = LEAD + 2
                for t in range(2, AHEAD):
                    load_next(t, t % 2)
                with sp.Fori(0, (TILES - AHEAD) // 2) as j:
                    for p in range(2):
                        load_next(2 * j + p + AHEAD, p)
                        store(2 * j + p, p)
                for t in range(TILES - AHEAD, TILES):
                    store(t, t % 2)
                for s in out_stored:
                    sp.wait_ge(s, DMA * (TILES // 2) + DMA)

            @block.tensor
            def _(pe):
                def split_products(out, lhs, rhs, first, last):
                    for n, (i, j) in enumerate(((0, 0), (0, 1), (1, 0))):
                        ins = nc.tensor.matmul(out, lhs[i], rhs[j], start=first and n == 0, stop=last and n == 2)
                    return ins

                pe.wait_ge(ident_ready, 3)
                pe.wait_ge(w_in, W_LOADS * DMA)
                for j, (kind, k) in enumerate(setup):
                    bank = banks[j % len(banks)]
                    if j >= len(banks):
                        pe.wait_ge(setup_lo, j - len(banks) + 1)
                    if kind == "wT":
                        for o in range(KD):
                            ins = nc.tensor.transpose(bank[:, o * P:(o + 1) * P], w_raw[:, o, k * P:(k + 1) * P], ident[:, :])
                    elif kind == "mixT":
                        nc.tensor.transpose(bank[:, 0:ER], u_raw[:, k * P:(k + 1) * P], ident[:, :])
                        ins = nc.tensor.transpose(bank[:, ER:MIX], g_raw[:, k * P:(k + 1) * P], ident[0:NE, 0:NE])
                    else:
                        for o in range(KD):
                            ins = nc.tensor.transpose(bank[:, o * P:(o + 1) * P], v_raw[:, o, :, :].rearrange("p e r -> p (e r)"), ident[:, :])
                    ins.then_inc(setup_full, 1)
                pe.wait_ge(setup_lo, len(setup))

                def run(task, t, half, v):
                    p = v % 2
                    if task == "xt":
                        pe.wait_ge(xn_ready, t + 1)
                        for k in range(KD):
                            ins = nc.tensor.transpose(ps_t[0][:, k * P:(k + 1) * P], xn[:, k * P:(k + 1) * P], ident[:, :])
                        ins.then_inc(xt_full, 1)
                    elif task == "ug":
                        pe.wait_ge(xt_lo, t + 1)
                        for k in range(KD):
                            ins = split_products(ps_u[p][:, 0:MIX], [x[:, k, :] for x in xnT[p]], [w[:, k, :] for w in mixT],
                                                 k == 0, k == KD - 1)
                        ins.then_inc(ug_full, 1)
                    elif task == "base":
                        pe.wait_ge(x3_ready, t + 1)
                        for k in range(KD):
                            split_products(ps_b[p][:, :], [x[:, k, :] for x in xnT[p]], [w[:, k, :] for w in wT], k == 0, False)
                    elif task == "gT":
                        pe.wait_ge(gt_ready, t + 1)
                        nc.tensor.transpose(ps_t[1][:, 0:ER], gt[:, :, :].rearrange("p e r -> p (e r)"), ident[:, :]).then_inc(gT_full, 1)
                    elif task == "lora":
                        pe.wait_ge(gT_lo, t + 1)
                        split_products(ps_b[p][:, :], [g[:, :] for g in gT], [v[:, :] for v in vT], False, True).then_inc(lora_full, 1)

                all_turns(pe, table["tensor"], run)

            @block.scalar
            def _(act):
                for j, use in enumerate(setup):
                    parts, n, factor = setup_parts(use)
                    act.wait_ge(setup_full, j + 1)
                    nc.scalar.activation(parts[0], banks[j % len(banks)][:, 0:n], ACT.Copy, scale=factor).then_inc(setup_hi, 1)

                def run(task, t, half, v):
                    p = v % 2
                    if task == "gexp":
                        act.wait_ge(negmax_ready, t + 1)
                        nc.scalar.activation(egate[:, :], ps_u[p][:, ER:MIX], ACT.Exp, bias=negmax[:, :], scale=1.0,
                                             accum_out=esum[:, :]).then_inc(egate_ready, 1)
                    elif task == "xt":
                        act.wait_ge(xt_full, t + 1)
                        nc.scalar.activation(xnT[p][0][:, :, :], ps_t[0][:, :].rearrange("p (k t) -> p k t", k=KD),
                                             ACT.Copy).then_inc(xt_hi, 1)
                    elif task == "yln":
                        act.wait_ge(y_shift_ready, t + 1)
                        nc.scalar.activation(yn[:, :], y_sb[:, p, :], ACT.Identity, bias=y_shift[:, :], scale=y_rstd[:, :]).then_inc(yn_ready, 1)
                    elif task == "xln":
                        act.wait_ge(x_shift_ready, t + 1)
                        nc.scalar.activation(xn[:, :], x2[:, v % 4, :], ACT.Identity, bias=x_shift[:, p:p + 1],
                                             scale=x_rstd[:, p:p + 1]).then_inc(xn_ready, 1)
                    elif task == "gT":
                        act.wait_ge(gT_full, t + 1)
                        nc.scalar.activation(gT[0][:, :], ps_t[1][:, 0:ER], ACT.Copy).then_inc(gT_hi, 1)

                all_turns(act, table["scalar"], run)

            @block.vector
            def _(dve):
                dve.sem_inc(x3_ready, 2)
                for s in out_stored:
                    dve.sem_inc(s, DMA)
                for j, use in enumerate(setup):
                    parts, n, factor = setup_parts(use)
                    dve.wait_ge(setup_hi, j + 1)
                    nc.vector.scalar_tensor_tensor(parts[1], banks[j % len(banks)][:, 0:n], factor, parts[0].bitcast(F32),
                                                   ALU.mult, ALU.subtract).then_inc(setup_lo, 1)

                def run(task, t, half, v):
                    p = v % 2
                    if task == "yst":
                        dve.wait_ge(y_in[p], 2 * DMA * half + 2 * DMA)
                        nc.vector.bn_stats(stats[:, 0, :], y_sb[:, p, :]).then_inc(y_stats, 1)
                    elif task == "yag":
                        dve.wait_ge(y_stats, t + 1)
                        dve.sem_inc(dve_passed, 1)
                        nc.vector.bn_aggr(moments[:, 0, :], stats[:, 0, :]).then_inc(y_moments, 1)
                    elif task == "yeps":
                        dve.wait_ge(y_moments, t + 1)
                        nc.vector.tensor_scalar(moments[:, 0, 1:2], moments[:, 0, 1:2], XLN_EPS, None, ALU.add).then_inc(y_var, 1)
                    elif task == "ysh":
                        dve.wait_ge(y_rstd_ready, t + 1)
                        nc.vector.tensor_scalar(y_shift[:, :], moments[:, 0, 0:1], y_rstd[:, :], -1.0, ALU.mult, ALU.mult).then_inc(y_shift_ready, 1)
                    elif task == "x2":
                        dve.wait_ge(ys_ready, t + 1)
                        dve.wait_ge(xb_ready, t + 1)
                        nc.vector.tensor_tensor(x2[:, v % 4, :], ys[:, :], xb[:, p, :], ALU.add).then_inc(x2_ready, 1)
                    elif task == "xst":
                        dve.wait_ge(x2_ready, t + 1)
                        nc.vector.bn_stats(stats[:, 1, :], x2[:, v % 4, :]).then_inc(x_stats, 1)
                    elif task == "xag":
                        dve.wait_ge(x_stats, t + 1)
                        dve.sem_inc(dve_passed, 1)
                        nc.vector.bn_aggr(moments[:, 1, :], stats[:, 1, :]).then_inc(x_moments, 1)
                    elif task == "xeps":
                        dve.wait_ge(x_moments, t + 1)
                        nc.vector.tensor_scalar(moments[:, 1, 1:2], moments[:, 1, 1:2], LN_EPS, None, ALU.add).then_inc(x_var, 1)
                    elif task == "xsh":
                        dve.wait_ge(x_rstd_ready, t + 1)
                        nc.vector.tensor_scalar(x_shift[:, p:p + 1], moments[:, 1, 0:1], x_rstd[:, p:p + 1], -1.0,
                                                ALU.mult, ALU.mult).then_inc(x_shift_ready, 1)
                    elif task == "gmax":
                        dve.wait_ge(ug_full, t + 1)
                        nc.vector.tensor_reduce(negmax[:, :], ps_u[p][:, ER:MIX], AX.X, ALU.max, negate=True).then_inc(negmax_ready, 1)
                    elif task == "gt":
                        dve.wait_ge(egate_ready, t + 1)
                        nc.vector.reciprocal(ersum[:, :], esum[:, :]).then_inc(ersum_ready, 1)
                        dve.wait_ge(ersum_ready, t + 1)
                        nc.vector.scalar_tensor_tensor(gt[:, :, :], ps_u[p][:, 0:ER].rearrange("p (e r) -> p e r", e=NE), ersum[:, :],
                                                       egate[:, :].unsqueeze(2).to_broadcast([P, NE, RANK]),
                                                       ALU.mult, ALU.mult).then_inc(gt_ready, 1)
                    elif task == "xt":
                        dve.wait_ge(xt_hi, t + 1)
                        nc.vector.tensor_tensor(xnT[p][1][:, :, :], ps_t[0][:, :].rearrange("p (k t) -> p k t", k=KD),
                                                xnT[p][0][:, :, :].bitcast(F32), ALU.subtract).then_inc(xt_lo, 1)
                    elif task == "gT":
                        dve.wait_ge(gT_hi, t + 1)
                        nc.vector.tensor_tensor(gT[1][:, :], ps_t[1][:, 0:ER], gT[0][:, :].bitcast(F32), ALU.subtract).then_inc(gT_lo, 1)
                    elif task == "fin":
                        dve.wait_ge(lora_full, t + 1)
                        dve.wait_ge(out_stored[p], DMA * half + DMA)
                        nc.vector.tensor_tensor(x3[:, p, :], ps_b[p][:, :], x2[:, v % 4, :], ALU.add).then_inc(x3_ready, 1)

                all_turns(dve, table["vector"], run)


_INS = ["x", "ctx_1024", "mask_BxS2_bf1", "L0_attn_w_qkv", "L0_attn_w_out", "L0_xattn_ln1_s", "L0_xattn_ln1_b",
        "L0_xattn_lnc_s", "L0_xattn_lnc_b", "L0_xattn_Wq", "L0_xattn_Wkv", "L0_xattn_null_kv", "L0_xattn_Wo",
        "L0_xattn_lno_s", "L0_xattn_lno_b", "L0_ffn_weight", "L0_ffn_gate_w", "L0_ffn_lora_U", "L0_ffn_lora_V"]


def decoder_layer(nc, x, context, mask, w_qkv, w_out, ln1_s, ln1_b, lnc_s, lnc_b, w_q, w_kv, null_kv, w_o,
                  lno_s, lno_b, weight, gate_w, lora_U, lora_V, out):
    B, T, D = x.shape
    x1 = nc.dram_tensor("x1", [B, T, D], F32, kind="Internal").ap()
    q_T = nc.dram_tensor("q_T", [B, w_q.shape[1], T], F32, kind="Internal").ap()
    y = nc.dram_tensor("y", [B, T, D], F32, kind="Internal").ap()
    self_attention(nc, x, w_qkv, w_out, x1)
    cross_queries(nc, x1, ln1_s, ln1_b, w_q, q_T)
    cross_attention(nc, context, mask, lnc_s, lnc_b, w_kv, null_kv, w_o, q_T, y)
    feed_forward(nc, x1, y, lno_s, lno_b, weight, gate_w, lora_U, lora_V, out)


def kernel(**inputs):
    import numpy as _np
    import concourse.bacc as _bacc
    from concourse import mybir as _mybir
    from concourse.bass_utils import run_bass_kernel_spmd as _run

    nc = _bacc.Bacc("TRN2", target_bir_lowering=False, num_devices=1, dynamic_dma_scratch_size=1024)
    arrays, args = {}, []
    for name in _INS:
        a = _np.ascontiguousarray(inputs[name])
        arrays[f"in_{name}_dram"] = a
        args.append(nc.dram_tensor(f"in_{name}_dram", a.shape, _mybir.dt.from_np(a.dtype), kind="ExternalInput").ap())
    shape = inputs["x"].shape
    args.append(nc.dram_tensor("out_0_dram", shape, F32, kind="ExternalOutput").ap())
    decoder_layer(nc, *args)
    r = _run(nc, [arrays], core_ids=[0])
    return r.results[0]["out_0_dram"]
```

```python
from contextlib import ExitStack

import concourse.bass as bass
from concourse import mybir

F32 = mybir.dt.float32
F32R = mybir.dt.float32r
U8 = mybir.dt.uint8
ACT = mybir.ActivationFunctionType
ALU = mybir.AluOpType
AX = mybir.AxisListType

P = 128
DMA = 16
BIG = 3.0e38
LN_EPS, XLN_EPS = 1e-5, 1e-6


class Ring:

    def __init__(self, full, done, parts, turns):
        self.full, self.done, self.slots, self.parts, self.turns = full, done, len(done), parts, turns
        assert len(parts["turn"]) % self.slots == 0

    def start(self, part):
        names = list(self.parts)
        return sum(len(self.parts[n]) for n in names[:names.index(part)] if n != "turn")

    def place(self, use, when):
        return when[1] * (len(self.parts["turn"]) // self.slots), self.start(when[0]) + self.parts[when[0]].index(use)

    def free(self, use, when):
        turns, rest = self.place(use, when)
        return self.done[rest % self.slots], turns + rest // self.slots + 1

    def slot(self, use, when):
        return self.place(use, when)[1] % self.slots

    def filled(self, use, when):
        return self.full, when[1] * len(self.parts["turn"]) + self.place(use, when)[1] + 1

    def emptied(self, use, when):
        done, count = self.free(use, when)
        return done, count + 1

    def emptied_before(self, use, when):
        names = list(self.parts)
        i, loop = names.index(when[0]), names.index("turn")
        if i not in (loop, loop + 1):
            return self.emptied(use, (names[i - 1], self.turns if i > loop else 0))
        before, turn = self.parts[names[loop - 1]], self.parts["turn"]
        assert len(before) - before.index(use) == len(turn) - turn.index(use)
        return self.emptied(use, (names[loop - 1], when[1]))


def tasks(table):
    found = []
    for word in table.split():
        name = word.rstrip("0123456789.")
        found.append((name,) + tuple(int(n) for n in word[len(name):].split(".") if n))
    return found


def latest(ring, *uses):
    last = {}
    for use, when in uses:
        turns, rest = ring.place(use, when)
        slot = rest % ring.slots
        if slot not in last or rest > last[slot][0]:
            last[slot] = (rest, use)
    return [use for _, use in last.values()]


def make_constants(nc, pool, ident, minus_half, ready):
    nc.gpsimd.memset(minus_half[:, :], -0.5).then_inc(ready, 1)
    nc.gpsimd.memset(ident[:, :], 1.0).then_inc(ready, 1)
    pool.wait_ge(ready, 2)
    nc.gpsimd.affine_select(out=ident[:, :], in_=ident[:, :], compare_op=ALU.is_equal, fill=0.0, base=0,
                            pattern=[[-1, P]], channel_multiplier=1).then_inc(ready, 1)




class Place:

    def __init__(self, nc, ctx, stage):
        self.nc, self.ctx, self.stage = nc, ctx, stage

    def sb(self, name, shape, dt=F32):
        return self.ctx.enter_context(self.nc.sbuf_tensor(f"{self.stage}_{name}", shape, dt))

    def psum(self, name, shape):
        return self.ctx.enter_context(self.nc.psum_tensor(f"{self.stage}_{name}", shape, F32))

    def sem(self, name):
        return self.ctx.enter_context(self.nc.semaphore(f"{self.stage}_{name}"))


class Shared:

    def __init__(self, nc, slab, base):
        self.nc, self.base, self.size, self.used = nc, base, 4 * slab.shape[1], 0
        assert nc.sbuf_base == base + self.size

    def restart(self):
        self.used = 0

    def tensor(self, name, shape, dt=F32):
        offset = self.base + self.used
        bytes_ = 4
        for n in shape[1:]:
            bytes_ *= n
        self.used += bytes_
        assert self.used <= self.size
        return self.nc.alloc_sbuf_tensor_at(name, shape, dt, offset=offset)


def moments_of(nc, dve, x, stats, moments, eps, step, before, var_ready, passed):
    nc.vector.bn_stats(stats, x).then_inc(step, 1)
    dve.wait_ge(step, before + 1)
    dve.sem_inc(passed, 1)
    nc.vector.bn_aggr(moments, stats).then_inc(step, 1)
    dve.wait_ge(step, before + 2)
    nc.vector.tensor_scalar(moments[:, 1:2], moments[:, 1:2], eps, None, ALU.add).then_inc(var_ready, 1)


def inverse_root(nc, pool, rstd, var, minus_half, var_ready, before, rstd_ready):
    pool.wait_ge(var_ready, before + 1)
    nc.gpsimd.tensor_tensor(rstd, var, minus_half, ALU.pow).then_inc(rstd_ready, 1)


def self_attention(nc, x, w_qkv, w_out, ln1_s, ln1_b, w_q, x1, q_T, shared, load_next_weights):
    B, T, D = x.shape
    E = w_q.shape[1]
    MD = E // P
    QSCALE = -0.25
    HEADS, DH = 16, 32
    QT = T // 2
    KD = D // P
    GROUP = P // DH
    GROUPS = HEADS // GROUP
    SCALE = float(D) ** -0.5

    table = {
        "tensor": """
            T2 xt0 S4 xt1 T3 S5 qk0 S6 T4 qk1 qk2 T5 S7 T6 qk3 qk4 S8 yt0 qk5 yt1 PV0 S9 T7 R0 S10 T8 cq0 cq1 S11 T9 qk6 qk7
            T10 S12 S13 PV1 cq2 T11 cq3 S14 T12 R1 S15 T13 PV2 cq4 R2 T14 T15 cq5 PV3 R3 cq6 S0 cq7 out0 S1 S2 T0 out1 T1 S3
            v0 v1""",
        "scalar": """
            xt0 xt1 S4 qk0 S5 T3 qk1 S6 inv0 qk2 T5 qk3 qk4 yt0 S7 qk5 yt1 S8 S9 R0 T7 cq0 inv1 cq1 S10 qk6 S11 qk7 T9 S12 cq2
            T11 S13 inv2 R1 S14 S15 cq3 T13 R2 inv3 cq4 T15 cq5 R3 S0 cq6 S1 S2 cq7 v0 S3 T1 v1""",
        "vector": """
            st0 st1 ln0 yst0 ln1 T2 S4 xt0 xt1 S5 yln0 yst1 S6 qk0 inv0 T4 zst0 qk1 yln1 qk2 zst1 zln0 qk3 T6 S7 zln1 S8 qk4
            inv1 yt0 yt1 S9 qk5 S10 T8 S11 qk6 qk7 T10 S12 R0 S13 inv2 S14 S15 T12 R1 inv3 T14 R2 R3 S0 S1 out0 S2 out1 S3 T0""",
        "gpsimd": """
            st0 st1 yst0 yst1 zst0 zst1""",
    }
    table = {engine: tasks(t) for engine, t in table.items()}

    def ahead(task):
        kind = task[0]
        return kind in ("st", "ln", "xt", "qk", "v") or (kind == "S" and task[1] < 4) or (kind == "T" and task[1] < 2)

    def behind(task):
        return task[0] in ("yst", "yln", "zst", "zln", "yt", "cq")

    def batch_of(task, turn):
        return turn + 1 if ahead(task) else turn - 1 if behind(task) else turn

    parts = {engine: {"first": [t for t in order if ahead(t)],
                      "zero": [t for t in order if not behind(t)],
                      "turn": order,
                      "last": [t for t in order if not ahead(t)],
                      "final": [t for t in order if behind(t)]} for engine, order in table.items()}
    TURNS = B - 2

    def only(order, *kinds):
        return [u for u in order if u[0] in kinds]

    def first_steps(part):
        return (only(part["first"], "xt"), only(part["first"], "qk"), [t for t in part["first"] if t[0] not in ("xt", "qk")])

    def all_turns(engine, part, run, zero=None):
        run(part["first"], -1, ("first", 0))
        if zero:
            zero()
        run(part["zero"], 0, ("zero", 0))
        with engine.Fori(0, TURNS) as t:
            run(part["turn"], t + 1, ("turn", t))
        run(part["last"], B - 1, ("last", TURNS))
        run(part["final"], B, ("final", TURNS))

    with ExitStack() as ctx:
        at = Place(nc, ctx, "sa")
        STAGED = 4
        staged = at.sb("staged", [P, STAGED, 2 * D])
        s_col, b_col = at.sb("s_col", [P, KD]), at.sb("b_col", [P, KD])
        qbias = at.sb("qbias", [P, MD])
        wqkv = [shared.tensor(f"sa_wqkv_{n}", [P, KD, 3 * D], F32R) for n in ("hi", "lo")]
        wout = [at.sb(f"wout_{n}", [P, KD, D], F32R) for n in ("hi", "lo")]
        wq = [at.sb(f"wq_{n}", [P, KD, E], F32R) for n in ("hi", "lo")]
        ident, minus_half = at.sb("ident", [P, P]), at.sb("minus_half", [P, 1])
        xn = at.sb("xn", [QT, 2, D])
        xres = at.sb("xres", [QT, 2, D])
        stats = at.sb("stats", [QT, 2, 6])
        moments = at.sb("moments", [QT, 2, 2])
        rstd = at.sb("rstd", [QT, 2])
        xnT = [at.sb(f"xnT_{n}", [P, KD, T], F32R) for n in ("hi", "lo")]
        qk = [at.sb(f"qk_{n}", [P, 2, GROUPS, T], F32R) for n in ("hi", "lo")]
        stack = at.sb("stack", [P, 2, GROUP, GROUPS, T], F32R)
        v_sb = at.sb("v", [QT, 2, D])
        negmax = at.sb("negmax", [QT, 4, 2])
        prob = at.sb("prob", [QT, 2, 2, T])
        sums, recip = at.sb("sums", [QT, 2, 2, GROUP]), at.sb("recip", [QT, 2, 2, GROUP])
        rsum = at.sb("rsum", [QT, 2, 2, P])
        probT = at.sb("probT", [QT, 2 * GROUP, 2, T])
        spread = at.sb("spread", [P, 2, T])
        o_sb = at.sb("o", [P, 2, T])
        oT = [at.sb(f"oT_{n}", [P, GROUPS, T], F32R) for n in ("hi", "lo")]
        yn = at.sb("yn", [QT, 2, D])
        y_stats, y_moments, y_rstd = at.sb("y_stats", [QT, 2, 6]), at.sb("y_moments", [QT, 2, 2]), at.sb("y_rstd", [QT, 2])
        ynT = [at.sb(f"ynT_{n}", [P, KD, T], F32R) for n in ("hi", "lo")]
        q_sb = at.sb("q", [P, MD, T])

        ps_s = [at.psum(f"ps_s{i}", [P, 512]) for i in range(2)]
        ps_t = [at.psum(f"ps_t{i}", [P, 512]) for i in range(2)]
        ps_f = [at.psum(f"ps_f{i}", [P, 512]) for i in range(2)]
        ps_o = [at.psum(f"ps_o{i}", [P, 512]) for i in range(2)]

        def ring(name, *kinds):
            return Ring(at.sem(f"{name}_full"), [at.sem(f"{name}_done{i}") for i in range(2)],
                        {name: only(order, *kinds) for name, order in parts["tensor"].items()}, TURNS)

        S = ring("scores", "S")
        TR = ring("transposed", "T", "xt", "yt")
        F = ring("projected", "qk", "v", "cq")
        O = ring("heads", "PV", "out")
        rings = [S, TR, F, O]

        def emptied(ring, use, when, task):
            return ring.emptied_before(use, when) if ahead(use) and not ahead(task) else ring.emptied(use, when)

        w_in = [at.sem(f"w_in{i}") for i in range(STAGED)]
        w_hi, w_lo, ln_in = at.sem("w_hi"), at.sem("w_lo"), at.sem("ln_in")
        bias_full, bias_step, bias_ready = at.sem("bias_full"), at.sem("bias_step"), at.sem("bias_ready")
        ident_ready = at.sem("ident_ready")
        y_step, y_var, y_rstd_ready, y_ready = at.sem("y_step"), at.sem("y_var"), at.sem("y_rstd_ready"), at.sem("y_ready")
        z_step, z_var, z_rstd_ready, z_ready = at.sem("z_step"), at.sem("z_var"), at.sem("z_rstd_ready"), at.sem("z_ready")
        yt_hi, q_stored = at.sem("yt_hi"), at.sem("q_stored")
        dve_passed, sp_passed = at.sem("dve_passed"), at.sem("sp_passed")
        x_in, xres_in, x1_stored = at.sem("x_in"), at.sem("xres_in"), at.sem("x1_stored")
        ln_step, var_ready, rstd_ready, xn_ready = at.sem("ln_step"), at.sem("var_ready"), at.sem("rstd_ready"), at.sem("xn_ready")
        xt_hi, qk_hi = at.sem("xt_hi"), at.sem("qk_hi")
        stacked = [at.sem(f"stacked{c}") for c in range(GROUP)]
        STACKED = 6 * DMA
        negmax_ready = at.sem("negmax_ready")
        recip_ready, rsum_ready, spread_ready, o_step = at.sem("recip_ready"), at.sem("rsum_ready"), at.sem("spread_ready"), at.sem("o_step")

        x_v = x.rearrange("b (q p) d -> b p q d", p=QT)
        x1_v = x1.rearrange("b (q p) d -> b p q d", p=QT)
        q_v = q_T.rearrange("b (m p) t -> b p m t", p=P)

        qkv_v, q_w_v, out_v = [w.rearrange("(k p) n -> p k n", p=P) for w in (w_qkv, w_q, w_out)]
        chunks = ([(qkv_v[:, k, 0:2 * D], [w[:, k, 0:2 * D] for w in wqkv], None) for k in range(KD)]
                  + [(qkv_v[:, k:k + 2, 2 * D:3 * D], [w[:, k:k + 2, 2 * D:3 * D] for w in wqkv], None) for k in (0, 2)]
                  + [(q_w_v[:, k, :], [w[:, k, :] for w in wq], k) for k in range(KD)]
                  + [(out_v[:, k:k + 2, :], [w[:, k:k + 2, :] for w in wout], None) for k in (0, 2)])
        EARLY, QUERY = KD + 2, range(KD + 2, 2 * KD + 2)

        def chunk_in(engine, n):
            engine.wait_ge(w_in[n % STAGED], DMA * (n // STAGED) + DMA)
            dst = staged[:, n % STAGED, :]
            return dst if len(chunks[n][0].shape) == 2 else dst.rearrange("p (k n) -> p k n", k=2)

        def batches(b):
            return bass.ds(b, 1)

        def dram(v, b):
            return v[batches(b)].rearrange("o p q d -> (o p) q d")

        with nc.Block() as block:

            @block.gpsimd
            def _(pool):
                make_constants(nc, pool, ident, minus_half, ident_ready)

                def run(order, turn, when):
                    for task in order:
                        kind, i = task
                        n = 2 * batch_of(task, turn) + i
                        if kind == "st":
                            inverse_root(nc, pool, rstd[:, i:i + 1], moments[:, i, 1:2], minus_half[0:QT, :], var_ready, n, rstd_ready)
                        else:
                            var, ready = (y_var, y_rstd_ready) if kind == "yst" else (z_var, z_rstd_ready)
                            inverse_root(nc, pool, y_rstd[:, i:i + 1], y_moments[:, i, 1:2], minus_half[0:QT, :], var, n, ready)

                all_turns(pool, parts["gpsimd"], run)

            @block.sync
            def _(sp):
                def load_chunk(n):
                    if n >= STAGED:
                        sp.wait_ge(w_lo, n - STAGED + 1)
                        if n - STAGED in QUERY:
                            sp.wait_ge(bias_full, n - STAGED - QUERY[0] + 1)
                    source = chunks[n][0]
                    dst = staged[:, n % STAGED, :]
                    sp.dma_start(dst if len(source.shape) == 2 else dst.rearrange("p (k n) -> p k n", k=2), source
                                 ).then_inc(w_in[n % STAGED], DMA)

                sp.dma_start(xn[:, :, :], dram(x_v, 0)).then_inc(x_in, DMA)
                for n in range(STAGED):
                    load_chunk(n)
                with nc.allow_non_contiguous_dma(reason="two vectors, once"):
                    sp.dma_start(s_col[:, :], ln1_s.rearrange("(k p) -> p k", p=P)).then_inc(ln_in, DMA)
                    sp.dma_start(b_col[:, :], ln1_b.rearrange("(k p) -> p k", p=P)).then_inc(ln_in, DMA)
                sp.dma_start(xres[:, :, :], dram(x_v, 0)).then_inc(xres_in, DMA)
                for n in range(STAGED, EARLY + STAGED):
                    load_chunk(n)

                def load(b):
                    sp.dma_start(xn[:, :, :], dram(x_v, b)).then_inc(x_in, DMA)

                def stack_heads(when):
                    for use in only(table["tensor"], "qk")[-2:]:
                        sp.wait_ge(*F.emptied(use, when))
                        sp.sem_inc(sp_passed, 1)
                    for c in range(GROUP):
                        if when[0] != "first":
                            sp.wait_ge(*S.filled(("S", HEADS - GROUP + c), when))
                            sp.sem_inc(sp_passed, 1)
                        for g, i, part in ((0, slice(0, 2), 0), (3, slice(0, 2), 1), (1, slice(0, 1), 1), (1, slice(1, 2), 0),
                                           (2, slice(0, 1), 0), (2, slice(1, 2), 1)):
                            sp.dma_start(stack[g * DH:(g + 1) * DH, i, c, :, :].bitcast(F32),
                                         qk[part][c * DH:(c + 1) * DH, i, :, :].bitcast(F32)).then_inc(stacked[c], DMA)

                def store(b, when):
                    for i in range(2):
                        sp.wait_ge(*O.emptied(("out", i), when))
                        sp.sem_inc(sp_passed, 1)
                    sp.dma_start(dram(x1_v, b), xres[:, :, :]).then_inc(x1_stored, DMA)

                def store_queries(b, when):
                    for use in latest(F, *((("cq", m), when) for m in range(MD))):
                        sp.wait_ge(*F.emptied(use, when))
                        sp.sem_inc(sp_passed, 1)
                    sp.dma_start(q_v[batches(b)].rearrange("o p m t -> (o p) m t"), q_sb[:, :, :]).then_inc(q_stored, DMA)

                def load_residual(b):
                    sp.wait_ge(y_ready, 2 * b)
                    sp.sem_inc(sp_passed, 1)
                    sp.wait_ge(x1_stored, DMA * b)
                    sp.sem_inc(sp_passed, 1)
                    sp.dma_start(xres[:, :, :], dram(x_v, b)).then_inc(xres_in, DMA)

                def next_input(b):
                    sp.wait_ge(xt_hi, 2 * b + 4)
                    sp.sem_inc(sp_passed, 1)
                    load(b + 2)

                def turn(b, when):
                    load_residual(b)
                    stack_heads(when)
                    store_queries(b - 1, when)
                    store(b, when)

                sp.wait_ge(xt_hi, 2)
                load(1)
                stack_heads(("first", 0))
                for n in range(EARLY + STAGED, len(chunks)):
                    load_chunk(n)
                next_input(0)
                stack_heads(("zero", 0))
                store(0, ("zero", 0))
                with sp.Fori(0, TURNS - 1) as t:
                    next_input(t + 1)
                    turn(t + 1, ("turn", t))
                turn(TURNS, ("turn", TURNS - 1))
                load_residual(B - 1)
                sp.wait_ge(*F.filled(only(table["tensor"], "qk", "v")[-1], ("turn", TURNS - 1)))
                load_next_weights(sp)
                store_queries(B - 2, ("last", TURNS))
                store(B - 1, ("last", TURNS))
                store_queries(B - 1, ("final", TURNS))
                sp.wait_ge(x1_stored, DMA * B)
                sp.wait_ge(q_stored, DMA * B + DMA)

            @block.tensor
            def _(pe):
                def split_products(out, lhs, rhs, first, last_):
                    for n, (i, j) in enumerate(((0, 0), (0, 1), (1, 0))):
                        ins = nc.tensor.matmul(out, lhs[i], rhs[j], start=first and n == 0, stop=last_ and n == 2)
                    return ins

                def run(order, turn, when):
                    for task in order:
                        kind, i = task
                        b = batch_of(task, turn)
                        if kind == "S":
                            c, a = i % GROUP, i // GROUP
                            pe.wait_ge(stacked[c], STACKED * b + STACKED)
                            pe.wait_ge(*S.free(task, when))
                            out = ps_s[S.slot(task, when)]
                            for q in range(2):
                                ins = nc.tensor.matmul(out[0:QT, q * T:(q + 1) * T],
                                                       stack[:, 0, c, a, q * QT:(q + 1) * QT],
                                                       stack[:, 1, c, a, :], start=True, stop=True)
                            ins.then_inc(S.full, 1)
                        elif kind == "T":
                            pe.wait_ge(*emptied(S, ("S", i), when, task))
                            pe.wait_ge(*TR.free(task, when))
                            out = ps_t[TR.slot(task, when)]
                            for k in range(2):
                                for q in range(2):
                                    ins = nc.tensor.transpose(out[0:QT, k * T + q * QT:k * T + (q + 1) * QT],
                                                              prob[:, i % 2, q, k * QT:(k + 1) * QT],
                                                              ident[0:QT, 0:QT])
                            ins.then_inc(TR.full, 1)
                        elif kind == "PV":
                            group = [("T", GROUP * i + c) for c in range(GROUP)]
                            waits = [TR.emptied(use, when) for use in latest(TR, *((t, when) for t in group if not ahead(t)))]
                            for use in group:
                                before = TR.emptied_before(use, when) if ahead(use) else waits[0]
                                if all(before[0] is not done for done, _ in waits):
                                    waits.append(before)
                            for done, count in waits:
                                pe.wait_ge(done, count)
                            if i == 0:
                                for use in latest(F, *((("v", t), ("turn", 0)) for t in range(2))):
                                    pe.wait_ge(*F.emptied_before(use, when))
                            pe.wait_ge(*O.free(task, when))
                            out = ps_o[O.slot(task, when)]
                            for k in range(2):
                                for c in range(GROUP):
                                    h = GROUP * i + c
                                    nc.tensor.matmul(out[c * DH:(c + 1) * DH, 0:T],
                                                     v_sb[:, k, h * DH:(h + 1) * DH],
                                                     probT[:, h % (2 * GROUP), k, :], start=k == 0, stop=k == 1)
                        elif kind == "R":
                            pe.wait_ge(rsum_ready, GROUPS * b + i + 1)
                            out = ps_o[O.slot(("PV", i), when)]
                            for q in range(2):
                                ins = nc.tensor.transpose(out[:, 256 + q * QT:256 + (q + 1) * QT], rsum[:, i % 2, q, :],
                                                          ident[0:QT, 0:QT])
                            ins.then_inc(O.full, 1)
                        elif kind == "out":
                            for use in latest(O, *((("PV", a), when) for a in range(GROUPS))):
                                pe.wait_ge(*O.emptied(use, when))
                            pe.wait_ge(*O.free(task, when))
                            out = ps_o[O.slot(task, when)]
                            for a in range(GROUPS):
                                ins = split_products(out[0:QT, :], [p[:, a, i * QT:(i + 1) * QT] for p in oT],
                                                     [w[:, a, :] for w in wout], a == 0, a == GROUPS - 1)
                            ins.then_inc(O.full, 1)
                        elif kind == "xt":
                            pe.wait_ge(xn_ready, 2 * b + i + 1)
                            pe.wait_ge(*TR.free(task, when))
                            out = ps_t[TR.slot(task, when)]
                            for k in range(KD):
                                ins = nc.tensor.transpose(out[:, k * QT:(k + 1) * QT], xn[:, i, k * P:(k + 1) * P],
                                                          ident[0:QT, 0:QT])
                            ins.then_inc(TR.full, 1)
                        elif kind == "qk":
                            if i == 0:
                                for use in latest(TR, *((("xt", t), when) for t in range(2))):
                                    pe.wait_ge(*TR.emptied(use, when))
                            pe.wait_ge(*F.free(task, when))
                            out = ps_f[F.slot(task, when)]
                            for k in range(KD):
                                ins = split_products(out[:, 0:T], [w[:, k, i * P:(i + 1) * P] for w in wqkv],
                                                     [t[:, k, :] for t in xnT], k == 0, k == KD - 1)
                            ins.then_inc(F.full, 1)
                        elif kind == "yt":
                            pe.wait_ge(z_ready, 2 * b + i + 1)
                            pe.wait_ge(*TR.free(task, when))
                            out = ps_t[TR.slot(task, when)]
                            for k in range(KD):
                                ins = nc.tensor.transpose(out[:, k * QT:(k + 1) * QT], yn[:, i, k * P:(k + 1) * P],
                                                          ident[0:QT, 0:QT])
                            ins.then_inc(TR.full, 1)
                        elif kind == "cq":
                            if i == 0:
                                for use in latest(TR, *((("yt", t), when) for t in range(2))):
                                    pe.wait_ge(*TR.emptied(use, when))
                            pe.wait_ge(*F.free(task, when))
                            out = ps_f[F.slot(task, when)]
                            for k in range(KD):
                                ins = split_products(out[:, 0:T], [w[:, k, i * P:(i + 1) * P] for w in wq],
                                                     [t[:, k, :] for t in ynT], k == 0, k == KD - 1)
                            ins.then_inc(F.full, 1)
                        elif kind == "v":
                            pe.wait_ge(*F.free(task, when))
                            out = ps_f[F.slot(task, when)]
                            for k in range(KD):
                                ins = split_products(out[0:QT, :], [t[:, k, i * QT:(i + 1) * QT] for t in xnT],
                                                     [w[:, k, 2 * D:3 * D] for w in wqkv], k == 0, k == KD - 1)
                            ins.then_inc(F.full, 1)

                def query_bias():
                    pe.wait_ge(ln_in, 2 * DMA)
                    for k, n in enumerate(QUERY):
                        raw = chunk_in(pe, n)
                        for m in range(MD):
                            ins = nc.tensor.matmul(ps_o[0][:, m * KD + k:m * KD + k + 1], raw[:, m * P:(m + 1) * P], b_col[:, k:k + 1],
                                                   start=True, stop=True)
                        ins.then_inc(bias_full, 1)

                def later_weights():
                    pe.wait_ge(bias_ready, 1)
                    pe.wait_ge(w_lo, len(chunks))

                pe.wait_ge(ident_ready, 3)
                transposes, to_qk, others = first_steps(parts["tensor"])
                run(transposes, -1, ("first", 0))
                pe.wait_ge(w_lo, KD)
                run(to_qk, -1, ("first", 0))
                query_bias()
                pe.wait_ge(w_lo, EARLY)
                all_turns(pe, parts["tensor"] | {"first": others}, run, later_weights)

            @block.scalar
            def _(act):
                def run(order, turn, when):
                    for task in order:
                        kind, i = task
                        b = batch_of(task, turn)
                        if kind == "S":
                            if when[0] != "first" or i >= 2:
                                act.wait_ge(*TR.filled(("T", (i - 2) % HEADS), when))
                            act.wait_ge(negmax_ready, HEADS * b + i + 1)
                            src = ps_s[S.slot(task, when)]
                            for q in range(2):
                                ins = nc.scalar.activation(prob[:, i % 2, q, :], src[0:QT, q * T:(q + 1) * T], ACT.Exp,
                                                           bias=negmax[:, i % 4, q:q + 1], scale=1.0,
                                                           accum_out=sums[:, (i // GROUP) % 2, q, i % GROUP:i % GROUP + 1])
                            ins.then_inc(S.done[S.slot(task, when)], 1)
                        elif kind == "T":
                            act.wait_ge(*TR.filled(task, when))
                            src = ps_t[TR.slot(task, when)]
                            nc.scalar.activation(probT[:, i % (2 * GROUP), :, :],
                                                 src[0:QT, 0:2 * T].rearrange("p (k t) -> p k t", k=2),
                                                 ACT.Copy).then_inc(TR.done[TR.slot(task, when)], 1)
                        elif kind == "inv":
                            act.wait_ge(recip_ready, GROUPS * b + i + 1)
                            nc.scalar.activation(rsum[:, i % 2, :, :].rearrange("p q (c d) -> p (q c) d", d=DH),
                                                 recip[:, i % 2, :, :].rearrange("p q c -> p (q c)").unsqueeze(2)
                                                 .to_broadcast([QT, 2 * GROUP, DH]), ACT.Copy).then_inc(rsum_ready, 1)
                        elif kind == "R":
                            act.wait_ge(*O.filled(("PV", i), when))
                            src = ps_o[O.slot(("PV", i), when)]
                            nc.scalar.activation(spread[:, i % 2, :], src[:, 256:256 + T], ACT.Copy).then_inc(spread_ready, 1)
                        elif kind == "xt":
                            act.wait_ge(*TR.filled(task, when))
                            src = ps_t[TR.slot(task, when)]
                            nc.scalar.activation(xnT[0][:, :, i * QT:(i + 1) * QT],
                                                 src[:, 0:KD * QT].rearrange("p (k t) -> p k t", k=KD),
                                                 ACT.Copy).then_inc(xt_hi, 1)
                        elif kind == "qk":
                            act.wait_ge(*F.filled(task, when))
                            if i == 0 and when[0] != "first":
                                for c in range(GROUP):
                                    act.wait_ge(stacked[c], STACKED * b)
                            src = ps_f[F.slot(task, when)]
                            nc.scalar.activation(qk[0][:, i // GROUPS, i % GROUPS, :], src[:, 0:T], ACT.Copy,
                                                 scale=SCALE if i < GROUPS else 1.0).then_inc(qk_hi, 1)
                        elif kind == "yt":
                            act.wait_ge(*TR.filled(task, when))
                            src = ps_t[TR.slot(task, when)]
                            nc.scalar.activation(ynT[0][:, :, i * QT:(i + 1) * QT],
                                                 src[:, 0:KD * QT].rearrange("p (k t) -> p k t", k=KD),
                                                 ACT.Copy).then_inc(yt_hi, 1)
                        elif kind == "cq":
                            if i == 0:
                                act.wait_ge(q_stored, DMA * b + DMA)
                            act.wait_ge(*F.filled(task, when))
                            nc.scalar.activation(q_sb[:, i, :], ps_f[F.slot(task, when)][:, 0:T], ACT.Identity, bias=qbias[:, i:i + 1],
                                                 scale=QSCALE).then_inc(F.done[F.slot(task, when)], 1)
                        elif kind == "v":
                            act.wait_ge(*F.filled(task, when))
                            if i == 0 and when[0] != "first":
                                act.wait_ge(*O.filled(("PV", GROUPS - 1), when))
                            src = ps_f[F.slot(task, when)]
                            nc.scalar.activation(v_sb[:, i, :], src[0:QT, :], ACT.Copy).then_inc(F.done[F.slot(task, when)], 1)

                def high_parts(numbers):
                    for n in numbers:
                        _, split_to, k = chunks[n]
                        raw = chunk_in(act, n)
                        if n == QUERY[0]:
                            act.wait_ge(ln_in, 2 * DMA)
                        nc.scalar.activation(split_to[0], raw, ACT.Copy, scale=1.0 if k is None else s_col[:, k:k + 1]).then_inc(w_hi, 1)

                def later_weights():
                    high_parts(range(EARLY + KD, len(chunks)))
                    act.wait_ge(bias_ready, 1)

                act.sem_inc(q_stored, DMA)
                transposes, to_qk, others = first_steps(parts["scalar"])
                high_parts(range(KD))
                run(transposes, -1, ("first", 0))
                high_parts(range(KD, EARLY))
                run(to_qk, -1, ("first", 0))
                high_parts(QUERY)
                all_turns(act, parts["scalar"] | {"first": others}, run, later_weights)

            @block.vector
            def _(dve):
                def run(order, turn, when):
                    for task in order:
                        kind, i = task
                        b = batch_of(task, turn)
                        if kind == "S":
                            dve.wait_ge(*S.filled(task, when))
                            src = ps_s[S.slot(task, when)]
                            nc.vector.tensor_reduce(negmax[:, i % 4, :],
                                                    src[0:QT, 0:2 * T].rearrange("p (q t) -> p q t", q=2),
                                                    AX.X, ALU.max, negate=True).then_inc(negmax_ready, 1)
                        elif kind == "T":
                            dve.wait_ge(*TR.filled(task, when))
                            src = ps_t[TR.slot(task, when)]
                            nc.vector.tensor_copy(probT[:, i % (2 * GROUP), :, :],
                                                  src[0:QT, 0:2 * T].rearrange("p (k t) -> p k t", k=2)
                                                  ).then_inc(TR.done[TR.slot(task, when)], 1)
                        elif kind == "inv":
                            use = ("S", GROUP * i + GROUP - 1)
                            dve.wait_ge(*emptied(S, use, when, task))
                            nc.vector.reciprocal(recip[:, i % 2, :, :], sums[:, i % 2, :, :]).then_inc(recip_ready, 1)
                        elif kind == "R":
                            src = ps_o[O.slot(("PV", i), when)]
                            steps = 2 * (GROUPS * b + i)
                            dve.wait_ge(spread_ready, GROUPS * b + i + 1)
                            nc.vector.tensor_tensor(o_sb[:, i % 2, :], src[:, 0:T], spread[:, i % 2, :], ALU.mult).then_inc(o_step, 1)
                            dve.wait_ge(o_step, steps + 1)
                            nc.vector.tensor_copy(oT[0][:, i, :], o_sb[:, i % 2, :]).then_inc(o_step, 1)
                            dve.wait_ge(o_step, steps + 2)
                            nc.vector.tensor_tensor(oT[1][:, i, :], o_sb[:, i % 2, :], oT[0][:, i, :].bitcast(F32),
                                                    ALU.subtract).then_inc(O.done[O.slot(("PV", i), when)], 1)
                        elif kind == "out":
                            if i == 0:
                                dve.wait_ge(xres_in, DMA * b + DMA)
                            dve.wait_ge(*O.filled(task, when))
                            src = ps_o[O.slot(task, when)]
                            nc.vector.tensor_tensor(xres[:, i, :], src[0:QT, :], xres[:, i, :],
                                                    ALU.add).then_inc(O.done[O.slot(task, when)], 1)
                        elif kind == "st":
                            if i == 0:
                                dve.wait_ge(x_in, DMA * b + DMA)
                            moments_of(nc, dve, xn[:, i, :], stats[:, i, :], moments[:, i, :], LN_EPS, ln_step,
                                       4 * b + 2 * i, var_ready, dve_passed)
                        elif kind == "ln":
                            dve.wait_ge(rstd_ready, 2 * b + i + 1)
                            nc.vector.tensor_scalar(xn[:, i, :], xn[:, i, :], moments[:, i, 0:1], rstd[:, i:i + 1],
                                                    ALU.subtract, ALU.mult).then_inc(xn_ready, 1)
                        elif kind == "yst":
                            dve.wait_ge(*O.emptied_before(("out", i), when))
                            moments_of(nc, dve, xres[:, i, :], y_stats[:, i, :], y_moments[:, i, :], LN_EPS, y_step,
                                       4 * b + 2 * i, y_var, dve_passed)
                        elif kind == "yln":
                            dve.wait_ge(y_rstd_ready, 2 * b + i + 1)
                            nc.vector.tensor_scalar(yn[:, i, :], xres[:, i, :], y_moments[:, i, 0:1], y_rstd[:, i:i + 1],
                                                    ALU.subtract, ALU.mult).then_inc(y_ready, 1)
                        elif kind == "zst":
                            dve.wait_ge(y_ready, 2 * b + i + 1)
                            moments_of(nc, dve, yn[:, i, :], y_stats[:, i, :], y_moments[:, i, :], XLN_EPS, z_step,
                                       4 * b + 2 * i, z_var, dve_passed)
                        elif kind == "zln":
                            dve.wait_ge(z_rstd_ready, 2 * b + i + 1)
                            nc.vector.tensor_scalar(yn[:, i, :], yn[:, i, :], y_moments[:, i, 0:1], y_rstd[:, i:i + 1],
                                                    ALU.subtract, ALU.mult).then_inc(z_ready, 1)
                        elif kind == "yt":
                            dve.wait_ge(yt_hi, 2 * b + i + 1)
                            src = ps_t[TR.slot(task, when)]
                            part = (slice(None), slice(None), slice(i * QT, (i + 1) * QT))
                            nc.vector.tensor_tensor(ynT[1][part], src[:, 0:KD * QT].rearrange("p (k t) -> p k t", k=KD),
                                                    ynT[0][part].bitcast(F32),
                                                    ALU.subtract).then_inc(TR.done[TR.slot(task, when)], 1)
                        elif kind == "xt":
                            dve.wait_ge(xt_hi, 2 * b + i + 1)
                            src = ps_t[TR.slot(task, when)]
                            part = (slice(None), slice(None), slice(i * QT, (i + 1) * QT))
                            nc.vector.tensor_tensor(xnT[1][part], src[:, 0:KD * QT].rearrange("p (k t) -> p k t", k=KD),
                                                    xnT[0][part].bitcast(F32),
                                                    ALU.subtract).then_inc(TR.done[TR.slot(task, when)], 1)
                        elif kind == "qk":
                            dve.wait_ge(qk_hi, 2 * GROUPS * b + i + 1)
                            src = ps_f[F.slot(task, when)]
                            part = (slice(None), i // GROUPS, i % GROUPS, slice(None))
                            nc.vector.scalar_tensor_tensor(
                                qk[1][part], src[:, 0:T], SCALE if i < GROUPS else 1.0, qk[0][part].bitcast(F32), ALU.mult,
                                ALU.subtract).then_inc(F.done[F.slot(task, when)], 1)

                for r in rings:
                    for d in r.done:
                        dve.sem_inc(d, 1)
                def low_parts(numbers):
                    for n in numbers:
                        _, split_to, k = chunks[n]
                        raw = chunk_in(dve, n)
                        dve.wait_ge(w_hi, n + 1)
                        nc.vector.scalar_tensor_tensor(split_to[1], raw, 1.0 if k is None else s_col[:, k:k + 1], split_to[0].bitcast(F32),
                                                       ALU.mult, ALU.subtract).then_inc(w_lo, 1)

                def later_weights():
                    low_parts(range(EARLY + KD, len(chunks)))
                    dve.wait_ge(bias_full, KD)
                    nc.vector.tensor_reduce(qbias[:, :], ps_o[0][:, 0:MD * KD].rearrange("p (m k) -> p m k", m=MD), AX.X, ALU.add).then_inc(bias_step, 1)
                    dve.wait_ge(bias_step, 1)
                    nc.vector.tensor_scalar(qbias[:, :], qbias[:, :], QSCALE, None, ALU.mult).then_inc(bias_ready, 1)

                transposes, to_qk, others = first_steps(parts["vector"])
                run(only(others, "st", "ln"), -1, ("first", 0))
                low_parts(range(KD))
                run(transposes, -1, ("first", 0))
                low_parts(range(KD, EARLY))
                run(to_qk, -1, ("first", 0))
                low_parts(QUERY)
                all_turns(dve, parts["vector"] | {"first": [t for t in others if t[0] not in ("st", "ln")]}, run, later_weights)


def cross_attention(nc, context, mask, null_kv, q_T, y, shared, kv_raw, kv_in, o_raw, o_in, s_col, b_col, ln_in, load_next_weights):
    B, KEYS, D = context.shape
    T = q_T.shape[2]
    E = q_T.shape[1]
    DH = null_kv.shape[1]
    HEADS = E // DH
    QT = T // 2
    KD = D // P
    ED = E // P
    STEPS, GH = 4, HEADS // 4
    GE = GH * DH
    KT = -(-(KEYS + 1) // P)
    KP = KT * P
    HALF = KP // 2
    FULL_T, TAIL = KEYS // P, KEYS % P
    KCHUNK = KEYS // 2
    TURNS = B - 1

    table = {
        "tensor": """
            T0.0.0 T0.0.1 K1.0.0 T0.0.2 S0.2.0 K1.0.1 T0.1.0 T0.1.1 S0.2.1 T0.1.2 V1.0 S0.3.0 PV0.0 S0.3.1 T0.2.0 T0.2.1 V1.1
            S1.0.0 T0.2.2 K1.1.0 T0.3.0 R0.0 S1.0.1 T0.3.1 K1.1.1 S1.1.0 T0.3.2 V1.2 S1.1.1 PV0.1
            T1.0.0 T1.0.1 R0.1 S1.2.0 T1.0.2 K2.0.0 T1.1.0 S1.2.1 K2.0.1 T1.1.1 T1.1.2 S1.3.0 V2.0 S1.3.1 PV1.0 T1.2.0 R1.0
            S2.0.0 T1.2.1 T1.2.2 V2.1 S2.0.1 T1.3.0 K2.1.0 S2.1.0 T1.3.1 K2.1.1 T1.3.2 V2.2 S2.1.1 PV1.1
            T2.0.0 S2.2.0 T2.0.1 R1.1 T2.0.2 K3.0.0 T2.1.0 S2.2.1 K3.0.1 T2.1.1 S2.3.0 T2.1.2 V3.0 PV2.0 T2.2.0 S2.3.1 T2.2.1
            V3.1 T2.2.2 S3.0.0 T2.3.0 R2.0 K3.1.0 S3.0.1 T2.3.1 T2.3.2 K3.1.1 S3.1.0 V3.2 xt0 xt1 S3.1.1 PV2.1
            T3.0.0 T3.0.1 S3.2.0 T3.0.2 xt2 xt3 S3.2.1 T3.1.0 R2.1 T3.1.1 T3.1.2 S3.3.0 xt4 xt5 PV3.0 S3.3.1 K0.0.0 R3.0
            T3.2.0 K0.0.1 T3.2.1 T3.2.2 V0.0 T3.3.0 S0.0.0 K0.1.0 T3.3.1 S0.0.1 K0.1.1 S0.1.0 T3.3.2 V0.1 PV3.1 R3.1 V0.2 out0
            S0.1.1 out1""",
        "scalar": """
            T0.0.0 T0.0.2 K1.0.0 S0.2.0 T0.1.0 T0.1.2 K1.0.1 S0.2.1 Q1.0 S0.3.0 S0.3.1 T0.2.0 Q1.1 inv0.0 inv0.1 T0.2.2 K1.1.0
            T0.3.0 S1.0.0 T0.3.2 R0.0 S1.0.1 K1.1.1
            T1.0.0 S1.1.0 S1.1.1 T1.0.2 Q2.0 K2.0.0 inv1.0 T1.1.0 S1.2.0 T1.1.2 S1.2.1 K2.0.1 T1.2.0 S1.3.0 R0.1 S1.3.1 Q2.1
            S2.0.0 T1.2.2 R1.0 T1.3.0 K2.1.0 inv1.1 T1.3.2 S2.0.1 K2.1.1
            T2.0.0 S2.1.0 S2.1.1 T2.0.2 T2.1.0 K3.0.0 S2.2.0 S2.2.1 Q3.0 T2.1.2 R1.1 K3.0.1 T2.2.0 S2.3.0 S2.3.1 inv2.0 T2.2.2
            Q3.1 T2.3.0 inv2.1 R2.0 K3.1.0 K3.1.1 S3.0.0 T2.3.2 S3.0.1 S3.1.0 xt0 xt1
            T3.0.0 S3.1.1 T3.0.2 xt2 xt3 inv3.0 T3.1.0 T3.1.2 R2.1 xt4 xt5 S3.2.0 S3.2.1 S3.3.0 K0.0.0 T3.2.0 S3.3.1 Q0.0
            K0.0.1 T3.2.2 T3.3.0 K0.1.0 S0.0.0 R3.0 inv3.1 S0.0.1 T3.3.2 K0.1.1 Q0.1 S0.1.0 R3.1 out0 S0.1.1 out1""",
        "vector": """
            T0.0.1 inv0.0 st0 S0.2.0 K1.0.0 T0.1.1 S0.2.1 S0.3.0 K1.0.1 S0.3.1 V1.0 Q1.0 T0.2.1 V1.1 inv0.1 S1.0.0 S1.0.1
            T0.3.1 K1.1.0 Q1.1 S1.1.0 K1.1.1 S1.1.1 R0.0 V1.2
            T1.0.1 ln0 S1.2.0 st1 inv1.0 S1.2.1 Q2.0 K2.0.0 S1.3.0 T1.1.1 S1.3.1 K2.0.1 T1.2.1 S2.0.0 V2.0 st2 Q2.1 S2.0.1
            V2.1 R0.1 K2.1.0 inv1.1 T1.3.1 S2.1.0 st3 S2.1.1 K2.1.1 V2.2 R1.0
            T2.0.1 S2.2.0 S2.2.1 K3.0.0 ln1 T2.1.1 st4 K3.0.1 S2.3.0 inv2.0 V3.0 S2.3.1 R1.1 Q3.0 T2.2.1 ln2 S3.0.0 inv2.1
            V3.1 ln3 S3.0.1 K3.1.0 Q3.1 R2.0 S3.1.0 T2.3.1 ln4 K3.1.1 st5 xt0 S3.1.1 xt1 V3.2
            T3.0.1 ln5 S3.2.0 inv3.0 xt2 xt3 S3.2.1 T3.1.1 S3.3.0 xt4 xt5 S3.3.1 K0.0.0 T3.2.1 Q0.0 K0.0.1 mask V0.0 S0.0.0
            R2.1 T3.3.1 S0.0.1 inv3.1 K0.1.0 R3.0 S0.1.0 V0.1 K0.1.1 R3.1 V0.2 S0.1.1 Q0.1""",
    }
    table = {engine: tasks(t) for engine, t in table.items()}

    def ahead(task):
        kind = task[0]
        return (kind in ("st", "ln", "xt", "mask") or (kind in ("K", "V", "Q") and task[1] == 0)
                or (kind == "S" and task[1] == 0 and task[2] < 2))

    first = {engine: [t for t in order if ahead(t)] for engine, order in table.items()}
    last = {engine: [t for t in order if not ahead(t)] for engine, order in table.items()}

    def only(order, *kinds):
        return [u for u in order if u[0] in kinds]

    with ExitStack() as ctx:
        at = Place(nc, ctx, "ca")
        wkv = [at.sb(f"wkv_{n}", [P, KD, 2 * E], F32R) for n in ("hi", "lo")]
        wo = [at.sb(f"wo_{n}", [P, ED, D], F32R) for n in ("hi", "lo")]
        kbias = at.sb("kbias", [P, ED])
        vbias = at.sb("vbias", [P, E])

        cn = at.sb("cn", [P, KT, D])
        ctx_in = at.sem("ctx_in")
        ctx_full = context[:, 0:FULL_T * P, :].rearrange("b (t p) d -> b p t d", p=P)

        def load_context(sp, b):
            sp.dma_start(cn[:, 0:FULL_T, :], ctx_full[bass.ds(b, 1)].rearrange("o p t d -> (o p) t d")).then_inc(ctx_in, DMA)
            sp.dma_start(cn[0:TAIL, FULL_T, :], context[bass.ds(b, 1), FULL_T * P:KEYS, :]
                         .rearrange("o p d -> (o p) d")).then_inc(ctx_in, DMA)

        stats, moments = at.sb("stats", [P, KT, 6]), at.sb("moments", [P, KT, 2])
        rstd = at.sb("rstd", [P, KT])
        ident, minus_half = at.sb("ident", [P, P]), at.sb("minus_half", [P, 1])
        ident_ready, dve_passed = at.sem("ident_ready"), at.sem("dve_passed")
        var_ready, rstd_ready, ln_step, cn_ready = at.sem("var_ready"), at.sem("rstd_ready"), at.sem("ln_step"), at.sem("cn_ready")
        ROWS = [P] * FULL_T + [TAIL]

        null_k = at.sb("null_k", [P, 1])
        null_part = [at.sb(f"null_{n}", [P, 1], F32R) for n in ("hi", "lo")]
        q_raw = at.sb("q_raw", [P, GH, T])
        mask_u8 = at.sb("mask_u8", [QT, KEYS], U8)
        mask_in, q_in, null_in, null_step = at.sem("mask_in"), at.sem("q_in"), at.sem("null_in"), at.sem("null_step")
        q_v = q_T.rearrange("b (h d) t -> b d h t", d=DH)

        def load_mask(sp, b):
            sp.dma_start(mask_u8[:, :], mask[bass.ds(b, 1), :].rearrange("o s -> (o s)").partition_broadcast(QT)).then_inc(mask_in, DMA)

        def load_queries(sp, b, g):
            for half in range(2):
                sp.dma_start(q_raw[half * DH:(half + 1) * DH, :, :],
                             q_v[bass.ds(b, 1), :, g * GH:(g + 1) * GH].rearrange("o d h t -> (o d) h t")).then_inc(q_in, DMA)

        def norm(dve, task, b):
            kind, i = task
            n = ROWS[i]
            if kind == "st":
                if i == 0:
                    dve.wait_ge(ctx_in, 2 * DMA * b + 2 * DMA)
                moments_of(nc, dve, cn[0:n, i, :], stats[0:n, i, :], moments[0:n, i, :], XLN_EPS, ln_step,
                           2 * (KT * b + i), var_ready, dve_passed)
            else:
                dve.wait_ge(rstd_ready, KT * b + i + 1)
                nc.vector.tensor_scalar(cn[0:n, i, :], cn[0:n, i, :], moments[0:n, i, 0:1], rstd[0:n, i:i + 1],
                                        ALU.subtract, ALU.mult).then_inc(cn_ready, 1)

        def run_norms(dve):
            for task in only(first["vector"], "st", "ln"):
                norm(dve, task, 0)

        def inverse_roots(pool, b):
            for t, n in enumerate(ROWS):
                inverse_root(nc, pool, rstd[0:n, t:t + 1], moments[0:n, t, 1:2], minus_half[0:n, :], var_ready, KT * b + t, rstd_ready)

        with ExitStack() as setup_ctx:
            su = Place(nc, setup_ctx, "cw")
            b_rows = su.sb("b_rows", [P, KD, P])
            krows = su.sb("krows", [P, ED, P])
            ps_b = su.psum("ps_b", [P, 2 * E])
            hi_step, lo_step, rows_ready, bias_full = su.sem("hi_step"), su.sem("lo_step"), su.sem("rows_ready"), su.sem("bias_full")

            with nc.Block() as block:

                @block.sync
                def _(sp):
                    load_context(sp, 0)
                    load_mask(sp, 0)
                    load_queries(sp, 0, 0)
                    for half in range(2):
                        sp.dma_start(null_k[half * DH:(half + 1) * DH, :], null_kv[0:1, :].rearrange("o (d x) -> (o d) x", x=1)).then_inc(null_in, DMA)

                @block.gpsimd
                def _(pool):
                    make_constants(nc, pool, ident, minus_half, ident_ready)
                    inverse_roots(pool, 0)
                    pool.wait_ge(hi_step, KD + 1)
                    nc.gpsimd.tensor_tensor(wo[1][:, :, :], o_raw[:, :, :], wo[0][:, :, :].bitcast(F32), ALU.subtract)

                @block.scalar
                def _(act):
                    act.wait_ge(ln_in, 2 * DMA)
                    for k in range(KD):
                        act.wait_ge(kv_in[k], DMA)
                        nc.scalar.activation(wkv[0][:, k, :], kv_raw[:, k, :], ACT.Copy, scale=s_col[:, k:k + 1]).then_inc(hi_step, 1)
                    act.wait_ge(o_in, DMA)
                    nc.scalar.activation(wo[0][:, :, :], o_raw[:, :, :], ACT.Copy).then_inc(hi_step, 1)
                    act.wait_ge(bias_full, 1)
                    nc.scalar.activation(vbias[:, :], ps_b[:, E:2 * E], ACT.Copy)

                @block.vector
                def _(dve):
                    dve.wait_ge(ln_in, 2 * DMA)
                    nc.vector.tensor_copy(b_rows[:, :, :], b_col[:, :].unsqueeze(2).to_broadcast([P, KD, P])).then_inc(rows_ready, 1)
                    run_norms(dve)
                    for k in range(KD):
                        dve.wait_ge(hi_step, k + 1)
                        nc.vector.scalar_tensor_tensor(wkv[1][:, k, :], kv_raw[:, k, :], s_col[:, k:k + 1],
                                                       wkv[0][:, k, :].bitcast(F32), ALU.mult, ALU.subtract)
                    dve.wait_ge(null_in, 2 * DMA)
                    nc.vector.tensor_copy(null_part[0][:, :], null_k[:, :]).then_inc(null_step, 1)
                    dve.wait_ge(null_step, 1)
                    nc.vector.tensor_tensor(null_part[1][:, :], null_k[:, :], null_part[0][:, :].bitcast(F32), ALU.subtract).then_inc(null_step, 1)
                    dve.wait_ge(null_step, 2)
                    dve.wait_ge(bias_full, 1)
                    dve.wait_ge(ident_ready, 3)
                    nc.vector.tensor_tensor(krows[:, :, :], ps_b[:, 0:E].rearrange("p (m n) -> p m n", m=ED),
                                            ident[:, :].unsqueeze(1).to_broadcast([P, ED, P]), ALU.mult).then_inc(lo_step, 1)
                    dve.wait_ge(lo_step, 1)
                    nc.vector.tensor_reduce(kbias[:, :], krows[:, :, :], AX.X, ALU.add).then_inc(lo_step, 1)
                    dve.wait_ge(lo_step, 2)

                @block.tensor
                def _(pe):
                    pe.wait_ge(rows_ready, 1)
                    for k in range(KD):
                        pe.wait_ge(kv_in[k], DMA)
                    for a in range(2 * E // 512):
                        for k in range(KD):
                            ins = nc.tensor.matmul(ps_b[:, a * 512:(a + 1) * 512], b_rows[:, k, :], kv_raw[:, k, a * 512:(a + 1) * 512],
                                                   start=k == 0, stop=k == KD - 1)
                    ins.then_inc(bias_full, 1)

        shared.restart()
        cnT = [shared.tensor(f"ca_cnT_{n}", [P, KD, KEYS + 2], F32R) for n in ("hi", "lo")]
        kstack = shared.tensor("ca_kstack", [P, GH, KP], F32R)
        v_sb = shared.tensor("ca_v", [P, 2, KT, GE])
        q_part = [at.sb(f"q_{n}", [P, GH, T], F32R) for n in ("hi", "lo")]
        penalty = at.sb("penalty", [QT, KP])
        prob = at.sb("prob", [QT, 2, 2, KP])
        low = at.sb("low", [QT, 2, 2])
        sums, recip = at.sb("sums", [QT, 2, 2, 2]), at.sb("recip", [QT, 2, 2, 2])
        rsum = at.sb("rsum", [QT, 2, 2, P])
        probT = at.sb("probT", [P, 2, KT, T])
        spread = at.sb("spread", [P, 2, T])
        o_sb = at.sb("o", [P, 2, T])
        oT = [at.sb(f"oT_{n}", [P, ED, T], F32R) for n in ("hi", "lo")]
        y_sb = at.sb("y", [QT, 2, D])

        ps_s = at.psum("ps_s", [P, 2, 512])
        ps_t = [at.psum(f"ps_t{i}", [P, 512]) for i in range(2)]
        ps_f = [at.psum(f"ps_f{i}", [P, 512]) for i in range(2)]
        ps_o = [at.psum(f"ps_o{i}", [P, 512]) for i in range(2)]

        def ring(name, slots, *kinds):
            return Ring(at.sem(f"{name}_full"), [at.sem(f"{name}_done{i}") for i in range(slots)],
                        {"first": only(first["tensor"], *kinds), "turn": only(table["tensor"], *kinds),
                         "last": only(last["tensor"], *kinds)}, TURNS)

        S = ring("scores", 1, "S")
        TR = ring("transposed", 2, "T", "xt")
        F = ring("projected", 2, "K", "V")
        O = ring("heads", 2, "PV", "out")
        rings = [S, TR, F, O]

        sp_passed = at.sem("sp_passed")
        y_stored = at.sem("y_stored")
        fixed_ready, nullv_in = at.sem("fixed_ready"), at.sem("nullv_in")
        xt_hi, k_hi = at.sem("xt_hi"), at.sem("k_hi")
        q_hi, q_lo, mask_ready = at.sem("q_hi"), at.sem("q_lo"), at.sem("mask_ready")
        exp_done, recip_ready, rsum_ready, spread_ready, o_step = at.sem("exp_done"), at.sem("recip_ready"), at.sem("rsum_ready"), at.sem("spread_ready"), at.sem("o_step")

        y_v = y.rearrange("b (q p) d -> b p q d", p=QT)

        with nc.Block() as block:

            @block.gpsimd
            def _(pool):
                nc.gpsimd.memset(kstack[:, :, KEYS + 1:KP].bitcast(F32), 0.0).then_inc(fixed_ready, 1)
                for c in cnT:
                    nc.gpsimd.memset(c[:, :, KEYS:KEYS + 2].bitcast(F32), 0.0).then_inc(fixed_ready, 1)
                nc.gpsimd.memset(penalty[:, KEYS:KEYS + 1], 0.0).then_inc(fixed_ready, 1)
                nc.gpsimd.memset(penalty[:, KEYS + 1:KP], BIG).then_inc(fixed_ready, 1)
                pool.wait_ge(fixed_ready, 5)
                nc.gpsimd.memset(v_sb[96:P, :, KT - 1, :], 0.0).then_inc(fixed_ready, 1)
                with pool.Fori(0, TURNS) as b:
                    inverse_roots(pool, b + 1)

            @block.sync
            def _(sp):
                def store(b, when):
                    sp.wait_ge(*O.emptied(("out", 0), when))
                    sp.sem_inc(sp_passed, 1)
                    sp.wait_ge(*O.emptied(("out", 1), when))
                    sp.sem_inc(sp_passed, 1)
                    sp.dma_start(y_v[bass.ds(b, 1)].rearrange("o p q d -> (o p) q d"), y_sb[:, :, :]).then_inc(y_stored, DMA)

                sp.wait_ge(fixed_ready, 6)
                for n in range(2):
                    for h in range(GH):
                        sp.dma_start(v_sb[TAIL:TAIL + 1, n, KT - 1, h * DH:(h + 1) * DH], null_kv[1:2, :]).then_inc(nullv_in, DMA)
                sp.wait_ge(q_lo, 2)
                load_queries(sp, 0, 1)
                sp.wait_ge(xt_hi, KT)
                load_context(sp, 1)

                def turn(b, when, more):
                    sp.wait_ge(mask_ready, b + 1)
                    sp.sem_inc(sp_passed, 1)
                    load_mask(sp, b + 1)
                    for g in range(STEPS):
                        if more and g == STEPS - 1:
                            sp.wait_ge(xt_hi, KT * b + 2 * KT)
                            sp.sem_inc(sp_passed, 1)
                            load_context(sp, b + 2)
                        sp.wait_ge(q_lo, 2 * STEPS * b + 2 * g + 4)
                        sp.sem_inc(sp_passed, 1)
                        if g + 2 < STEPS:
                            load_queries(sp, b, g + 2)
                        else:
                            load_queries(sp, b + 1, g + 2 - STEPS)
                    store(b, when)

                with sp.Fori(0, TURNS - 1) as b:
                    turn(b, ("turn", b), True)
                turn(TURNS - 1, ("turn", TURNS - 1), False)
                for g in range(STEPS - 2):
                    sp.wait_ge(q_lo, 2 * STEPS * TURNS + 2 * g + 4)
                    sp.sem_inc(sp_passed, 1)
                    load_queries(sp, TURNS, g + 2)
                sp.wait_ge(*F.filled(only(last["tensor"], "K", "V")[-1], ("last", TURNS)))
                load_next_weights(sp)
                store(TURNS, ("last", TURNS))
                sp.wait_ge(y_stored, DMA * B + DMA)

            @block.tensor
            def _(pe):
                def split_products(out, lhs, rhs, first_, last_):
                    for n, (i, j) in enumerate(((0, 0), (0, 1), (1, 0))):
                        ins = nc.tensor.matmul(out, lhs[i], rhs[j], start=first_ and n == 0, stop=last_ and n == 2)
                    return ins

                def run(order, turn, when):
                    for task in order:
                        kind, b = task[0], turn + 1 if ahead(task) else turn
                        if kind == "S":
                            _, g, h, q = task
                            if h % 2 == 0 and q == 0:
                                pe.wait_ge(q_lo, 2 * STEPS * b + 2 * g + h // 2 + 1)
                                for c in range(2):
                                    pe.wait_ge(*(F.emptied_before if g == 0 and h >= 2 else F.emptied)(("K", g, h // 2, c), when))
                            pe.wait_ge(*S.free(task, when))
                            for n in range(2):
                                for c in range(2):
                                    ins = nc.tensor.matmul(ps_s[0:QT, c, 0:HALF], q_part[n][:, h, q * QT:(q + 1) * QT],
                                                           kstack[:, h, c * HALF:(c + 1) * HALF], start=n == 0, stop=n == 1)
                            ins.then_inc(S.full, 1)
                        elif kind == "T":
                            _, g, h, u = task
                            if u == 0:
                                pe.wait_ge(exp_done, 2 * (HEADS * b + GH * g + h) + 2)
                            pe.wait_ge(*TR.free(task, when))
                            out = ps_t[TR.slot(task, when)]
                            for k in range(2):
                                for q in range(2):
                                    ins = nc.tensor.transpose(out[:, k * T + q * QT:k * T + (q + 1) * QT],
                                                              prob[:, h % 2, q, (2 * u + k) * P:(2 * u + k + 1) * P],
                                                              ident[0:QT, 0:QT])
                            ins.then_inc(TR.full, 1)
                        elif kind == "PV":
                            _, g, i = task
                            for use in latest(TR, *((("T", g, 2 * i + j, u), when) for j in range(2) for u in range(KT // 2))):
                                pe.wait_ge(*TR.emptied(use, when))
                            if i == 0:
                                mine = when if g else ("turn", 0)
                                for use in latest(F, *((("V", g, j), mine) for j in range(KT // 2))):
                                    pe.wait_ge(*(F.emptied if g else F.emptied_before)(use, when))
                            pe.wait_ge(*O.free(task, when))
                            out = ps_o[O.slot(task, when)]
                            for k in range(KT):
                                for j in range(2):
                                    col = (2 * i + j) * DH
                                    nc.tensor.matmul(out[j * DH:(j + 1) * DH, 0:T], v_sb[:, g % 2, k, col:col + DH],
                                                     probT[:, j, k, :], start=k == 0, stop=k == KT - 1)
                        elif kind == "R":
                            _, g, i = task
                            pe.wait_ge(rsum_ready, ED * b + 2 * g + i + 1)
                            out = ps_o[O.slot(("PV", g, i), when)]
                            for q in range(2):
                                ins = nc.tensor.transpose(out[:, 256 + q * QT:256 + (q + 1) * QT], rsum[:, i, q, :], ident[0:QT, 0:QT])
                            ins.then_inc(O.full, 1)
                        elif kind == "xt":
                            _, i = task
                            pe.wait_ge(cn_ready, KT * b + i + 1)
                            pe.wait_ge(*TR.free(task, when))
                            out = ps_t[TR.slot(task, when)]
                            n = ROWS[i]
                            for k in range(KD):
                                ins = nc.tensor.transpose(out[:, k * P:k * P + n], cn[0:n, i, k * P:(k + 1) * P], ident[0:n, 0:n])
                            ins.then_inc(TR.full, 1)
                        elif kind == "K":
                            _, g, i, c = task
                            if g == 0 and i == 0 and c == 0:
                                for use in latest(TR, *((("xt", t), when) for t in range(KT))):
                                    pe.wait_ge(*TR.emptied(use, when))
                            pe.wait_ge(*F.free(task, when))
                            out = ps_f[F.slot(task, when)]
                            col = (2 * g + i) * P
                            for k in range(KD):
                                ins = split_products(out[:, 0:KCHUNK + 1], [w[:, k, col:col + P] for w in wkv],
                                                     [t[:, k, c * KCHUNK:(c + 1) * KCHUNK + 1] for t in cnT], k == 0, k == KD - 1)
                            ins.then_inc(F.full, 1)
                        elif kind == "V":
                            _, g, j = task
                            pe.wait_ge(*F.free(task, when))
                            out = ps_f[F.slot(task, when)]
                            col = E + g * GE
                            for t in (2 * j, 2 * j + 1):
                                n = ROWS[t]
                                for k in range(KD):
                                    ins = split_products(out[0:n, (t % 2) * GE:(t % 2 + 1) * GE],
                                                         [c[:, k, t * P:t * P + n] for c in cnT],
                                                         [w[:, k, col:col + GE] for w in wkv], k == 0, k == KD - 1)
                            ins.then_inc(F.full, 1)
                        elif kind == "out":
                            _, i = task
                            for p in range(2):
                                pe.wait_ge(*O.emptied(("PV", STEPS - 1, p), when))
                            pe.wait_ge(*O.free(task, when))
                            out = ps_o[O.slot(task, when)]
                            for m in range(ED):
                                ins = split_products(out[0:QT, :], [o[:, m, i * QT:(i + 1) * QT] for o in oT],
                                                     [w[:, m, :] for w in wo], m == 0, m == ED - 1)
                            ins.then_inc(O.full, 1)

                pe.wait_ge(ident_ready, 3)
                pe.wait_ge(fixed_ready, 6)
                scores = first["tensor"].index(only(first["tensor"], "S")[0])
                run(first["tensor"][:scores], -1, ("first", 0))
                pe.wait_ge(null_step, 6)
                run(first["tensor"][scores:], -1, ("first", 0))
                pe.wait_ge(nullv_in, 2 * GH * DMA)
                with pe.Fori(0, TURNS) as b:
                    run(table["tensor"], b, ("turn", b))
                run(last["tensor"], TURNS, ("last", TURNS))

            @block.scalar
            def _(act):
                def run(order, turn, when):
                    for task in order:
                        kind, b = task[0], turn + 1 if ahead(task) else turn
                        if kind == "S":
                            _, g, h, q = task
                            act.wait_ge(*S.emptied(task, when))
                            nc.scalar.activation(prob[:, h % 2, q, :], prob[:, h % 2, q, :], ACT.Exp,
                                                 bias=low[:, h % 2, q:q + 1], scale=-1.0,
                                                 accum_out=sums[:, h // 2, q, h % 2:h % 2 + 1]).then_inc(exp_done, 1)
                        elif kind == "T":
                            _, g, h, u = task
                            act.wait_ge(*TR.filled(task, when))
                            src = ps_t[TR.slot(task, when)]
                            nc.scalar.activation(probT[:, h % 2, 2 * u:2 * u + 2, :],
                                                 src[:, 0:2 * T].rearrange("p (k t) -> p k t", k=2),
                                                 ACT.Copy).then_inc(TR.done[TR.slot(task, when)], 1)
                        elif kind == "inv":
                            _, g, i = task
                            act.wait_ge(recip_ready, ED * b + 2 * g + i + 1)
                            nc.scalar.activation(rsum[:, i, :, :].rearrange("p q (j d) -> p (q j) d", d=DH),
                                                 recip[:, i, :, :].rearrange("p q j -> p (q j)").unsqueeze(2)
                                                 .to_broadcast([QT, 4, DH]), ACT.Copy).then_inc(rsum_ready, 1)
                        elif kind == "R":
                            _, g, i = task
                            use = ("PV", g, i)
                            act.wait_ge(*O.filled(use, when))
                            nc.scalar.activation(spread[:, i, :], ps_o[O.slot(use, when)][:, 256:256 + T], ACT.Copy).then_inc(spread_ready, 1)
                        elif kind == "xt":
                            _, i = task
                            act.wait_ge(*TR.filled(task, when))
                            n = ROWS[i]
                            nc.scalar.activation(cnT[0][:, :, i * P:i * P + n],
                                                 ps_t[TR.slot(task, when)][:, :].rearrange("p (k t) -> p k t", k=KD)[:, :, 0:n],
                                                 ACT.Copy).then_inc(xt_hi, 1)
                        elif kind == "K":
                            _, g, i, c = task
                            act.wait_ge(*F.filled(task, when))
                            src = ps_f[F.slot(task, when)]
                            for j in range(2):
                                rows = slice(j * DH, (j + 1) * DH)
                                ins = nc.scalar.activation(kstack[rows, 2 * i + j, c * KCHUNK:(c + 1) * KCHUNK], src[rows, 0:KCHUNK],
                                                           ACT.Identity, bias=kbias[rows, 2 * g + i:2 * g + i + 1], scale=1.0)
                            ins.then_inc(k_hi, 1)
                        elif kind == "Q":
                            _, g, i = task
                            if i == 0:
                                act.wait_ge(q_in, 2 * DMA * (STEPS * b + g) + 2 * DMA)
                            nc.scalar.activation(q_part[0][:, 2 * i:2 * i + 2, :], q_raw[:, 2 * i:2 * i + 2, :], ACT.Copy).then_inc(q_hi, 1)
                        elif kind == "out":
                            _, i = task
                            if i == 0:
                                act.wait_ge(y_stored, DMA * b + DMA)
                            act.wait_ge(*O.filled(task, when))
                            nc.scalar.activation(y_sb[:, i, :], ps_o[O.slot(task, when)][0:QT, :], ACT.Copy).then_inc(O.done[O.slot(task, when)], 1)

                act.sem_inc(y_stored, DMA)
                act.wait_ge(fixed_ready, 6)
                run(first["scalar"], -1, ("first", 0))
                with act.Fori(0, TURNS) as b:
                    run(table["scalar"], b, ("turn", b))
                run(last["scalar"], TURNS, ("last", TURNS))

            @block.vector
            def _(dve):
                def run(order, turn, when):
                    for task in order:
                        kind, b = task[0], turn + 1 if ahead(task) else turn
                        if kind == "S":
                            _, g, h, q = task
                            if g == 0 and h == 0 and q == 0:
                                dve.wait_ge(mask_ready, b + 1)
                            if q == 0 and when[0] != "first":
                                dve.wait_ge(*TR.filled(("T", g, h - 2, 2) if h >= 2 else ("T", (g - 1) % STEPS, h + 2, 2), when))
                            dve.wait_ge(*S.filled(task, when))
                            dve.sem_inc(dve_passed, 1)
                            nc.vector.tensor_tensor_reduce(out=prob[:, h % 2, q, :].rearrange("p (c s) -> p c s", c=2),
                                                           in0=ps_s[0:QT, :, 0:HALF],
                                                           in1=penalty[:, :].rearrange("p (c s) -> p c s", c=2),
                                                           scale=1.0, scalar=BIG, op0=ALU.add, op1=ALU.min,
                                                           accum_out=low[:, h % 2, q:q + 1]).then_inc(S.done[0], 1)
                        elif kind == "T":
                            _, g, h, u = task
                            dve.wait_ge(*TR.filled(task, when))
                            nc.vector.tensor_copy(probT[:, h % 2, 2 * u:2 * u + 2, :],
                                                  ps_t[TR.slot(task, when)][:, 0:2 * T].rearrange("p (k t) -> p k t", k=2)
                                                  ).then_inc(TR.done[TR.slot(task, when)], 1)
                        elif kind == "inv":
                            _, g, i = task
                            dve.wait_ge(exp_done, 2 * (HEADS * b + GH * g + 2 * i + 1) + 2)
                            nc.vector.reciprocal(recip[:, i, :, :], sums[:, i, :, :]).then_inc(recip_ready, 1)
                        elif kind == "R":
                            _, g, i = task
                            use = ("PV", g, i)
                            m = 2 * g + i
                            steps = 2 * (ED * b + m)
                            dve.wait_ge(spread_ready, ED * b + m + 1)
                            nc.vector.tensor_tensor(o_sb[:, i, :], ps_o[O.slot(use, when)][:, 0:T], spread[:, i, :], ALU.mult).then_inc(o_step, 1)
                            dve.wait_ge(o_step, steps + 1)
                            nc.vector.tensor_copy(oT[0][:, m, :], o_sb[:, i, :]).then_inc(o_step, 1)
                            dve.wait_ge(o_step, steps + 2)
                            nc.vector.tensor_tensor(oT[1][:, m, :], o_sb[:, i, :], oT[0][:, m, :].bitcast(F32),
                                                    ALU.subtract).then_inc(O.done[O.slot(use, when)], 1)
                        elif kind in ("st", "ln"):
                            norm(dve, task, b)
                        elif kind == "xt":
                            _, i = task
                            dve.wait_ge(xt_hi, KT * b + i + 1)
                            n = ROWS[i]
                            part = (slice(None), slice(None), slice(i * P, i * P + n))
                            nc.vector.tensor_tensor(cnT[1][part], ps_t[TR.slot(task, when)][:, :].rearrange("p (k t) -> p k t", k=KD)[:, :, 0:n],
                                                    cnT[0][part].bitcast(F32), ALU.subtract).then_inc(TR.done[TR.slot(task, when)], 1)
                        elif kind == "K":
                            _, g, i, c = task
                            dve.wait_ge(k_hi, 4 * (STEPS * b + g) + 2 * i + c + 1)
                            src = ps_f[F.slot(task, when)]
                            keys = slice(c * KCHUNK, (c + 1) * KCHUNK)
                            for j in range(2):
                                rows, other = slice(j * DH, (j + 1) * DH), slice((1 - j) * DH, (2 - j) * DH)
                                ins = nc.vector.scalar_tensor_tensor(
                                    kstack[other, 2 * i + j, keys], src[rows, 0:KCHUNK], kbias[rows, 2 * g + i:2 * g + i + 1],
                                    kstack[rows, 2 * i + j, keys].bitcast(F32), ALU.add, ALU.subtract)
                            ins.then_inc(F.done[F.slot(task, when)], 1)
                        elif kind == "V":
                            _, g, j = task
                            dve.wait_ge(*F.filled(task, when))
                            src = ps_f[F.slot(task, when)][:, :].rearrange("p (t n) -> p t n", t=2)
                            bias = vbias[:, g * GE:(g + 1) * GE]
                            if ROWS[2 * j + 1] == P:
                                ins = nc.vector.tensor_tensor(v_sb[:, g % 2, 2 * j:2 * j + 2, :], src,
                                                              bias.unsqueeze(1).to_broadcast([P, 2, GE]), ALU.add)
                            else:
                                for t in (2 * j, 2 * j + 1):
                                    n = ROWS[t]
                                    ins = nc.vector.tensor_tensor(v_sb[0:n, g % 2, t, :], src[0:n, t % 2, :], bias[0:n, :], ALU.add)
                            ins.then_inc(F.done[F.slot(task, when)], 1)
                        elif kind == "Q":
                            _, g, i = task
                            part = (slice(None), slice(2 * i, 2 * i + 2), slice(None))
                            dve.wait_ge(q_hi, 2 * (STEPS * b + g) + i + 1)
                            nc.vector.tensor_tensor(q_part[1][part], q_raw[part], q_part[0][part].bitcast(F32),
                                                    ALU.subtract).then_inc(q_lo, 1)
                        elif kind == "mask":
                            dve.wait_ge(mask_in, DMA * b + DMA)
                            nc.vector.tensor_scalar(penalty[:, 0:KEYS], mask_u8[:, :], -1.0, -BIG, ALU.add, ALU.mult).then_inc(mask_ready, 1)

                for r in rings:
                    for d in r.done:
                        dve.sem_inc(d, 1)
                dve.wait_ge(fixed_ready, 6)
                for j in range(2):
                    for half in range(2):
                        rows = slice(half * DH, (half + 1) * DH)
                        nc.vector.tensor_copy(kstack[rows, j:GH:2, KEYS:KEYS + 1],
                                              null_part[(half + j) % 2][rows, :].bitcast(F32).unsqueeze(1).to_broadcast([DH, GH // 2, 1])
                                              ).then_inc(null_step, 1)
                run([t for t in first["vector"] if t[0] not in ("st", "ln")], -1, ("first", 0))
                with dve.Fori(0, TURNS) as b:
                    run(table["vector"], b, ("turn", b))
                run(last["vector"], TURNS, ("last", TURNS))


def feed_forward(nc, x1, y, lno_s, lno_b, w_raw, u_raw, g_raw, v_raw, w_in, w_loads, out):
    B, T, D = x1.shape
    _, KD, NE, RANK = v_raw.shape
    ER = NE * RANK
    TILES = B * T // P
    MIX = ER + NE
    UNROLL, LEAD = 4, 4
    assert TILES % UNROLL == 0 and LEAD == UNROLL

    table = {
        "tensor": [("base", 0), ("gT", 0), ("ug", 1), ("lora", 0), ("xt", 2)],
        "scalar": [("gexp", 0), ("xt", 1), ("yln", 3), ("xln", 2), ("gT", 0)],
        "vector": [("xsh", 2), ("xt", 1), ("gt", 0), ("yst", 4), ("x2", 3), ("gT", 0), ("yag", 4), ("xst", 3), ("yeps", 4),
                   ("xag", 3), ("gmax", 1), ("xeps", 3), ("ysh", 4), ("fin", 0)],
        "gpsimd": [("ymul", 3), ("xb", 4), ("yinv", 4), ("xinv", 3)],
    }

    with ExitStack() as ctx:
        at = Place(nc, ctx, "ff")
        wT = [at.sb(f"wT_{n}", [P, KD, D], F32R) for n in ("hi", "lo")]
        mixT = [at.sb(f"mixT_{n}", [P, KD, MIX], F32R) for n in ("hi", "lo")]
        vT = [at.sb(f"vT_{n}", [P, D], F32R) for n in ("hi", "lo")]
        s_rows, b_rows = at.sb("s_rows", [P, D]), at.sb("b_rows", [P, D])
        ident, minus_half = at.sb("ident", [P, P]), at.sb("minus_half", [P, 1])
        y_sb, x1_sb = at.sb("y", [P, 2, D]), at.sb("x1", [P, 2, D])
        xb = at.sb("xb", [P, 2, D])
        yn, ys = at.sb("yn", [P, D]), at.sb("ys", [P, D])
        x2 = at.sb("x2", [P, 4, D])
        xn = at.sb("xn", [P, D])
        x3 = at.sb("x3", [P, 2, D])
        stats, moments = at.sb("stats", [P, 2, 6]), at.sb("moments", [P, 2, 2])
        y_rstd, y_shift = at.sb("y_rstd", [P, 1]), at.sb("y_shift", [P, 1])
        x_rstd, x_shift = at.sb("x_rstd", [P, 2]), at.sb("x_shift", [P, 2])
        xnT = [[at.sb(f"xnT{i}_{n}", [P, KD, P], F32R) for n in ("hi", "lo")] for i in range(2)]
        negmax, esum, ersum = at.sb("negmax", [P, 1]), at.sb("esum", [P, 1]), at.sb("ersum", [P, 1])
        egate = at.sb("egate", [P, NE])
        gt = at.sb("gt", [P, NE, RANK])
        gT = [at.sb(f"gT_{n}", [P, P], F32R) for n in ("hi", "lo")]

        ps_t = [at.psum(f"ps_t{i}", [P, 512]) for i in range(2)]
        ps_u = [at.psum(f"ps_u{i}", [P, 512]) for i in range(2)]
        ps_b = [at.psum(f"ps_b{i}", [P, 512]) for i in range(2)]

        rows_in = at.sem("rows_in")
        dve_passed, sp_passed = at.sem("dve_passed"), at.sem("sp_passed")
        ident_ready, setup_full, setup_hi, setup_lo = at.sem("ident_ready"), at.sem("setup_full"), at.sem("setup_hi"), at.sem("setup_lo")
        y_in = [at.sem(f"y_in{i}") for i in range(2)]
        y_stats, y_moments, y_var = at.sem("y_stats"), at.sem("y_moments"), at.sem("y_var")
        x_stats, x_moments, x_var = at.sem("x_stats"), at.sem("x_moments"), at.sem("x_var")
        y_rstd_ready, y_shift_ready, yn_ready, ys_ready = at.sem("y_rstd_ready"), at.sem("y_shift_ready"), at.sem("yn_ready"), at.sem("ys_ready")
        x_rstd_ready, x_shift_ready = at.sem("x_rstd_ready"), at.sem("x_shift_ready")
        xb_ready, x2_ready, xn_ready = at.sem("xb_ready"), at.sem("x2_ready"), at.sem("xn_ready")
        xt_full, xt_hi, xt_lo = at.sem("xt_full"), at.sem("xt_hi"), at.sem("xt_lo")
        ug_full, lora_full = at.sem("ug_full"), at.sem("lora_full")
        negmax_ready, egate_ready, ersum_ready, gt_ready = at.sem("negmax_ready"), at.sem("egate_ready"), at.sem("ersum_ready"), at.sem("gt_ready")
        gT_full, gT_hi, gT_lo = at.sem("gT_full"), at.sem("gT_hi"), at.sem("gT_lo")
        x3_ready = at.sem("x3_ready")
        out_stored = [at.sem(f"out_stored{i}") for i in range(2)]

        rows = [v.rearrange("b t d -> (b t) d").rearrange("(i p) d -> i p d", p=P) for v in (y, x1, out)]
        setup = [("wT", k) for k in range(KD)] + [("mixT", k) for k in range(KD)] + [("vT", 0)]
        banks = ps_t + ps_u + ps_b

        def setup_parts(use):
            kind, k = use
            return {"wT": ([w[:, k, :] for w in wT], D, 1.0), "mixT": ([w[:, k, :] for w in mixT], MIX, 1.0),
                    "vT": ([w[:, :] for w in vT], D, 1.0 / RANK)}[kind]

        def all_turns(engine, order, run):
            def turns(j, whole):
                for u in range(UNROLL):
                    for task, lead in order:
                        v = u + lead
                        if whole or 0 <= UNROLL * j + v < TILES:
                            run(task, UNROLL * j + v, UNROLL // 2 * j + v // 2, v)

            LAST = TILES // UNROLL - 1
            turns(-1, False)
            with engine.Fori(0, LAST) as j:
                turns(j, True)
            turns(LAST, False)

        with nc.Block() as block:

            @block.gpsimd
            def _(pool):
                make_constants(nc, pool, ident, minus_half, ident_ready)
                pool.wait_ge(rows_in, 2 * DMA)

                def run(task, t, half, v):
                    p = v % 2
                    if task == "xb":
                        pool.wait_ge(y_in[p], 2 * DMA * half + 2 * DMA)
                        nc.gpsimd.tensor_tensor(xb[:, p, :], x1_sb[:, p, :], b_rows[:, :], ALU.add).then_inc(xb_ready, 1)
                    elif task == "yinv":
                        inverse_root(nc, pool, y_rstd[:, :], moments[:, 0, 1:2], minus_half[:, :], y_var, t, y_rstd_ready)
                    elif task == "ymul":
                        pool.wait_ge(yn_ready, t + 1)
                        nc.gpsimd.tensor_tensor(ys[:, :], yn[:, :], s_rows[:, :], ALU.mult).then_inc(ys_ready, 1)
                    elif task == "xinv":
                        inverse_root(nc, pool, x_rstd[:, p:p + 1], moments[:, 1, 1:2], minus_half[:, :], x_var, t, x_rstd_ready)

                all_turns(pool, table["gpsimd"], run)

            @block.sync
            def _(sp):
                def load(t, p):
                    for v, buf in zip(rows[0:2], (y_sb, x1_sb)):
                        sp.dma_start(buf[:, p, :], v[bass.ds(t, 1)].rearrange("o p d -> (o p) d")).then_inc(y_in[p], DMA)

                def load_next(t, p):
                    sp.wait_ge(ys_ready, t - 1)
                    sp.sem_inc(sp_passed, 1)
                    load(t, p)

                def store(t, p):
                    sp.wait_ge(x3_ready, t + 3)
                    sp.sem_inc(sp_passed, 1)
                    sp.dma_start(rows[2][bass.ds(t, 1)].rearrange("o p d -> (o p) d"), x3[:, p, :]).then_inc(out_stored[p], DMA)

                load(0, 0)
                load(1, 1)
                sp.dma_start(s_rows[:, :], lno_s.partition_broadcast(P)).then_inc(rows_in, DMA)
                sp.dma_start(b_rows[:, :], lno_b.partition_broadcast(P)).then_inc(rows_in, DMA)
                AHEAD = LEAD + 2
                for t in range(2, AHEAD):
                    load_next(t, t % 2)
                with sp.Fori(0, (TILES - AHEAD) // 2) as j:
                    for p in range(2):
                        load_next(2 * j + p + AHEAD, p)
                        store(2 * j + p, p)
                for t in range(TILES - AHEAD, TILES):
                    store(t, t % 2)
                for s in out_stored:
                    sp.wait_ge(s, DMA * (TILES // 2) + DMA)

            @block.tensor
            def _(pe):
                def split_products(out, lhs, rhs, first, last):
                    for n, (i, j) in enumerate(((0, 0), (0, 1), (1, 0))):
                        ins = nc.tensor.matmul(out, lhs[i], rhs[j], start=first and n == 0, stop=last and n == 2)
                    return ins

                pe.wait_ge(ident_ready, 3)
                pe.wait_ge(w_in, w_loads * DMA)
                for j, (kind, k) in enumerate(setup):
                    bank = banks[j % len(banks)]
                    if j >= len(banks):
                        pe.wait_ge(setup_lo, j - len(banks) + 1)
                    if kind == "wT":
                        for o in range(KD):
                            ins = nc.tensor.transpose(bank[:, o * P:(o + 1) * P], w_raw[:, o, k * P:(k + 1) * P], ident[:, :])
                    elif kind == "mixT":
                        nc.tensor.transpose(bank[:, 0:ER], u_raw[:, k * P:(k + 1) * P], ident[:, :])
                        ins = nc.tensor.transpose(bank[:, ER:MIX], g_raw[:, k * P:(k + 1) * P], ident[0:NE, 0:NE])
                    else:
                        for o in range(KD):
                            ins = nc.tensor.transpose(bank[:, o * P:(o + 1) * P], v_raw[:, o, :, :].rearrange("p e r -> p (e r)"), ident[:, :])
                    ins.then_inc(setup_full, 1)
                pe.wait_ge(setup_lo, len(setup))

                def run(task, t, half, v):
                    p = v % 2
                    if task == "xt":
                        pe.wait_ge(xn_ready, t + 1)
                        for k in range(KD):
                            ins = nc.tensor.transpose(ps_t[0][:, k * P:(k + 1) * P], xn[:, k * P:(k + 1) * P], ident[:, :])
                        ins.then_inc(xt_full, 1)
                    elif task == "ug":
                        pe.wait_ge(xt_lo, t + 1)
                        for k in range(KD):
                            ins = split_products(ps_u[p][:, 0:MIX], [x[:, k, :] for x in xnT[p]], [w[:, k, :] for w in mixT],
                                                 k == 0, k == KD - 1)
                        ins.then_inc(ug_full, 1)
                    elif task == "base":
                        pe.wait_ge(x3_ready, t + 1)
                        for k in range(KD):
                            split_products(ps_b[p][:, :], [x[:, k, :] for x in xnT[p]], [w[:, k, :] for w in wT], k == 0, False)
                    elif task == "gT":
                        pe.wait_ge(gt_ready, t + 1)
                        nc.tensor.transpose(ps_t[1][:, 0:ER], gt[:, :, :].rearrange("p e r -> p (e r)"), ident[:, :]).then_inc(gT_full, 1)
                    elif task == "lora":
                        pe.wait_ge(gT_lo, t + 1)
                        split_products(ps_b[p][:, :], [g[:, :] for g in gT], [v[:, :] for v in vT], False, True).then_inc(lora_full, 1)

                all_turns(pe, table["tensor"], run)

            @block.scalar
            def _(act):
                for j, use in enumerate(setup):
                    parts, n, factor = setup_parts(use)
                    act.wait_ge(setup_full, j + 1)
                    nc.scalar.activation(parts[0], banks[j % len(banks)][:, 0:n], ACT.Copy, scale=factor).then_inc(setup_hi, 1)

                def run(task, t, half, v):
                    p = v % 2
                    if task == "gexp":
                        act.wait_ge(negmax_ready, t + 1)
                        nc.scalar.activation(egate[:, :], ps_u[p][:, ER:MIX], ACT.Exp, bias=negmax[:, :], scale=1.0,
                                             accum_out=esum[:, :]).then_inc(egate_ready, 1)
                    elif task == "xt":
                        act.wait_ge(xt_full, t + 1)
                        nc.scalar.activation(xnT[p][0][:, :, :], ps_t[0][:, :].rearrange("p (k t) -> p k t", k=KD),
                                             ACT.Copy).then_inc(xt_hi, 1)
                    elif task == "yln":
                        act.wait_ge(y_shift_ready, t + 1)
                        nc.scalar.activation(yn[:, :], y_sb[:, p, :], ACT.Identity, bias=y_shift[:, :], scale=y_rstd[:, :]).then_inc(yn_ready, 1)
                    elif task == "xln":
                        act.wait_ge(x_shift_ready, t + 1)
                        nc.scalar.activation(xn[:, :], x2[:, v % 4, :], ACT.Identity, bias=x_shift[:, p:p + 1],
                                             scale=x_rstd[:, p:p + 1]).then_inc(xn_ready, 1)
                    elif task == "gT":
                        act.wait_ge(gT_full, t + 1)
                        nc.scalar.activation(gT[0][:, :], ps_t[1][:, 0:ER], ACT.Copy).then_inc(gT_hi, 1)

                all_turns(act, table["scalar"], run)

            @block.vector
            def _(dve):
                dve.sem_inc(x3_ready, 2)
                for s in out_stored:
                    dve.sem_inc(s, DMA)
                for j, use in enumerate(setup):
                    parts, n, factor = setup_parts(use)
                    dve.wait_ge(setup_hi, j + 1)
                    nc.vector.scalar_tensor_tensor(parts[1], banks[j % len(banks)][:, 0:n], factor, parts[0].bitcast(F32),
                                                   ALU.mult, ALU.subtract).then_inc(setup_lo, 1)

                def run(task, t, half, v):
                    p = v % 2
                    if task == "yst":
                        dve.wait_ge(y_in[p], 2 * DMA * half + 2 * DMA)
                        nc.vector.bn_stats(stats[:, 0, :], y_sb[:, p, :]).then_inc(y_stats, 1)
                    elif task == "yag":
                        dve.wait_ge(y_stats, t + 1)
                        dve.sem_inc(dve_passed, 1)
                        nc.vector.bn_aggr(moments[:, 0, :], stats[:, 0, :]).then_inc(y_moments, 1)
                    elif task == "yeps":
                        dve.wait_ge(y_moments, t + 1)
                        nc.vector.tensor_scalar(moments[:, 0, 1:2], moments[:, 0, 1:2], XLN_EPS, None, ALU.add).then_inc(y_var, 1)
                    elif task == "ysh":
                        dve.wait_ge(y_rstd_ready, t + 1)
                        nc.vector.tensor_scalar(y_shift[:, :], moments[:, 0, 0:1], y_rstd[:, :], -1.0, ALU.mult, ALU.mult).then_inc(y_shift_ready, 1)
                    elif task == "x2":
                        dve.wait_ge(ys_ready, t + 1)
                        dve.wait_ge(xb_ready, t + 1)
                        nc.vector.tensor_tensor(x2[:, v % 4, :], ys[:, :], xb[:, p, :], ALU.add).then_inc(x2_ready, 1)
                    elif task == "xst":
                        dve.wait_ge(x2_ready, t + 1)
                        nc.vector.bn_stats(stats[:, 1, :], x2[:, v % 4, :]).then_inc(x_stats, 1)
                    elif task == "xag":
                        dve.wait_ge(x_stats, t + 1)
                        dve.sem_inc(dve_passed, 1)
                        nc.vector.bn_aggr(moments[:, 1, :], stats[:, 1, :]).then_inc(x_moments, 1)
                    elif task == "xeps":
                        dve.wait_ge(x_moments, t + 1)
                        nc.vector.tensor_scalar(moments[:, 1, 1:2], moments[:, 1, 1:2], LN_EPS, None, ALU.add).then_inc(x_var, 1)
                    elif task == "xsh":
                        dve.wait_ge(x_rstd_ready, t + 1)
                        nc.vector.tensor_scalar(x_shift[:, p:p + 1], moments[:, 1, 0:1], x_rstd[:, p:p + 1], -1.0,
                                                ALU.mult, ALU.mult).then_inc(x_shift_ready, 1)
                    elif task == "gmax":
                        dve.wait_ge(ug_full, t + 1)
                        nc.vector.tensor_reduce(negmax[:, :], ps_u[p][:, ER:MIX], AX.X, ALU.max, negate=True).then_inc(negmax_ready, 1)
                    elif task == "gt":
                        dve.wait_ge(egate_ready, t + 1)
                        nc.vector.reciprocal(ersum[:, :], esum[:, :]).then_inc(ersum_ready, 1)
                        dve.wait_ge(ersum_ready, t + 1)
                        nc.vector.scalar_tensor_tensor(gt[:, :, :], ps_u[p][:, 0:ER].rearrange("p (e r) -> p e r", e=NE), ersum[:, :],
                                                       egate[:, :].unsqueeze(2).to_broadcast([P, NE, RANK]),
                                                       ALU.mult, ALU.mult).then_inc(gt_ready, 1)
                    elif task == "xt":
                        dve.wait_ge(xt_hi, t + 1)
                        nc.vector.tensor_tensor(xnT[p][1][:, :, :], ps_t[0][:, :].rearrange("p (k t) -> p k t", k=KD),
                                                xnT[p][0][:, :, :].bitcast(F32), ALU.subtract).then_inc(xt_lo, 1)
                    elif task == "gT":
                        dve.wait_ge(gT_hi, t + 1)
                        nc.vector.tensor_tensor(gT[1][:, :], ps_t[1][:, 0:ER], gT[0][:, :].bitcast(F32), ALU.subtract).then_inc(gT_lo, 1)
                    elif task == "fin":
                        dve.wait_ge(lora_full, t + 1)
                        dve.wait_ge(out_stored[p], DMA * half + DMA)
                        nc.vector.tensor_tensor(x3[:, p, :], ps_b[p][:, :], x2[:, v % 4, :], ALU.add).then_inc(x3_ready, 1)

                all_turns(dve, table["vector"], run)


_INS = ["x", "ctx_1024", "mask_BxS2_bf1", "L0_attn_w_qkv", "L0_attn_w_out", "L0_xattn_ln1_s", "L0_xattn_ln1_b",
        "L0_xattn_lnc_s", "L0_xattn_lnc_b", "L0_xattn_Wq", "L0_xattn_Wkv", "L0_xattn_null_kv", "L0_xattn_Wo",
        "L0_xattn_lno_s", "L0_xattn_lno_b", "L0_ffn_weight", "L0_ffn_gate_w", "L0_ffn_lora_U", "L0_ffn_lora_V"]


def decoder_layer(nc, x, context, mask, w_qkv, w_out, ln1_s, ln1_b, lnc_s, lnc_b, w_q, w_kv, null_kv, w_o,
                  lno_s, lno_b, weight, gate_w, lora_U, lora_V, out):
    B, T, D = x.shape
    x1 = nc.dram_tensor("x1", [B, T, D], F32, kind="Internal").ap()
    q_T = nc.dram_tensor("q_T", [B, w_q.shape[1], T], F32, kind="Internal").ap()
    y = nc.dram_tensor("y", [B, T, D], F32, kind="Internal").ap()
    KD, ED = D // P, w_o.shape[0] // P
    NE, RANK, _ = lora_U.shape

    with ExitStack() as ctx:
        at = Place(nc, ctx, "dl")
        base = -(-nc.sbuf_base // 32) * 32
        shared = Shared(nc, at.sb("shared", [P, 2 * KD * w_qkv.shape[1]]), base)
        kv_in, o_in, w_in = [at.sem(f"kv_in{k}") for k in range(KD)], at.sem("o_in"), at.sem("w_in")
        kv_raw, o_raw = shared.tensor("kv_raw", [P, KD, w_kv.shape[1]]), shared.tensor("o_raw", [P, ED, D])
        shared.restart()
        w_raw = shared.tensor("w_raw", [P, KD, D])
        u_raw, g_raw = shared.tensor("u_raw", [NE * RANK, D]), shared.tensor("g_raw", [NE, D])
        v_raw = shared.tensor("v_raw", [P, KD, NE, RANK])
        shared.restart()

        s_col, b_col = at.sb("s_col", [P, KD]), at.sb("b_col", [P, KD])
        ln_in = at.sem("ln_in")

        def load_attention_weights(sp):
            with nc.allow_non_contiguous_dma(reason="two vectors, once"):
                sp.dma_start(s_col[:, :], lnc_s.rearrange("(k p) -> p k", p=P)).then_inc(ln_in, DMA)
                sp.dma_start(b_col[:, :], lnc_b.rearrange("(k p) -> p k", p=P)).then_inc(ln_in, DMA)
            for k in range(KD):
                sp.dma_start(kv_raw[:, k, :], w_kv[k * P:(k + 1) * P, :]).then_inc(kv_in[k], DMA)
            sp.dma_start(o_raw[:, :, :], w_o.rearrange("(k p) n -> p k n", p=P)).then_inc(o_in, DMA)

        def load_dense_weights(sp):
            sp.dma_start(w_raw[:, :, :], weight.rearrange("(k p) n -> p k n", p=P)).then_inc(w_in, DMA)
            sp.dma_start(u_raw[:, :], lora_U.rearrange("e r n -> (e r) n")).then_inc(w_in, DMA)
            sp.dma_start(g_raw[:, :], gate_w).then_inc(w_in, DMA)
            for k in range(KD):
                sp.dma_start(v_raw[:, k, :, :], lora_V[:, k * P:(k + 1) * P, :].rearrange("e o r -> o e r")).then_inc(w_in, DMA)

        self_attention(nc, x, w_qkv, w_out, ln1_s, ln1_b, w_q, x1, q_T, shared, load_attention_weights)
        cross_attention(nc, context, mask, null_kv, q_T, y, shared, kv_raw, kv_in, o_raw, o_in, s_col, b_col, ln_in, load_dense_weights)
        feed_forward(nc, x1, y, lno_s, lno_b, w_raw, u_raw, g_raw, v_raw, w_in, 3 + KD, out)


def kernel(**inputs):
    import numpy as _np
    import concourse.bacc as _bacc
    from concourse import mybir as _mybir
    from concourse.bass_utils import run_bass_kernel_spmd as _run

    nc = _bacc.Bacc("TRN2", target_bir_lowering=False, num_devices=1, dynamic_dma_scratch_size=1024)
    arrays, args = {}, []
    for name in _INS:
        a = _np.ascontiguousarray(inputs[name])
        arrays[f"in_{name}_dram"] = a
        args.append(nc.dram_tensor(f"in_{name}_dram", a.shape, _mybir.dt.from_np(a.dtype), kind="ExternalInput").ap())
    shape = inputs["x"].shape
    args.append(nc.dram_tensor("out_0_dram", shape, F32, kind="ExternalOutput").ap())
    decoder_layer(nc, *args)
    r = _run(nc, [arrays], core_ids=[0])
    return r.results[0]["out_0_dram"]
```
